# Optimizing a Trainium2 kernel written in Bass

```python
import numpy as np
import jax
import jax.numpy as jnp

def _softmax(x, axis=-1):
    return jax.nn.softmax(x, axis=axis)

def _gelu(x):
    return jax.nn.gelu(x, approximate=True)

def _silu(x):
    return jax.nn.silu(x)

def _sigmoid(x):
    return jax.nn.sigmoid(x)

def _layernorm(x, axis=-1, eps=1e-05):
    m = jnp.mean(x, axis=axis, keepdims=True)
    v = jnp.var(x, axis=axis, keepdims=True)
    return (x - m) / jnp.sqrt(v + eps)

def _scatter_add(tgt, idx, src, axis=0):
    return tgt.at[idx].add(src)

def _segment_sum(src, seg, n):
    return jax.ops.segment_sum(src, seg, n)
kernel_name = 'mk_decoder_preln_d2_seqx_r8_cba8d7'

def setup_inputs(seed: int=0):
    np.random.seed(seed)
    _w = jnp.asarray

    def _rec_inputs():
        import jax
        import jax.numpy as jnp
        _rk = jax.random.key(seed)
        x = 7.22e-05 + 1 * jax.random.normal(jax.random.fold_in(_rk, 1), (8, 128, 128), jnp.float32)
        _lenS = 128 - jax.random.randint(jax.random.fold_in(_rk, 7), (8,), 0, max(1, 128 // 4) + 1, jnp.int32)
        _lenS2 = 77 - jax.random.randint(jax.random.fold_in(_rk, 8), (8,), 0, max(1, 77 // 4) + 1, jnp.int32)
        _ctx_1024P = jax.random.normal(jax.random.fold_in(_rk, 11), (8, 16, 128), jnp.float32)
        _ctx_1024c = jax.random.dirichlet(jax.random.fold_in(_rk, 511), 0.3 * jnp.ones((16,), jnp.float32), (8, 77))
        _ctx_1024t = jnp.einsum('bsk,bkd->bsd', _ctx_1024c, _ctx_1024P)
        _ctx_1024t = _ctx_1024t * jax.lax.rsqrt(jnp.mean(jnp.square(_ctx_1024t)) + 1e-12) * 0.953939
        ctx_1024 = 4.13588e-05 + 0.999923 * (_ctx_1024t + 0.3 * jax.random.normal(jax.random.fold_in(_rk, 611), (8, 77, 128), jnp.float32))
        itok_BxS_1_4095 = jax.random.randint(jax.random.fold_in(_rk, 12), (8, 128), 1, 512, jnp.int32)
        return (x, ctx_1024, itok_BxS_1_4095)
    x, ctx_1024, itok_BxS_1_4095 = _rec_inputs()

    def _L0_attn_setup():
        import jax, jax.numpy as jnp
        import numpy as np
        B, L, D = (4, 128, 128)
        DI, DS, DC, DR = (256, 16, 4, 64)

        def _mamba(x, in_proj, conv_w, conv_b, x_proj, dt_w, dt_b, A_log, Dsk, out_proj):
            xz = x @ in_proj.T
            xh, z = jnp.split(xz, 2, axis=-1)
            xp = jnp.pad(xh, ((0, 0), (DC - 1, 0), (0, 0)))
            Ls = xh.shape[1]
            xc = conv_b + sum((xp[:, k:k + Ls, :] * conv_w[:, k] for k in range(DC)))
            xc = jax.nn.silu(xc)
            dbc = xc @ x_proj.T
            dt, Bm, Cm = jnp.split(dbc, [DR, DR + DS], axis=-1)
            delta = jax.nn.softplus(dt @ dt_w.T + dt_b)
            A = -jnp.exp(A_log)

            def step(h, inp):
                u_t, d_t, B_t, C_t = inp
                h = h * jnp.exp(d_t[:, :, None] * A) + (d_t * u_t)[:, :, None] * B_t[:, None, :]
                return (h, jnp.einsum('bds,bs->bd', h, C_t))
            inps = (jnp.moveaxis(xc, 1, 0), jnp.moveaxis(delta, 1, 0), jnp.moveaxis(Bm, 1, 0), jnp.moveaxis(Cm, 1, 0))
            h0 = jnp.zeros((x.shape[0], DI, DS), x.dtype)
            _, ys = jax.lax.scan(step, h0, inps)
            y = jnp.moveaxis(ys, 0, 1) + xc * Dsk
            y = y * jax.nn.silu(z)
            return y @ out_proj.T
        key = jax.random.key(seed)
        ks = jax.random.split(key, 24)
        rn = lambda k, shape, s=0.02: s * jax.random.normal(k, shape, jnp.float32)
        inp = {'x': jax.random.normal(ks[0], (B, L, D), jnp.float32)}
        for i, p in enumerate(('f', 'b')):
            o = 1 + i * 8
            inp[f'in_proj_{p}'] = rn(ks[o], (2 * DI, D))
            inp[f'conv_w_{p}'] = rn(ks[o + 1], (DI, DC), 0.2)
            inp[f'conv_b_{p}'] = rn(ks[o + 2], (DI,), 0.1)
            inp[f'x_proj_{p}'] = rn(ks[o + 3], (DR + 2 * DS, DI))
            inp[f'dt_w_{p}'] = rn(ks[o + 4], (DI, DR), 0.1)
            inp[f'dt_b_{p}'] = rn(ks[o + 5], (DI,), 0.5)
            inp[f'A_log_{p}'] = jnp.log(jnp.broadcast_to(jnp.arange(1.0, DS + 1.0, dtype=jnp.float32), (DI, DS))) + 0.0
            inp[f'D_{p}'] = jnp.ones((DI,), jnp.float32)
            inp[f'out_proj_{p}'] = rn(ks[o + 6], (D, DI))
        inp['ln_w'] = jnp.ones((D,), jnp.float32)
        inp['ln_b'] = jnp.zeros((D,), jnp.float32)
        return inp
    _L0_attn_all = _L0_attn_setup()
    _L0_attn_in = {k: v for k, v in _L0_attn_all.items() if k in ('in_proj_f', 'conv_w_f', 'conv_b_f', 'x_proj_f', 'dt_w_f', 'dt_b_f', 'A_log_f', 'D_f', 'out_proj_f', 'in_proj_b', 'conv_w_b', 'conv_b_b', 'x_proj_b', 'dt_w_b', 'dt_b_b', 'A_log_b', 'D_b', 'out_proj_b', 'ln_w', 'ln_b')}
    del _L0_attn_all

    def _L0_xattn_setup():
        import jax, jax.numpy as jnp
        import numpy as np
        EMBED_DIM = 128
        NUM_HEADS = 16
        HEAD_DIM = EMBED_DIM // NUM_HEADS
        ROPE_BASE = 10000.0

        def _apply_rope(q, position_ids):
            hd = q.shape[-1]
            inv_freq = 1.0 / ROPE_BASE ** (jnp.arange(0, hd, 2, dtype=jnp.float32) / hd)
            ang = position_ids.astype(jnp.float32)[:, :, None] * inv_freq
            cos = jnp.cos(ang)[:, :, None, :]
            sin = jnp.sin(ang)[:, :, None, :]
            q1, q2 = (q[..., :hd // 2], q[..., hd // 2:])
            return jnp.concatenate([q1 * cos - q2 * sin, q2 * cos + q1 * sin], axis=-1)
        key = jax.random.key(seed)
        ks = jax.random.split(key, 12)
        B, T, M, D = (4, 256, 256, EMBED_DIM)
        query = jax.random.normal(ks[0], (B, T, D), dtype=jnp.float32)
        k_in = jax.random.normal(ks[1], (B, M, D), dtype=jnp.float32)
        v_in = jax.random.normal(ks[2], (B, M, D), dtype=jnp.float32)
        query_position_ids = jnp.sort(jax.random.randint(ks[3], (B, T), 0, 512), axis=-1).astype(jnp.int64)
        lim = float(np.sqrt(6.0 / (D + D)))
        Wq = jax.random.uniform(ks[4], (D, D), minval=-lim, maxval=lim, dtype=jnp.float32)
        Wk = jax.random.uniform(ks[5], (D, D), minval=-lim, maxval=lim, dtype=jnp.float32)
        Wv = jax.random.uniform(ks[6], (D, D), minval=-lim, maxval=lim, dtype=jnp.float32)
        Wo = jax.random.uniform(ks[7], (D, D), minval=-lim, maxval=lim, dtype=jnp.float32)
        bq = jnp.zeros((D,), jnp.float32)
        bk = jnp.zeros((D,), jnp.float32)
        bv = jnp.zeros((D,), jnp.float32)
        bo = jnp.zeros((D,), jnp.float32)
        return dict(query=query, key=k_in, value=v_in, query_position_ids=query_position_ids, Wq=Wq, bq=bq, Wk=Wk, bk=bk, Wv=Wv, bv=bv, Wo=Wo, bo=bo)
    _L0_xattn_all = _L0_xattn_setup()
    _L0_xattn_in = {k: v for k, v in _L0_xattn_all.items() if k in ('Wq', 'bq', 'Wk', 'bk', 'Wv', 'bv', 'Wo', 'bo')}
    del _L0_xattn_all

    def _L0_ffn_setup():
        import jax, jax.numpy as jnp
        import numpy as np
        E = 8
        TOP_K = 2
        DIM = 128
        HID = 256
        key = jax.random.key(seed)
        k1, k2, k3, k4, k5 = jax.random.split(key, 5)
        s = 0.02
        x = jax.random.normal(k1, (2, 256, DIM), dtype=jnp.float32)
        Wg = jax.random.normal(k2, (DIM, E), dtype=jnp.float32) * s
        W1 = jax.random.normal(k3, (E, DIM, HID), dtype=jnp.float32) * s
        W2 = jax.random.normal(k4, (E, DIM, HID), dtype=jnp.float32) * s
        W3 = jax.random.normal(k5, (E, HID, DIM), dtype=jnp.float32) * s
        return {'x': x, 'Wg': Wg, 'W1': W1, 'W2': W2, 'W3': W3}
    _L0_ffn_all = _L0_ffn_setup()
    _L0_ffn_in = {k: v for k, v in _L0_ffn_all.items() if k in ('Wg', 'W1', 'W2', 'W3')}
    del _L0_ffn_all

    def _L1_attn_setup():
        import jax, jax.numpy as jnp
        import numpy as np
        SPS_AMPLIFY = 1.5
        SPS_DAMPEN = 0.3
        SPS_DEEP_QUESTION = 0.1
        SPS_EXCLAIM = 0.85
        SPS_QUESTION = 0.25
        SPS_SUPER_EXCLAIM = 0.95
        B, S, D = (4, 256, 128)
        NUM_HEADS = 16
        HEAD_DIM = D // NUM_HEADS
        SCALE = HEAD_DIM ** (-0.5)

        def sps_pro(x):
            xn = jax.nn.sigmoid(x)
            mult = jnp.where(xn > SPS_SUPER_EXCLAIM, 2.0, jnp.where(xn > SPS_EXCLAIM, SPS_AMPLIFY, jnp.where(xn < SPS_DEEP_QUESTION, 0.1, jnp.where(xn < SPS_QUESTION, SPS_DAMPEN, 1.0))))
            return x * mult
        key = jax.random.key(seed)
        k0, k1, k2, k3, k4 = jax.random.split(key, 5)
        s = 1.0 / np.sqrt(D)
        return {'x': jax.random.normal(k0, (B, S, D), dtype=jnp.float32), 'W_qkv': jax.random.uniform(k1, (D, 3 * D), dtype=jnp.float32, minval=-s, maxval=s), 'b_qkv': jax.random.uniform(k2, (3 * D,), dtype=jnp.float32, minval=-s, maxval=s), 'W_proj': jax.random.uniform(k3, (D, D), dtype=jnp.float32, minval=-s, maxval=s), 'b_proj': jax.random.uniform(k4, (D,), dtype=jnp.float32, minval=-s, maxval=s)}
    _L1_attn_all = _L1_attn_setup()
    _L1_attn_in = {k: v for k, v in _L1_attn_all.items() if k in ('W_qkv', 'b_qkv', 'W_proj', 'b_proj')}
    del _L1_attn_all

    def _L1_xattn_setup():
        import jax, jax.numpy as jnp
        import numpy as np
        D_MODEL = 128
        D_HEAD = 64
        NHEADS = 8
        IN_DIM = D_HEAD * NHEADS
        EPS = 1e-05

        def layernorm(x, g, b):
            mu = jnp.mean(x, axis=-1, keepdims=True)
            var = jnp.var(x, axis=-1, keepdims=True)
            return (x - mu) * jax.lax.rsqrt(var + EPS) * g + b
        key = jax.random.key(seed)
        ks = jax.random.split(key, 8)
        B, M, L = (4, 1024, 64)
        x = jax.random.normal(ks[0], (B, M, D_MODEL), dtype=jnp.float32)
        latents = jax.random.normal(ks[1], (B, L, D_MODEL), dtype=jnp.float32)
        s = 1.0 / np.sqrt(D_MODEL)
        Wq = jax.random.normal(ks[2], (D_MODEL, IN_DIM), dtype=jnp.float32) * s
        Wkv = jax.random.normal(ks[3], (D_MODEL, 2 * IN_DIM), dtype=jnp.float32) * s
        Wout = jax.random.normal(ks[4], (IN_DIM, D_MODEL), dtype=jnp.float32) * (1.0 / np.sqrt(IN_DIM))
        gm = jnp.ones((D_MODEL,), jnp.float32)
        bm = jnp.zeros((D_MODEL,), jnp.float32)
        gl = jnp.ones((D_MODEL,), jnp.float32)
        bl = jnp.zeros((D_MODEL,), jnp.float32)
        return {'x': x, 'latents': latents, 'Wq': Wq, 'Wkv': Wkv, 'Wout': Wout, 'gm': gm, 'bm': bm, 'gl': gl, 'bl': bl}
    _L1_xattn_all = _L1_xattn_setup()
    _L1_xattn_in = {k: v for k, v in _L1_xattn_all.items() if k in ('Wq', 'Wkv', 'Wout', 'gm', 'bm', 'gl', 'bl')}
    del _L1_xattn_all

    def _L1_ffn_setup():
        import jax, jax.numpy as jnp
        import numpy as np
        DIM, HEADS, EXPERTS, DFF = (128, 16, 8, 512)
        EPS = 1e-05

        def layernorm(x, g, b):
            mu = jnp.mean(x, -1, keepdims=True)
            var = jnp.mean(jnp.square(x - mu), -1, keepdims=True)
            return (x - mu) * jax.lax.rsqrt(var + EPS) * g + b
        key = jax.random.key(seed)
        ks = jax.random.split(key, 12)
        s = lambda d: 1.0 / np.sqrt(d)
        return {'x': jax.random.normal(ks[0], (2, 256, DIM), jnp.float32), 'conv_w': jax.random.normal(ks[1], (DIM, DIM, 3), jnp.float32) * s(DIM * 3), 'conv_b': jnp.zeros((DIM,), jnp.float32), 'wqkv': jax.random.normal(ks[2], (3 * DIM, DIM), jnp.float32) * s(DIM), 'bqkv': jnp.zeros((3 * DIM,), jnp.float32), 'wo': jax.random.normal(ks[3], (DIM, DIM), jnp.float32) * s(DIM), 'bo': jnp.zeros((DIM,), jnp.float32), 'ln1_g': jnp.ones((DIM,), jnp.float32), 'ln1_b': jnp.zeros((DIM,), jnp.float32), 'gate_w': jax.random.normal(ks[4], (DIM, EXPERTS), jnp.float32) * s(DIM), 'gate_b': jnp.zeros((EXPERTS,), jnp.float32), 'w1': jax.random.normal(ks[5], (EXPERTS, DIM, DFF), jnp.float32) * s(DIM), 'b1': jnp.zeros((EXPERTS, DFF), jnp.float32), 'w2': jax.random.normal(ks[6], (EXPERTS, DFF, DIM), jnp.float32) * s(DFF), 'b2': jnp.zeros((EXPERTS, DIM), jnp.float32), 'ln2_g': jnp.ones((DIM,), jnp.float32), 'ln2_b': jnp.zeros((DIM,), jnp.float32)}
    _L1_ffn_all = _L1_ffn_setup()
    _L1_ffn_in = {k: v for k, v in _L1_ffn_all.items() if k in ('conv_w', 'conv_b', 'wqkv', 'bqkv', 'wo', 'bo', 'ln1_g', 'ln1_b', 'gate_w', 'gate_b', 'w1', 'b1', 'w2', 'b2', 'ln2_g', 'ln2_b')}
    del _L1_ffn_all
    return {'x': x, 'ctx_1024': ctx_1024, 'itok_BxS_1_4095': itok_BxS_1_4095, 'L0_attn_in_proj_f': _L0_attn_in['in_proj_f'], 'L0_attn_conv_w_f': _L0_attn_in['conv_w_f'], 'L0_attn_conv_b_f': _L0_attn_in['conv_b_f'], 'L0_attn_x_proj_f': _L0_attn_in['x_proj_f'], 'L0_attn_dt_w_f': _L0_attn_in['dt_w_f'], 'L0_attn_dt_b_f': _L0_attn_in['dt_b_f'], 'L0_attn_A_log_f': _L0_attn_in['A_log_f'], 'L0_attn_D_f': _L0_attn_in['D_f'], 'L0_attn_out_proj_f': _L0_attn_in['out_proj_f'], 'L0_attn_in_proj_b': _L0_attn_in['in_proj_b'], 'L0_attn_conv_w_b': _L0_attn_in['conv_w_b'], 'L0_attn_conv_b_b': _L0_attn_in['conv_b_b'], 'L0_attn_x_proj_b': _L0_attn_in['x_proj_b'], 'L0_attn_dt_w_b': _L0_attn_in['dt_w_b'], 'L0_attn_dt_b_b': _L0_attn_in['dt_b_b'], 'L0_attn_A_log_b': _L0_attn_in['A_log_b'], 'L0_attn_D_b': _L0_attn_in['D_b'], 'L0_attn_out_proj_b': _L0_attn_in['out_proj_b'], 'L0_attn_ln_w': _L0_attn_in['ln_w'], 'L0_attn_ln_b': _L0_attn_in['ln_b'], 'L0_xattn_Wq': _L0_xattn_in['Wq'], 'L0_xattn_bq': _L0_xattn_in['bq'], 'L0_xattn_Wk': _L0_xattn_in['Wk'], 'L0_xattn_bk': _L0_xattn_in['bk'], 'L0_xattn_Wv': _L0_xattn_in['Wv'], 'L0_xattn_bv': _L0_xattn_in['bv'], 'L0_xattn_Wo': _L0_xattn_in['Wo'], 'L0_xattn_bo': _L0_xattn_in['bo'], 'L0_ffn_Wg': _L0_ffn_in['Wg'], 'L0_ffn_W1': _L0_ffn_in['W1'], 'L0_ffn_W2': _L0_ffn_in['W2'], 'L0_ffn_W3': _L0_ffn_in['W3'], 'L1_attn_W_qkv': _L1_attn_in['W_qkv'], 'L1_attn_b_qkv': _L1_attn_in['b_qkv'], 'L1_attn_W_proj': _L1_attn_in['W_proj'], 'L1_attn_b_proj': _L1_attn_in['b_proj'], 'L1_xattn_Wq': _L1_xattn_in['Wq'], 'L1_xattn_Wkv': _L1_xattn_in['Wkv'], 'L1_xattn_Wout': _L1_xattn_in['Wout'], 'L1_xattn_gm': _L1_xattn_in['gm'], 'L1_xattn_bm': _L1_xattn_in['bm'], 'L1_xattn_gl': _L1_xattn_in['gl'], 'L1_xattn_bl': _L1_xattn_in['bl'], 'L1_ffn_conv_w': _L1_ffn_in['conv_w'], 'L1_ffn_conv_b': _L1_ffn_in['conv_b'], 'L1_ffn_wqkv': _L1_ffn_in['wqkv'], 'L1_ffn_bqkv': _L1_ffn_in['bqkv'], 'L1_ffn_wo': _L1_ffn_in['wo'], 'L1_ffn_bo': _L1_ffn_in['bo'], 'L1_ffn_ln1_g': _L1_ffn_in['ln1_g'], 'L1_ffn_ln1_b': _L1_ffn_in['ln1_b'], 'L1_ffn_gate_w': _L1_ffn_in['gate_w'], 'L1_ffn_gate_b': _L1_ffn_in['gate_b'], 'L1_ffn_w1': _L1_ffn_in['w1'], 'L1_ffn_b1': _L1_ffn_in['b1'], 'L1_ffn_w2': _L1_ffn_in['w2'], 'L1_ffn_b2': _L1_ffn_in['b2'], 'L1_ffn_ln2_g': _L1_ffn_in['ln2_g'], 'L1_ffn_ln2_b': _L1_ffn_in['ln2_b']}

def reference(x, ctx_1024, itok_BxS_1_4095, L0_attn_in_proj_f, L0_attn_conv_w_f, L0_attn_conv_b_f, L0_attn_x_proj_f, L0_attn_dt_w_f, L0_attn_dt_b_f, L0_attn_A_log_f, L0_attn_D_f, L0_attn_out_proj_f, L0_attn_in_proj_b, L0_attn_conv_w_b, L0_attn_conv_b_b, L0_attn_x_proj_b, L0_attn_dt_w_b, L0_attn_dt_b_b, L0_attn_A_log_b, L0_attn_D_b, L0_attn_out_proj_b, L0_attn_ln_w, L0_attn_ln_b, L0_xattn_Wq, L0_xattn_bq, L0_xattn_Wk, L0_xattn_bk, L0_xattn_Wv, L0_xattn_bv, L0_xattn_Wo, L0_xattn_bo, L0_ffn_Wg, L0_ffn_W1, L0_ffn_W2, L0_ffn_W3, L1_attn_W_qkv, L1_attn_b_qkv, L1_attn_W_proj, L1_attn_b_proj, L1_xattn_Wq, L1_xattn_Wkv, L1_xattn_Wout, L1_xattn_gm, L1_xattn_bm, L1_xattn_gl, L1_xattn_bl, L1_ffn_conv_w, L1_ffn_conv_b, L1_ffn_wqkv, L1_ffn_bqkv, L1_ffn_wo, L1_ffn_bo, L1_ffn_ln1_g, L1_ffn_ln1_b, L1_ffn_gate_w, L1_ffn_gate_b, L1_ffn_w1, L1_ffn_b1, L1_ffn_w2, L1_ffn_b2, L1_ffn_ln2_g, L1_ffn_ln2_b):
    import jax
    import jax.numpy as jnp

    def _L0_attn_ref(x, in_proj_f, conv_w_f, conv_b_f, x_proj_f, dt_w_f, dt_b_f, A_log_f, D_f, out_proj_f, in_proj_b, conv_w_b, conv_b_b, x_proj_b, dt_w_b, dt_b_b, A_log_b, D_b, out_proj_b, ln_w, ln_b):
        import jax, jax.numpy as jnp
        import numpy as np
        B, L, D = (4, 128, 128)
        DI, DS, DC, DR = (256, 16, 4, 64)

        def _mamba(x, in_proj, conv_w, conv_b, x_proj, dt_w, dt_b, A_log, Dsk, out_proj):
            xz = x @ in_proj.T
            xh, z = jnp.split(xz, 2, axis=-1)
            xp = jnp.pad(xh, ((0, 0), (DC - 1, 0), (0, 0)))
            Ls = xh.shape[1]
            xc = conv_b + sum((xp[:, k:k + Ls, :] * conv_w[:, k] for k in range(DC)))
            xc = jax.nn.silu(xc)
            dbc = xc @ x_proj.T
            dt, Bm, Cm = jnp.split(dbc, [DR, DR + DS], axis=-1)
            delta = jax.nn.softplus(dt @ dt_w.T + dt_b)
            A = -jnp.exp(A_log)

            def step(h, inp):
                u_t, d_t, B_t, C_t = inp
                h = h * jnp.exp(d_t[:, :, None] * A) + (d_t * u_t)[:, :, None] * B_t[:, None, :]
                return (h, jnp.einsum('bds,bs->bd', h, C_t))
            inps = (jnp.moveaxis(xc, 1, 0), jnp.moveaxis(delta, 1, 0), jnp.moveaxis(Bm, 1, 0), jnp.moveaxis(Cm, 1, 0))
            h0 = jnp.zeros((x.shape[0], DI, DS), x.dtype)
            _, ys = jax.lax.scan(step, h0, inps)
            y = jnp.moveaxis(ys, 0, 1) + xc * Dsk
            y = y * jax.nn.silu(z)
            return y @ out_proj.T
        yf = _mamba(x, in_proj_f, conv_w_f, conv_b_f, x_proj_f, dt_w_f, dt_b_f, A_log_f, D_f, out_proj_f)
        yb = jnp.flip(_mamba(jnp.flip(x, 1), in_proj_b, conv_w_b, conv_b_b, x_proj_b, dt_w_b, dt_b_b, A_log_b, D_b, out_proj_b), 1)
        h = x + yf + yb
        mu = jnp.mean(h, axis=-1, keepdims=True)
        var = jnp.mean(jnp.square(h - mu), axis=-1, keepdims=True)
        return (h - mu) / jnp.sqrt(var + 1e-05) * ln_w + ln_b

    def _L0_xattn_ref(query, key, value, query_position_ids, Wq, bq, Wk, bk, Wv, bv, Wo, bo):
        import jax, jax.numpy as jnp
        import numpy as np
        EMBED_DIM = 128
        NUM_HEADS = 16
        HEAD_DIM = EMBED_DIM // NUM_HEADS
        ROPE_BASE = 10000.0

        def _apply_rope(q, position_ids):
            hd = q.shape[-1]
            inv_freq = 1.0 / ROPE_BASE ** (jnp.arange(0, hd, 2, dtype=jnp.float32) / hd)
            ang = position_ids.astype(jnp.float32)[:, :, None] * inv_freq
            cos = jnp.cos(ang)[:, :, None, :]
            sin = jnp.sin(ang)[:, :, None, :]
            q1, q2 = (q[..., :hd // 2], q[..., hd // 2:])
            return jnp.concatenate([q1 * cos - q2 * sin, q2 * cos + q1 * sin], axis=-1)
        B, T, D = query.shape
        M = key.shape[1]
        H, hd = (NUM_HEADS, HEAD_DIM)
        scaling = 1.0 / np.sqrt(hd)
        q = (query @ Wq.T + bq).reshape(B, T, H, hd)
        k = (key @ Wk.T + bk).reshape(B, M, H, hd)
        v = (value @ Wv.T + bv).reshape(B, M, H, hd)
        q = _apply_rope(q, query_position_ids)
        scores = jnp.einsum('bthd,bmhd->bhtm', q, k) * scaling
        attn = jax.nn.softmax(scores, axis=-1)
        out = jnp.einsum('bhtm,bmhd->bthd', attn, v).reshape(B, T, D)
        return out @ Wo.T + bo

    def _L0_ffn_ref(x, Wg, W1, W2, W3):
        import jax, jax.numpy as jnp
        import numpy as np
        E = 8
        TOP_K = 2
        DIM = 128
        HID = 256
        B, T, C = x.shape
        xf = x.reshape(-1, C)
        logits = xf @ Wg
        top_w, top_i = jax.lax.top_k(logits, TOP_K)
        top_w = jax.nn.softmax(top_w, axis=-1)
        one_hot = jax.nn.one_hot(top_i, E, dtype=xf.dtype)
        combine = jnp.einsum('nk,nke->ne', top_w, one_hot)
        h = jnp.einsum('nc,ech->enh', xf, W1)
        g = jnp.einsum('nc,ech->enh', xf, W2)
        y = jnp.einsum('enh,ehc->enc', jax.nn.silu(h) * g, W3)
        out = jnp.einsum('enc,ne->nc', y, combine)
        return out.reshape(B, T, C)

    def _L1_attn_ref(x, W_qkv, b_qkv, W_proj, b_proj):
        import jax, jax.numpy as jnp
        import numpy as np
        SPS_AMPLIFY = 1.5
        SPS_DAMPEN = 0.3
        SPS_DEEP_QUESTION = 0.1
        SPS_EXCLAIM = 0.85
        SPS_QUESTION = 0.25
        SPS_SUPER_EXCLAIM = 0.95
        B, S, D = (4, 256, 128)
        NUM_HEADS = 16
        HEAD_DIM = D // NUM_HEADS
        SCALE = HEAD_DIM ** (-0.5)

        def sps_pro(x):
            xn = jax.nn.sigmoid(x)
            mult = jnp.where(xn > SPS_SUPER_EXCLAIM, 2.0, jnp.where(xn > SPS_EXCLAIM, SPS_AMPLIFY, jnp.where(xn < SPS_DEEP_QUESTION, 0.1, jnp.where(xn < SPS_QUESTION, SPS_DAMPEN, 1.0))))
            return x * mult
        qkv = jnp.einsum('bsd,de->bse', x, W_qkv) + b_qkv
        q, k, v = jnp.split(qkv, 3, axis=-1)
        attn = jnp.einsum('bsd,btd->bst', q, k) * SCALE
        attn = sps_pro(attn)
        attn = jax.nn.softmax(attn, axis=-1)
        out = jnp.einsum('bst,btd->bsd', attn, v)
        out = jnp.einsum('bsd,de->bse', out, W_proj) + b_proj
        return out

    def _L1_xattn_ref(x, latents, Wq, Wkv, Wout, gm, bm, gl, bl):
        import jax, jax.numpy as jnp
        import numpy as np
        D_MODEL = 128
        D_HEAD = 64
        NHEADS = 8
        IN_DIM = D_HEAD * NHEADS
        EPS = 1e-05

        def layernorm(x, g, b):
            mu = jnp.mean(x, axis=-1, keepdims=True)
            var = jnp.var(x, axis=-1, keepdims=True)
            return (x - mu) * jax.lax.rsqrt(var + EPS) * g + b
        scale = D_HEAD ** (-0.5)
        xn = layernorm(x, gm, bm)
        ln = layernorm(latents, gl, bl)
        q = ln @ Wq
        kv_input = jnp.concatenate([xn, ln], axis=-2)
        kv = kv_input @ Wkv
        k, v = jnp.split(kv, 2, axis=-1)

        def heads(t):
            B, S, _ = t.shape
            return t.reshape(B, S, NHEADS, D_HEAD).transpose(0, 2, 1, 3)
        q, k, v = (heads(q), heads(k), heads(v))
        q = q / scale
        sim = jnp.einsum('bhid,bhjd->bhij', q, k)
        sim = sim - jax.lax.stop_gradient(jnp.max(sim, axis=-1, keepdims=True))
        attn = jax.nn.softmax(sim, axis=-1)
        out = jnp.einsum('bhij,bhjd->bhid', attn, v)
        B, H, L, dh = out.shape
        out = out.transpose(0, 2, 1, 3).reshape(B, L, H * dh)
        return out @ Wout

    def _L1_ffn_ref(x, conv_w, conv_b, wqkv, bqkv, wo, bo, ln1_g, ln1_b, gate_w, gate_b, w1, b1, w2, b2, ln2_g, ln2_b):
        import jax, jax.numpy as jnp
        import numpy as np
        DIM, HEADS, EXPERTS, DFF = (128, 16, 8, 512)
        EPS = 1e-05

        def layernorm(x, g, b):
            mu = jnp.mean(x, -1, keepdims=True)
            var = jnp.mean(jnp.square(x - mu), -1, keepdims=True)
            return (x - mu) * jax.lax.rsqrt(var + EPS) * g + b
        B, S, D = x.shape
        H, dh = (HEADS, D // HEADS)
        xt = jnp.transpose(x, (0, 2, 1))
        xt = jax.lax.conv_general_dilated(xt, conv_w, (1,), [(1, 1)], dimension_numbers=('NCH', 'OIH', 'NCH'))
        x = jnp.transpose(xt + conv_b[None, :, None], (0, 2, 1))
        qkv = x @ wqkv.T + bqkv
        q, k, v = jnp.split(qkv, 3, axis=-1)
        q = q.reshape(B, S, H, dh).transpose(0, 2, 1, 3)
        k = k.reshape(B, S, H, dh).transpose(0, 2, 1, 3)
        v = v.reshape(B, S, H, dh).transpose(0, 2, 1, 3)
        scores = jnp.einsum('bhqd,bhkd->bhqk', q, k) / jnp.sqrt(jnp.float32(dh))
        attn = jax.nn.softmax(scores, axis=-1)
        ctx = jnp.einsum('bhqk,bhkd->bhqd', attn, v)
        ctx = ctx.transpose(0, 2, 1, 3).reshape(B, S, D)
        attn_out = ctx @ wo.T + bo
        x = layernorm(x + attn_out, ln1_g, ln1_b)
        probs = jax.nn.softmax(x @ gate_w + gate_b, axis=-1)
        h = jax.nn.relu(jnp.einsum('bsd,edf->bsef', x, w1) + b1)
        y = jnp.einsum('bsef,efd->bsed', h, w2) + b2
        moe_out = jnp.einsum('bse,bsed->bsd', probs, y)
        x = layernorm(x + moe_out, ln2_g, ln2_b)
        return x
    x = x + _L0_attn_ref(_layernorm(x, axis=-1), L0_attn_in_proj_f, L0_attn_conv_w_f, L0_attn_conv_b_f, L0_attn_x_proj_f, L0_attn_dt_w_f, L0_attn_dt_b_f, L0_attn_A_log_f, L0_attn_D_f, L0_attn_out_proj_f, L0_attn_in_proj_b, L0_attn_conv_w_b, L0_attn_conv_b_b, L0_attn_x_proj_b, L0_attn_dt_w_b, L0_attn_dt_b_b, L0_attn_A_log_b, L0_attn_D_b, L0_attn_out_proj_b, L0_attn_ln_w, L0_attn_ln_b)
    x = x + _L0_xattn_ref(_layernorm(x, axis=-1), ctx_1024, ctx_1024, itok_BxS_1_4095, L0_xattn_Wq, L0_xattn_bq, L0_xattn_Wk, L0_xattn_bk, L0_xattn_Wv, L0_xattn_bv, L0_xattn_Wo, L0_xattn_bo)
    x = x + _L0_ffn_ref(_layernorm(x, axis=-1), L0_ffn_Wg, L0_ffn_W1, L0_ffn_W2, L0_ffn_W3)
    x = x + _L1_attn_ref(_layernorm(x, axis=-1), L1_attn_W_qkv, L1_attn_b_qkv, L1_attn_W_proj, L1_attn_b_proj)
    x = x + _L1_xattn_ref(ctx_1024, _layernorm(x, axis=-1), L1_xattn_Wq, L1_xattn_Wkv, L1_xattn_Wout, L1_xattn_gm, L1_xattn_bm, L1_xattn_gl, L1_xattn_bl)
    x = x + _L1_ffn_ref(_layernorm(x, axis=-1), L1_ffn_conv_w, L1_ffn_conv_b, L1_ffn_wqkv, L1_ffn_bqkv, L1_ffn_wo, L1_ffn_bo, L1_ffn_ln1_g, L1_ffn_ln1_b, L1_ffn_gate_w, L1_ffn_gate_b, L1_ffn_w1, L1_ffn_b1, L1_ffn_w2, L1_ffn_b2, L1_ffn_ln2_g, L1_ffn_ln2_b)
    return x

_drawn_inputs = setup_inputs


def setup_inputs(seed=0):
    import zlib

    import numpy as np

    out = dict(_drawn_inputs(seed))
    spreads = {'L0_attn_D_f': (1.0, 0.6),
     'L0_attn_D_b': (1.0, 0.6),
     'L0_attn_ln_w': (1.0, 0.2),
     'L0_attn_ln_b': (0.0, 0.1),
     'L0_xattn_bq': (0.0, 0.1),
     'L0_xattn_bk': (0.0, 0.8),
     'L0_xattn_bv': (0.0, 0.1),
     'L0_xattn_bo': (0.0, 0.1),
     'L1_xattn_gm': (1.0, 0.2),
     'L1_xattn_bm': (0.0, 0.1),
     'L1_xattn_gl': (1.0, 0.2),
     'L1_xattn_bl': (0.0, 0.1),
     'L1_ffn_conv_b': (0.0, 0.1),
     'L1_ffn_bqkv': (0.0, 0.1),
     'L1_ffn_bo': (0.0, 0.1),
     'L1_ffn_ln1_g': (1.0, 0.2),
     'L1_ffn_ln1_b': (0.0, 0.1),
     'L1_ffn_gate_b': (0.0, 0.8),
     'L1_ffn_b1': (0.0, 0.624),
     'L1_ffn_b2': (0.0, 0.434),
     'L1_ffn_ln2_g': (1.0, 0.2),
     'L1_ffn_ln2_b': (0.0, 0.1)}
    factors = {'L0_attn_in_proj_f': 8.0,
     'L0_attn_conv_w_f': 8.0,
     'L0_attn_conv_b_f': 8.0,
     'L0_attn_x_proj_f': 8.0,
     'L0_attn_dt_w_f': 8.0,
     'L0_attn_dt_b_f': 8.0,
     'L0_attn_A_log_f': 8.0,
     'L0_attn_out_proj_f': 6.584,
     'L0_attn_in_proj_b': 8.0,
     'L0_attn_conv_w_b': 7.368,
     'L0_attn_conv_b_b': 8.0,
     'L0_attn_x_proj_b': 8.0,
     'L0_attn_dt_w_b': 8.0,
     'L0_attn_dt_b_b': 8.0,
     'L0_attn_A_log_b': 8.0,
     'L0_attn_out_proj_b': 6.893,
     'L0_ffn_Wg': 4.784,
     'L0_ffn_W1': 3.979,
     'L0_ffn_W2': 4.035,
     'L0_ffn_W3': 3.953}
    for name, (base, spread) in spreads.items():
        noise = np.random.default_rng([zlib.crc32(name.encode()), seed]).standard_normal(out[name].shape)
        drawn = base * np.exp(spread * noise) if base else spread * noise
        out[name] = jnp.asarray(drawn.astype(out[name].dtype))
    for name, factor in factors.items():
        out[name] = (out[name] * factor).astype(out[name].dtype)
    return out
```

```python
from contextlib import ExitStack

import numpy as np

import concourse.bass as bass
from concourse import mybir

F32 = mybir.dt.float32
BF16 = mybir.dt.bfloat16
I32 = mybir.dt.int32
U32 = mybir.dt.uint32
ALU = mybir.AluOpType
ACT = mybir.ActivationFunctionType
AX = mybir.AxisListType.X

B, T, D = 8, 128, 128
N = B * T
M = 77
H0, HD0 = 16, 8
DI, DS, DC, DR = 256, 16, 4, 64
NC = DI // 128
E0, HID0 = 8, 256
H1, HD1 = 8, 64
J1 = M + T
E1, HID1 = 8, 512
EPS = 1e-5
MAGIC = 1.5 * 2.0 ** 23
TWO_PI = (6.28125, 0.0019350051879882812, 3.0198604e-07)
HALF = N // 2

ROWS = ["ln_w", "ln_b", "gm", "bm", "gl", "bl", "ln1_g", "ln1_b", "ln2_g", "ln2_b",
        "x0_bq", "x0_bv", "x0_bo", "a1_bv", "a1_bproj", "conv_b", "f1_bv", "f1_bo", "gate_b"]


class Steps:

    def __init__(self, sem, order):
        self.sem, self.order, self.n = sem, list(order), 0
        self.value = {k: i + 1 for i, k in enumerate(self.order)}
        assert len(self.value) == len(self.order)

    def at(self, *key):
        return self.sem, self.value[key]

    def did(self, *key):
        assert self.order[self.n] == key, (self.order[self.n], key)
        self.n += 1
        return self.sem, 1


def pairs(*groups):
    return [(g, 2 * i + s) for i in range(B // 2) for g in groups for s in range(2)]


def decoder_kernel(nc, x, ctx, ctx_t, pos, w_m, dtw_t, consts, rows, cols, w_x0, w_f0, w_a1, w_x1, w_f1, b2, out):
    with ExitStack() as stack:
        def sb(name, shape, dt=F32):
            return stack.enter_context(nc.sbuf_tensor(name, shape, dt))

        def sem(name):
            return stack.enter_context(nc.semaphore(name))

        X = sb("residual", [T, B, D])
        XNT = sb("normed_t", [D, B, T])
        CTX = sb("context", [M, B, D])
        CTXT = sb("context_t", [D, B, M])
        KT0 = sb("x0_keys_t", [D, B, M])
        V0 = sb("x0_values", [M, B, H0, HD0 + 1])
        KVT = sb("x1_kv_input_t", [D, B, J1])
        WM = sb("w_m", [128, w_m.shape[1]])
        DTW = sb("dt_w_t", [DR, 2, DI])
        SEL = sb("row_selectors", [128, 2 * DS], BF16)
        CONST = sb("consts", [128, consts.shape[1]])
        ROW = sb("rows", [128, len(ROWS) * D])
        COL = sb("cols", [128, cols.shape[1]])
        WX0 = sb("w_x0", [128, w_x0.shape[1]])
        WF0 = sb("w_f0", [128, w_f0.shape[1]])
        WA1 = sb("w_a1", [128, w_a1.shape[1]])
        WX1 = WM[:, 0:w_x1.shape[1]]
        WF1 = sb("w_f1", [128, w_f1.shape[1]])
        B2 = sb("moe1_b2", [E1, D])
        POSI = sb("positions", [T, B], I32)
        ROPE = sb("rope_tables", [T, 2, B, 2, 4])
        ONES = sb("ones", [128, 128])
        HALFNEG = sb("minus_half", [128, B])
        DIAG = sb("diag_D", [128, 2, NC, 128])
        NEGA = sb("neg_A", [128, 2, NC, DS])
        ST6 = sb("bn_stats", [128, B, 6])
        MV = sb("mean_var", [128, B, 2])
        RS = sb("rstd", [128, B])
        SMALL = sb("small", [128, 8, B, 8])
        TOPI = sb("top_index", [128, B, 8], U32)
        PS = stack.enter_context(nc.psum_tensor("ps", [128, 8, 512], F32))

        ARENA_N = 22016
        ARENA = sb("arena", [128, ARENA_N])

        class Region:
            def __init__(self, start=0, of=None):
                self.o, self.of = start, ARENA if of is None else of

            def take(self, *shape):
                n = int(np.prod(shape))
                v = self.of[:, self.o:self.o + n]
                self.o += n
                assert self.o <= self.of.shape[1], self.o
                if len(shape) > 1:
                    names = "abcd"[:len(shape)]
                    v = v.rearrange(f"p ({' '.join(names)}) -> p {' '.join(names)}",
                                    **{k: s for k, s in zip(names[1:], shape[1:])})
                return v

        r = Region()
        XN = r.take(B, D)
        ZS = r.take(2, NC, N)
        U = [r.take(NC, N)]
        DELTA = [r.take(NC, N)]
        S3 = [r.take(N // 2).bitcast(BF16)]
        m_shared = r.o
        DA = r.take(2, NC, N)
        HB = [r.take(NC, N) for _ in range(2)]
        BS = r.take(2, N)
        CS = r.take(2, N)
        q = Region(m_shared)
        SPL = ARENA[:, m_shared:m_shared + NC * N].rearrange("p (c n) -> p c n", c=NC)
        DTS = q.take(N)
        RES = q.take(N)
        SPR = q.take(NC, N)
        SPE = q.take(NC, N)
        SPT = ARENA[:, q.o:q.o + NC * N]
        XP = [q.take(NC, B, T + DC - 1)]
        SMALLE = q.take(NC * N).bitcast(I32)
        f = Region(0, WF1)
        XP.append(f.take(NC, B, T + DC - 1))
        f = Region(0, WF1)
        HB += [f.take(NC, N) for _ in range(2)]
        U.append(f.take(NC, N))
        DELTA.append(f.take(NC, N))
        S3.append(f.take(N // 2).bitcast(BF16))

        slot = []
        for s in range(2):
            r = Region(s * (ARENA_N // 2))
            v = dict(xn=r.take(D), xt=r.take(D), q=r.take(D), r1=r.take(D), r2=r.take(D), qr=r.take(D), qt=r.take(D),
                     o=r.take(H1 * HD1), ot=r.take(4, D), mx=r.take(H0), rz=r.take(H0), mx1=r.take(1), st=r.take(6),
                     mv=r.take(2), var=r.take(1), rs=r.take(1), st2=r.take(6), mv2=r.take(2), var2=r.take(1),
                     rs2=r.take(1), y=r.take(D), yt=r.take(D), kt=r.take(D), l1=r.take(D), l2=r.take(D),
                     v1=r.take(H0, HD0 + 1), xp=r.take(T + 2))
            big = r.o
            v.update(p=r.take(2048), pt=r.take(2048), kx=r.take(2048))
            r = Region(big)
            v.update(p1=r.take(H1 * J1), pta=r.take(H1, T), ptb=r.take(H1, T), qt1=r.take(4, T), kt1=r.take(4, J1),
                     va=r.take(H1, HD1 + 1), vb=r.take(H1, HD1 + 1))
            slot.append(v)
        r = Region()
        ACTS = r.take(4, HALF)
        ACTB = r.take(4, HALF)
        XA = r.take(B, D)
        XAT = r.take(B, T)
        PROB = r.take(B, E1)
        PROBT = r.take(B, T)
        FIN = r.take(B, D)
        XN1 = XNT[:, :, :]
        XAT1 = KVT[:, :, :].rearrange("p b j -> p (b j)")[:, 0:N].rearrange("p (b t) -> p b t", b=B)

        def row(name, n=D, p=128):
            i = ROWS.index(name)
            return ROW[0:p, i * D:i * D + n]

        def row_b(name, p=128):
            return row(name, D, p).unsqueeze(1).to_broadcast([p, B, D])

        IDN = CONST[:, 0:128]
        MASK = CONST[:, 128:128 + H0]
        FREQ = CONST[:, 144:148]
        IOTA = CONST[:, 148:156]
        c0 = [0]

        def col(n):
            c0[0] += n
            return COL[:, c0[0] - n:c0[0]]

        CONVW = [col(NC * DC).rearrange("p (c k) -> p c k", c=NC) for _ in range(2)]
        CONVB = [col(NC) for _ in range(2)]
        DTB = [col(NC) for _ in range(2)]
        DSK = [col(NC) for _ in range(2)]
        ALOG = col(2 * NC * DS)
        X0BK = col(1)
        A1B = col(2)
        F1B = col(2)
        B1 = col(E1 * 4).rearrange("p (e c) -> p e c", e=E1)

        def split(t, *sizes):
            o, parts = 0, []
            for n in sizes:
                parts.append(t[:, o:o + n])
                o += n
            return parts

        m_in, m_dt, m_bc, m_out = split(WM, 2 * 512, 2 * NC * DR, 2 * NC * 96, 2 * NC * 128)
        WIN = m_in.rearrange("p (d n) -> p d n", d=2)
        WDT = m_dt.rearrange("p (d c n) -> p d c n", d=2, c=NC)
        WBC = m_bc.rearrange("p (d c n) -> p d c n", d=2, c=NC)
        WOUT = m_out.rearrange("p (d c n) -> p d c n", d=2, c=NC)
        X0Q, X0K, X0V, X0O = split(WX0, D, D, D, D)
        f_g, f_1, f_2, f_3 = split(WF0, E0, E0 * HID0, E0 * HID0, E0 * 2 * D)
        FW = [f_1.rearrange("p (e n) -> p e n", e=E0), f_2.rearrange("p (e n) -> p e n", e=E0)]
        FW3 = f_3.rearrange("p (e c n) -> p e c n", e=E0, c=2)
        A1W, A1P = split(WA1, 3 * D, D)
        X1Q, X1KV, x1_o = split(WX1, 512, 1024, 4 * D)
        X1O = x1_o.rearrange("p (c n) -> p c n", c=4)
        g_c, G_QKV, G_O, G_G, g_1, g_2 = split(WF1, 3 * D, 3 * D, D, E1, E1 * HID1, E1 * 4 * D)
        GC = g_c.rearrange("p (k n) -> p k n", k=3)
        G1 = g_1.rearrange("p (e n) -> p e n", e=E1)
        G2 = g_2.rearrange("p (e c n) -> p e c n", e=E1, c=4)

        def bank(i, n=1):
            v = PS[:, i:i + n, :]
            return v.rearrange("p a b -> p (a b)")

        ld_x, ld_m, ld_c, ld_ctx, ld_w1, ld_w2, ld_x1 = (sem(f"loaded_{n}") for n in ("x", "m", "c", "ctx", "w1", "w2", "x1"))
        stored = sem("stored")

        both = range(2)
        mpe = Steps(sem("pe_mamba"), [("kt0",), ("v0",), ("ct",), ("xnt",)] + [
            (k, d) for d in both for k in ("xz0", "xz1", "xz2", "xz3")] + [
            (k, d) for d in both for k in ("dbc", "dt0", "dt1")] + [("y0", 0), ("y0", 1), ("out",)])
        mact = Steps(sem("act_mamba"), [("nega",), ("kt0",), ("sin_abs",), ("sin",), ("ct",), ("xnt",)] + [
            (k, d) for d in both for k in ("xp", "zs")] + [("u", 0), ("u", 1)] + [
            (k, d) for d in both for k in ("dts", "relu0", "abs0", "relu1", "abs1", "exp", "ln")])
        mdve = Steps(sem("dve_mamba"), [("const",), ("stats",), ("mv",), ("var",), ("xn",), ("cstats",), ("cmv",), ("cvar",)]
                     + [("cn",), ("cg",), ("cb",), ("v0",)]
                     + [(f"rope{i}",) for i in range(9)] + [("rope",), ("nega",), ("diag",)] + [
            (k, d) for d in both for k in ("pad", "tap0", "tap1", "tap2", "conv")] + [
            (k, d) for d in both for k in ("s3a", "s3b", "s3c", "s3d", "s3",
                                           "poly0", "poly1", "poly", "small", "pick", "delta0", "delta")] + [
            (k, d) for d in both for k in ("du", "edge", "y")] + [
            ("h",), ("hstats",), ("hmv",), ("hvar",), ("hn",), ("hg",), ("hb",), ("x",)])
        mpool = Steps(sem("pool_mamba"), [("rstd",), ("crstd",), ("hrstd",)])
        CREDIT = 4
        names = ["b_ps", "c_ps", "b_sb", "c_sb", "da0", "da1", "bu0", "bu1", "h0", "h1", "hc0", "hc1", "yacc"]
        L = {k: sem("state_" + k) for k in names}

        X0 = {"pe": ("xt", "q", "qt", "sc", "pt0", "pt1", "pv", "ot", "wo"),
              "act": ("xt", "qt", "p", "pt0", "ot"),
              "dve": ("stats", "mv", "var", "xn", "rope_a", "rope", "mx", "sub", "pt1", "rz", "o", "res"),
              "pool": ("rstd", "kx")}
        x0 = {e: Steps(sem(f"{e}_x0"), pairs(*X0[e])) for e in X0}

        def units(n):
            return [(h, e, c) for h in range(2) for e in range(E0) for c in range(n)]

        def moe_steps(name, n, first, act_unit, dve_extra_first, dve_last):
            us = units(n)
            pe = list(first["pe"])
            ev = [("hg",) + us[0]]
            for i, u in enumerate(us):
                if i + 1 < len(us):
                    ev.append(("hg",) + us[i + 1])
                if u[2] == n - 1:
                    ev.append(("y",) + u[:2])
                else:
                    ev.append(("yp",) + u)
            a = [(act_unit,) + u for u in us]
            dv = []
            prev = None
            for u in us:
                if dve_extra_first:
                    dv.append(("act",) + u)
                if u[2] == n - 1:
                    if prev is not None:
                        dv.append(("acc",) + prev)
                    prev = u[:2]
            dv.append(("acc",) + prev)
            return {"pe": Steps(sem(f"pe_{name}"), pe + ev),
                    "act": Steps(sem(f"act_{name}"), list(first["act"]) + a),
                    "dve": Steps(sem(f"dve_{name}"), list(first["dve"]) + dv + list(dve_last)),
                    "pool": Steps(sem(f"pool_{name}"), first["pool"])}

        f0 = moe_steps("f0", 2, {
            "pe": [("xnt",), ("gate",)], "act": [("xnt",), ("top_exp",)],
            "dve": [(k,) for k in ("stats", "mv", "var", "xn", "lg", "max", "index", "top_i", "dif", "den", "w1", "w2",
                                   "s1", "s2", "s1w", "s2w", "comb")],
            "pool": [("rstd",)]}, "silu", True, [])
        A1 = {"pe": ("xt", "q", "k", "v", "s", "pt", "o", "out"),
              "act": ("xt", "q", "k", "p", "pt", "o"),
              "dve": ("stats", "mv", "var", "xn", "v", "a", "g1", "l1", "g", "l", "ls", "m", "am", "mx", "nmx", "rz", "y", "res"),
              "pool": ("rstd",)}
        a1 = {e: Steps(sem(f"{e}_a1"), pairs(*A1[e])) for e in A1}
        X1 = {"pe": ("lt", "q", "k", "v", "s", "pt", "o", "ot", "out"),
              "act": ("lt", "q", "k", "p", "pta", "ot"),
              "dve": ("stats", "mv", "var", "xn", "stats2", "mv2", "var2", "l0", "l1", "l2", "v", "mx", "sub", "ptb", "rz", "o", "res"),
              "pool": ("rstd", "rstd2")}
        x1 = {e: Steps(sem(f"{e}_x1"), [("ones", 0)] * (e == "dve") + pairs(*X1[e])) for e in X1}
        G1S = {"pe": ("xt", "y", "yt", "q", "k", "v", "s", "pt0", "pt1", "pv", "ot", "wo", "xat", "gate"),
               "act": ("xt", "yt", "q", "k", "p", "pt0", "ot", "xat"),
               "dve": ("stats", "mv", "var", "xn", "y", "v", "mx", "sub", "pt1", "rz", "o", "h", "stats2", "mv2", "var2",
                       "l0", "l1", "xa", "lg"),
               "pool": ("rstd", "kx", "rstd2")}
        g1 = {e: Steps(sem(f"{e}_g1"), [("ones", 0)] * (e == "dve") + pairs(*G1S[e])) for e in G1S}
        f1 = moe_steps("f1", 4, {
            "pe": [("pt",), ("b2",)], "act": [("gexp",), ("pt",)],
            "dve": [(k,) for k in ("gmx", "gsub", "gsum", "grz", "prob", "b2")],
            "pool": [("rstd",)]}, "relu", False,
            [("stats",), ("mv",), ("var",), ("xn",), ("g",), ("b",), ("fin",)])

        block = stack.enter_context(nc.Block())

        @block.sync
        def _(sp):
            sp.dma_start(X[:, :, :], x.rearrange("b t c -> t b c")).then_inc(ld_x, 16)
            sp.dma_start(CONST[:, :], consts).then_inc(ld_x, 16)
            sp.dma_start(WM[:, :], w_m).then_inc(ld_m, 16)
            sp.dma_start(COL[:, :], cols).then_inc(ld_c, 16)
            sp.dma_start(ROW[:, :], rows.to_broadcast([128, rows.shape[1]])).then_inc(ld_c, 16)
            sp.dma_start(POSI[:, :], pos).then_inc(ld_c, 16)
            sp.dma_start(CTXT[:, :, :], ctx_t).then_inc(ld_ctx, 16)
            sp.dma_start(CTX[:, :, :], ctx.rearrange("b t c -> t b c")).then_inc(ld_ctx, 16)
            sp.dma_start(WX0[:, :], w_x0).then_inc(ld_ctx, 16)
            sp.dma_start(DTW[:, :, :], dtw_t).then_inc(ld_m, 16)
            for dst, src in ((WF0, w_f0), (WA1, w_a1)):
                sp.dma_start(dst[:, :], src).then_inc(ld_w1, 16)
            sp.dma_start(B2[:, :], b2).then_inc(ld_w2, 16)
            sp.wait_ge(*mpe.at("out"))
            sp.dma_start(WX1, w_x1).then_inc(ld_x1, 16)
            sp.dma_start(WF1[:, :], w_f1).then_inc(ld_w2, 16)
            sp.wait_ge(*f1["dve"].at("fin"))
            sp.dma_start(out.rearrange("b t c -> t b c"), FIN).then_inc(stored, 16)
            sp.wait_ge(stored, 16)

        @block.vector
        def _(dve):
            def stats_all(S, src, p, a, b_, c, at_=None):
                for b in range(B):
                    i = dve.bn_stats(ST6[0:p, b, :], src[0:p, b, :])
                i.then_inc(*S.did(a))
                dve.wait_ge(*S.at(a))
                for b in range(B):
                    i = dve.bn_aggr(MV[0:p, b, :], ST6[0:p, b, :])
                i.then_inc(*S.did(b_))
                dve.wait_ge(*S.at(b_))
                dve.tensor_scalar(RS[0:p, :], MV[0:p, :, 1], EPS, None, ALU.add).then_inc(*S.did(c))

            def norm_all(S, dst, src, p, step):
                for b in range(B):
                    i = dve.tensor_scalar(dst[0:p, b, :], src[0:p, b, :], MV[0:p, b, 0:1], RS[0:p, b:b + 1],
                                          ALU.subtract, ALU.mult)
                i.then_inc(*S.did(step))

            dve.memset(ONES[:, :], 1.0)
            dve.memset(HALFNEG[:, :], -0.5)
            dve.memset(V0[:, :, :, HD0:HD0 + 1], 1.0)
            dve.memset(S3[0][96:128, :], 0.0)
            dve.memset(S3[1][96:128, :], 0.0).then_inc(*mdve.did("const"))
            dve.wait_ge(ld_x, 32)
            dve.tensor_copy(SEL[:, :], CONST[:, 156:156 + 2 * DS])
            stats_all(mdve, X, 128, "stats", "mv", "var")
            dve.wait_ge(*mpool.at("rstd"))
            norm_all(mdve, XN, X, 128, "xn")
            dve.wait_ge(ld_ctx, 48)
            dve.wait_ge(*mdve.at("xn"))
            stats_all(mdve, CTX, M, "cstats", "cmv", "cvar")
            dve.wait_ge(*mpool.at("crstd"))
            norm_all(mdve, CTX, CTX, M, "cn")
            dve.wait_ge(ld_c, 48)
            dve.wait_ge(*mdve.at("cn"))
            dve.tensor_tensor(CTX[:, :, :], CTX[:, :, :], row_b("gm", M), ALU.mult).then_inc(*mdve.did("cg"))
            dve.wait_ge(*mdve.at("cg"))
            dve.tensor_tensor(CTX[:, :, :], CTX[:, :, :], row_b("bm", M), ALU.add).then_inc(*mdve.did("cb"))
            dve.wait_ge(*mpe.at("v0"))
            for g in range(2):
                i = dve.tensor_copy(V0[:, 4 * g:4 * g + 4, :, 0:HD0].rearrange("p b h d -> p (b h) d"),
                                    bank(2 + g)[0:M, :].rearrange("p (h d) -> p h d", d=HD0))
            i.then_inc(*mdve.did("v0"))
            posf, ang, k, rr = (SMALL[:, i, :, 0:4] for i in range(4))
            dve.tensor_copy(SMALL[:, 4, :, 0:1], POSI[:, :].unsqueeze(2)).then_inc(*mdve.did("rope0"))
            dve.wait_ge(*mdve.at("rope0"))
            dve.tensor_tensor(ang, SMALL[:, 4, :, 0:1].to_broadcast([T, B, 4]),
                              FREQ.unsqueeze(1).to_broadcast([T, B, 4]), ALU.mult).then_inc(*mdve.did("rope1"))
            dve.wait_ge(*mdve.at("rope1"))
            dve.tensor_scalar(k, ang, float(1 / (2 * np.pi)), MAGIC, ALU.mult, ALU.add).then_inc(*mdve.did("rope2"))
            dve.wait_ge(*mdve.at("rope2"))
            dve.tensor_scalar(k, k, -MAGIC, None, ALU.add).then_inc(*mdve.did("rope3"))
            for i, part in enumerate(TWO_PI):
                dve.wait_ge(*mdve.at(f"rope{3 + i}"))
                dve.scalar_tensor_tensor(ang, k, -part, ang, ALU.mult, ALU.add).then_inc(*mdve.did(f"rope{4 + i}"))
            dve.wait_ge(*mdve.at("rope6"))
            pi = float(np.float32(3.1415925))
            dve.tensor_scalar(ang, ang, pi, -pi, ALU.min, ALU.max).then_inc(*mdve.did("rope7"))
            dve.wait_ge(*mact.at("sin_abs"))
            dve.tensor_scalar(rr, rr, -1.0, float(np.pi / 2), ALU.mult, ALU.add).then_inc(*mdve.did("rope8"))
            dve.wait_ge(*mact.at("sin"))
            for g in range(2):
                dve.tensor_copy(ROPE[:, 0, :, g, :], SMALL[:, 5, :, 0:4])
            dve.tensor_scalar(ROPE[:, 1, :, 0, :], SMALL[:, 6, :, 0:4], -1.0, None, ALU.mult)
            dve.tensor_copy(ROPE[:, 1, :, 1, :], SMALL[:, 6, :, 0:4]).then_inc(*mdve.did("rope"))
            dve.wait_ge(*mact.at("nega"))
            na = NEGA[:, :, :, :].rearrange("p a b c -> p (a b c)")
            dve.tensor_scalar(na, na, -1.0, None, ALU.mult).then_inc(*mdve.did("nega"))
            for d in range(2):
                for c in range(NC):
                    i = dve.tensor_scalar(DIAG[:, d, c, :], IDN, DSK[d][:, c:c + 1], None, ALU.mult)
            i.then_inc(*mdve.did("diag"))

            for d in range(2):
                pad = slice(0, DC - 1) if d == 0 else slice(T, T + DC - 1)
                dve.memset(XP[d][:, :, :, pad], 0.0).then_inc(*mdve.did("pad", d))
                dve.wait_ge(*mact.at("xp", d))
                dve.wait_ge(*mdve.at("pad", d))
                for kk in range(DC):
                    shift = kk if d == 0 else DC - 1 - kk
                    for c in range(NC):
                        src = XP[d][:, c, :, shift:shift + T]
                        dst = U[d][:, c, :].rearrange("p (b t) -> p b t", b=B)
                        if kk == 0:
                            i = dve.tensor_scalar(dst, src, CONVW[d][:, c, 0:1], CONVB[d][:, c:c + 1], ALU.mult, ALU.add)
                        else:
                            i = dve.scalar_tensor_tensor(dst, src, CONVW[d][:, c, kk:kk + 1], dst, ALU.mult, ALU.add)
                    i.then_inc(*mdve.did(("tap0", "tap1", "tap2", "conv")[kk], d))
                    dve.wait_ge(*mdve.at(("tap0", "tap1", "tap2", "conv")[kk], d))
            for d in range(2):
                src, s3 = bank(2, 2), S3[d]
                dve.wait_ge(*mpe.at("dbc", d))
                dve.tensor_copy(s3[0:96, :], src[0:96, :]).then_inc(*mdve.did("s3a", d))
                dve.wait_ge(*mdve.at("s3a", d))
                dve.tensor_tensor(RES[0:64, :], src[0:64, :], s3[0:64, :], ALU.subtract).then_inc(*mdve.did("s3b", d))
                dve.wait_ge(*mdve.at("s3b", d))
                dve.tensor_copy(s3[0:64, :], RES[0:64, :]).then_inc(*mdve.did("s3c", d))
                dve.wait_ge(*mdve.at("s3c", d))
                dve.tensor_tensor(RES[0:32, :], RES[0:32, :], s3[0:32, :], ALU.subtract).then_inc(*mdve.did("s3d", d))
                dve.wait_ge(*mdve.at("s3d", d))
                dve.tensor_copy(s3[0:32, :], RES[0:32, :]).then_inc(*mdve.did("s3", d))
                e_ = SPE.rearrange("p c n -> p (c n)")
                dve.wait_ge(*mact.at("exp", d))
                dve.tensor_scalar(SPT, e_, 1.0 / 3.0, -0.5, ALU.mult, ALU.add).then_inc(*mdve.did("poly0", d))
                dve.wait_ge(*mdve.at("poly0", d))
                dve.tensor_tensor(SPT, SPT, e_, ALU.mult).then_inc(*mdve.did("poly1", d))
                dve.wait_ge(*mdve.at("poly1", d))
                dve.scalar_tensor_tensor(SPT, SPT, 1.0, e_, ALU.add, ALU.mult).then_inc(*mdve.did("poly", d))
                dve.tensor_scalar(SMALLE, e_, 2.0 ** -6, None, ALU.is_lt).then_inc(*mdve.did("small", d))
                dve.wait_ge(*mact.at("ln", d))
                dve.wait_ge(*mdve.at("small", d))
                dve.copy_predicated(SPL.rearrange("p c n -> p (c n)"), SMALLE, SPT).then_inc(*mdve.did("pick", d))
                dve.wait_ge(*mdve.at("pick", d))
                for c in range(NC):
                    i = dve.tensor_tensor(DELTA[d][:, c, :], SPR[:, c, :], SPL[:, c, :], ALU.add)
                    i.then_inc(*mdve.did("delta0" if c == 0 else "delta", d))
            dve.wait_ge(*mdve.at("delta", 1))

            for d in range(2):
                dve.wait_ge(*mpe.at("y0", d))
                for c in range(NC):
                    i = dve.tensor_tensor(U[d][:, c, :], DELTA[d][:, c, :], U[d][:, c, :], ALU.mult)
                i.then_inc(*mdve.did("du", d))
                edge = slice(0, 1) if d == 0 else slice(T - 1, T)
                dav = DA.rearrange("p s c (b t) -> p (s c b) t", b=B)
                dve.memset(dav[:, :, edge], 0.0).then_inc(*mdve.did("edge", d))
                if d == 0:
                    for kx in ("bu0", "h0", "h1", "hc0"):
                        dve.nop().then_inc(L[kx], CREDIT)
                dve.wait_ge(*mdve.at("edge", d))
                order = slice(None) if d == 0 else slice(None, None, -1)
                with dve.Fori(0, DS // 4) as it:
                    for s in range(4):
                        n = it * 4 + (s + d * DS + CREDIT)
                        h0, h1 = HB[s][:, 0, :], HB[s][:, 1, :]
                        dve.wait_ge(L["b_sb"], n + 1)
                        dve.wait_ge(L["yacc"], n - 3)
                        dve.tensor_tensor(h0, U[d][:, 0, :], BS[:, s % 2, :], ALU.mult).then_inc(L["bu0"], 1)
                        dve.wait_ge(L["bu1"], n + 1)
                        dve.wait_ge(L["da1"], n + 1)
                        dve.tensor_tensor_scan(h1[:, order], DA[:, s % 2, 1, order], h1[:, order], 0.0,
                                               ALU.mult, ALU.add).then_inc(L["h1"], 1)
                        dve.wait_ge(L["bu0"], n + 1)
                        dve.wait_ge(L["da0"], n + 1)
                        dve.tensor_tensor_scan(h0[:, order], DA[:, s % 2, 0, order], h0[:, order], 0.0,
                                               ALU.mult, ALU.add).then_inc(L["h0"], 1)
                        dve.wait_ge(L["c_sb"], n + 1)
                        dve.wait_ge(L["h0"], n + 1)
                        dve.tensor_tensor(h0, h0, CS[:, s % 2, :], ALU.mult).then_inc(L["hc0"], 1)
                dve.wait_ge(L["yacc"], CREDIT + (d + 1) * DS)
                for c in range(NC):
                    i = dve.tensor_tensor(ZS[:, d, c, :], bank(4 + 2 * c, 2), ZS[:, d, c, :], ALU.mult)
                i.then_inc(*mdve.did("y", d))

            dve.wait_ge(*mpe.at("out"))
            xnf = XN.rearrange("p b c -> p (b c)")
            dve.tensor_tensor(xnf, xnf, bank(0, 2), ALU.add).then_inc(*mdve.did("h"))
            dve.wait_ge(*mdve.at("h"))
            stats_all(mdve, XN, 128, "hstats", "hmv", "hvar")
            dve.wait_ge(*mpool.at("hrstd"))
            norm_all(mdve, XN, XN, 128, "hn")
            dve.wait_ge(*mdve.at("hn"))
            dve.tensor_tensor(XN, XN, row_b("ln_w"), ALU.mult).then_inc(*mdve.did("hg"))
            dve.wait_ge(*mdve.at("hg"))
            dve.tensor_tensor(XN, XN, row_b("ln_b"), ALU.add).then_inc(*mdve.did("hb"))
            dve.wait_ge(*mdve.at("hb"))
            dve.tensor_tensor(X[:, :, :], X[:, :, :], XN, ALU.add).then_inc(*mdve.did("x"))
            dve.wait_ge(*mdve.at("x"))

            def ln_stats(S, i, src, names_, st="st", mv="mv", var="var"):
                for s in range(2):
                    dve.bn_stats(slot[s][st], src(s)).then_inc(*S.did(names_[0], 2 * i + s))
                for s in range(2):
                    dve.wait_ge(*S.at(names_[0], 2 * i + s))
                    dve.bn_aggr(slot[s][mv], slot[s][st]).then_inc(*S.did(names_[1], 2 * i + s))
                for s in range(2):
                    dve.wait_ge(*S.at(names_[1], 2 * i + s))
                    dve.tensor_scalar(slot[s][var], slot[s][mv][:, 1:2], EPS, None, ALU.add)\
                       .then_inc(*S.did(names_[2], 2 * i + s))

            def heads_softmax(S, P, i, keys, scale=None):
                for s in range(2):
                    b = 2 * i + s
                    sc = PS[:, 4 * s:4 * s + 4, 0:4 * keys].rearrange("p g (h m) -> p g h m", h=4)
                    dve.wait_ge(*P.at("sc" if keys == M else "s", b))
                    dve.tensor_reduce(slot[s]["mx"].rearrange("p (g h) -> p g h", g=4), sc, AX, ALU.max)\
                       .then_inc(*S.did("mx", b))
                for s in range(2):
                    b = 2 * i + s
                    dve.wait_ge(*S.at("mx", b))
                    for g in range(4):
                        sc = PS[:, 4 * s + g, 0:4 * keys].rearrange("p (h m) -> p h m", h=4)
                        ins = dve.tensor_tensor(
                            slot[s]["p"][:, 4 * g * keys:4 * (g + 1) * keys].rearrange("p (h m) -> p h m", h=4), sc,
                            slot[s]["mx"][:, 4 * g:4 * g + 4].unsqueeze(2).to_broadcast([128, 4, keys]), ALU.subtract)
                    ins.then_inc(*S.did("sub", b))

            def heads_out(S, P, i, keys):
                for s in range(2):
                    b = 2 * i + s
                    dve.wait_ge(*P.at("pt1", b))
                    dve.tensor_copy(slot[s]["pt"][0:keys, 1024:2048], bank(4 * s + 2, 2)[0:keys, :])\
                       .then_inc(*S.did("pt1", b))
                for s in range(2):
                    b = 2 * i + s
                    o = bank(4 * s)[:, 0:H0 * (HD0 + 1)].rearrange("p (h d) -> p h d", h=H0)
                    dve.wait_ge(*P.at("pv", b))
                    dve.reciprocal(slot[s]["rz"].unsqueeze(2), o[:, :, HD0:HD0 + 1]).then_inc(*S.did("rz", b))
                for s in range(2):
                    b = 2 * i + s
                    o = bank(4 * s)[:, 0:H0 * (HD0 + 1)].rearrange("p (h d) -> p h d", h=H0)
                    dve.wait_ge(*S.at("rz", b))
                    dve.tensor_tensor(slot[s]["o"][:, 0:D].rearrange("p (h d) -> p h d", h=H0), o[:, :, 0:HD0],
                                      slot[s]["rz"].unsqueeze(2).to_broadcast([128, H0, HD0]), ALU.mult)\
                       .then_inc(*S.did("o", b))

            S, P = x0["dve"], x0["pe"]
            for i in range(B // 2):
                ln_stats(S, i, lambda s: X[:, 2 * i + s, :], ("stats", "mv", "var"))
                for s in range(2):
                    b = 2 * i + s
                    dve.wait_ge(*x0["pool"].at("rstd", b))
                    dve.tensor_scalar(slot[s]["xn"], X[:, b, :], slot[s]["mv"][:, 0:1], slot[s]["rs"],
                                      ALU.subtract, ALU.mult).then_inc(*S.did("xn", b))
                for s in range(2):
                    b, v = 2 * i + s, slot[s]
                    q_ps = PS[:, 4 * s + 3, 384:512].rearrange("p (h g d) -> p h g d", h=H0, g=2)
                    r1 = v["r1"].rearrange("p (h g d) -> p h g d", h=H0, g=2)
                    r2 = v["r2"].rearrange("p (h g d) -> p h g d", h=H0, g=2)
                    dve.wait_ge(*P.at("q", b))
                    for g in range(2):
                        cos = ROPE[:, 0, b, g, :].unsqueeze(1).to_broadcast([T, H0, 4])
                        sin = ROPE[:, 1, b, g, :].unsqueeze(1).to_broadcast([T, H0, 4])
                        dve.tensor_tensor(r1[:, :, g, :], q_ps[:, :, g, :], cos, ALU.mult)
                        ins = dve.tensor_tensor(r2[:, :, g, :], q_ps[:, :, 1 - g, :], sin, ALU.mult)
                    ins.then_inc(*S.did("rope_a", b))
                for s in range(2):
                    b, v = 2 * i + s, slot[s]
                    dve.wait_ge(*S.at("rope_a", b))
                    dve.tensor_tensor(v["qr"], v["r1"], v["r2"], ALU.add).then_inc(*S.did("rope", b))
                heads_softmax(S, P, i, M)
                heads_out(S, P, i, M)
                for s in range(2):
                    b = 2 * i + s
                    dve.wait_ge(*P.at("wo", b))
                    dve.tensor_tensor(X[:, b, :], X[:, b, :], PS[:, 4 * s + 2, 0:D], ALU.add)\
                       .then_inc(*S.did("res", b))
            dve.wait_ge(*S.at("res", B - 1))

            S, P = f0["dve"], f0["pe"]
            stats_all(S, X, 128, "stats", "mv", "var")
            dve.wait_ge(*f0["pool"].at("rstd"))
            norm_all(S, XA, X, 128, "xn")
            lg, top = SMALL[:, 0, :, :], SMALL[:, 1, :, :]
            dve.wait_ge(*P.at("gate"))
            dve.tensor_copy(lg, bank(4)[:, 0:B * E0].rearrange("p (b e) -> p b e", b=B)).then_inc(*S.did("lg"))
            dve.wait_ge(*S.at("lg"))
            for b in range(B):
                ins = dve.max(top[:, b, :], lg[:, b, :])
            ins.then_inc(*S.did("max"))
            dve.wait_ge(*S.at("max"))
            for b in range(B):
                ins = dve.max_index(TOPI[:, b, :], top[:, b, :], lg[:, b, :])
            ins.then_inc(*S.did("index"))
            dve.wait_ge(*S.at("index"))
            ti = SMALL[:, 2, :, :]
            dve.tensor_copy(ti, TOPI[:, :, :]).then_inc(*S.did("top_i"))
            w = SMALL[:, 3, :, :]
            dve.tensor_tensor(w[:, :, 0:1], top[:, :, 1:2], top[:, :, 0:1], ALU.subtract).then_inc(*S.did("dif"))
            dve.wait_ge(*f0["act"].at("top_exp"))
            dve.tensor_scalar(w[:, :, 2:3], w[:, :, 1:2], 1.0, None, ALU.add).then_inc(*S.did("den"))
            dve.wait_ge(*S.at("den"))
            dve.reciprocal(w[:, :, 3:4], w[:, :, 2:3]).then_inc(*S.did("w1"))
            dve.wait_ge(*S.at("w1"))
            dve.tensor_tensor(w[:, :, 4:5], w[:, :, 1:2], w[:, :, 3:4], ALU.mult).then_inc(*S.did("w2"))
            iota = IOTA.unsqueeze(1).to_broadcast([T, B, E0])
            for j, (step, stepw) in enumerate((("s1", "s1w"), ("s2", "s2w"))):
                dve.tensor_tensor(SMALL[:, 4 + j, :, :], iota, ti[:, :, j:j + 1].to_broadcast([T, B, E0]),
                                  ALU.is_equal).then_inc(*S.did(step))
            for j, (step, stepw) in enumerate((("s1", "s1w"), ("s2", "s2w"))):
                dve.wait_ge(*S.at("s2"))
                dve.tensor_tensor(SMALL[:, 4 + j, :, :], SMALL[:, 4 + j, :, :],
                                  w[:, :, 3 + j:4 + j].to_broadcast([T, B, E0]), ALU.mult).then_inc(*S.did(stepw))
            dve.wait_ge(*S.at("s2w"))
            dve.tensor_tensor(PROB, SMALL[:, 4, :, :], SMALL[:, 5, :, :], ALU.add).then_inc(*S.did("comb"))

            def moe_units(F, n, gated, last_step):
                S, P = F["dve"], F["pe"]

                def acc(h, e):
                    dve.wait_ge(*P.at("y", h, e))
                    if (h, e) != (0, 0):
                        dve.wait_ge(*S.at("acc", *divmod(h * E0 + e - 1, E0)))
                    for j in range(4):
                        b = 4 * h + j
                        ins = dve.scalar_tensor_tensor(last_step[:, b, :], PS[:, 6 + e % 2, j * D:(j + 1) * D],
                                                       PROB[:, b, e:e + 1], last_step[:, b, :], ALU.mult, ALU.add)
                    ins.then_inc(*S.did("acc", h, e))

                prev = None
                for k_, (h, e, c) in enumerate(units(n)):
                    if gated:
                        if k_ >= 3:
                            ub = units(n)[k_ - 3]
                            dve.wait_ge(*P.at("y" if ub[2] == n - 1 else "yp", *(ub[:2] if ub[2] == n - 1 else ub)))
                        dve.wait_ge(*F["act"].at("silu", h, e, c))
                        dve.tensor_tensor(ACTB[:, k_ % 3, :], ACTS[:, k_ % 3, :], bank(2 * (k_ % 3) + 1), ALU.mult)\
                           .then_inc(*S.did("act", h, e, c))
                    if c == n - 1:
                        if prev is not None:
                            acc(*prev)
                        prev = (h, e)
                acc(*prev)

            dve.wait_ge(*S.at("comb"))
            moe_units(f0, 2, True, X)
            dve.wait_ge(*S.at("acc", 1, E0 - 1))

            S, P, A = a1["dve"], a1["pe"], a1["act"]
            for i in range(B // 2):
                ln_stats(S, i, lambda s: X[:, 2 * i + s, :], ("stats", "mv", "var"))
                for s in range(2):
                    b = 2 * i + s
                    dve.wait_ge(*a1["pool"].at("rstd", b))
                    dve.tensor_scalar(slot[s]["xn"], X[:, b, :], slot[s]["mv"][:, 0:1], slot[s]["rs"],
                                      ALU.subtract, ALU.mult).then_inc(*S.did("xn", b))
                for s in range(2):
                    b, v = 2 * i + s, slot[s]
                    dve.wait_ge(*P.at("v", b))
                    dve.tensor_copy(v["y"], PS[:, 4 * s + 3, 0:D]).then_inc(*S.did("v", b))
                bound = {p: float(np.log(p / (1 - p))) for p in (0.95, 0.85, 0.1, 0.25)}
                for s in range(2):
                    b, v = 2 * i + s, slot[s]
                    dve.wait_ge(*P.at("s", b))
                    dve.tensor_scalar(v["q"], PS[:, 4 * s, 0:T], float(HD0 ** -0.5), None, ALU.mult)\
                       .then_inc(*S.did("a", b))
                for s in range(2):
                    b, v = 2 * i + s, slot[s]
                    dve.wait_ge(*S.at("a", b))
                    dve.tensor_scalar(v["r1"], v["q"], bound[0.95], None, ALU.is_gt).then_inc(*S.did("g1", b))
                for s in range(2):
                    b, v = 2 * i + s, slot[s]
                    dve.tensor_scalar(v["r2"], v["q"], bound[0.1], 2.0 / 7.0, ALU.is_lt, ALU.mult)\
                       .then_inc(*S.did("l1", b))
                for s in range(2):
                    b, v = 2 * i + s, slot[s]
                    dve.wait_ge(*S.at("g1", b))
                    dve.scalar_tensor_tensor(v["r1"], v["q"], bound[0.85], v["r1"], ALU.is_gt, ALU.add)\
                       .then_inc(*S.did("g", b))
                for s in range(2):
                    b, v = 2 * i + s, slot[s]
                    dve.wait_ge(*S.at("l1", b))
                    dve.scalar_tensor_tensor(v["r2"], v["q"], bound[0.25], v["r2"], ALU.is_lt, ALU.add)\
                       .then_inc(*S.did("l", b))
                for s in range(2):
                    b, v = 2 * i + s, slot[s]
                    dve.wait_ge(*S.at("l", b))
                    dve.tensor_scalar(v["r2"], v["r2"], -0.7, 1.0, ALU.mult, ALU.add).then_inc(*S.did("ls", b))
                for s in range(2):
                    b, v = 2 * i + s, slot[s]
                    dve.wait_ge(*S.at("ls", b))
                    dve.scalar_tensor_tensor(v["r1"], v["r1"], 0.5, v["r2"], ALU.mult, ALU.add).then_inc(*S.did("m", b))
                for s in range(2):
                    b, v = 2 * i + s, slot[s]
                    dve.wait_ge(*S.at("m", b))
                    dve.tensor_tensor(v["q"], v["q"], v["r1"], ALU.mult).then_inc(*S.did("am", b))
                for s in range(2):
                    b, v = 2 * i + s, slot[s]
                    dve.wait_ge(*S.at("am", b))
                    dve.tensor_reduce(v["mx1"], v["q"], AX, ALU.max).then_inc(*S.did("mx", b))
                for s in range(2):
                    b, v = 2 * i + s, slot[s]
                    dve.wait_ge(*S.at("mx", b))
                    dve.tensor_scalar(v["mx1"], v["mx1"], -1.0, None, ALU.mult).then_inc(*S.did("nmx", b))
                for s in range(2):
                    b, v = 2 * i + s, slot[s]
                    dve.wait_ge(*A.at("p", b))
                    dve.reciprocal(v["rz"][:, 1:2], v["rz"][:, 0:1]).then_inc(*S.did("rz", b))
                for s in range(2):
                    b, v = 2 * i + s, slot[s]
                    dve.wait_ge(*P.at("out", b))
                    dve.wait_ge(*S.at("rz", b))
                    dve.scalar_tensor_tensor(v["l1"], PS[:, 4 * s + 1, D:2 * D], v["rz"][:, 1:2], X[:, b, :],
                                             ALU.mult, ALU.add).then_inc(*S.did("y", b))
                for s in range(2):
                    b, v = 2 * i + s, slot[s]
                    dve.wait_ge(*S.at("y", b))
                    dve.tensor_tensor(X[:, b, :], v["l1"], row("a1_bproj"), ALU.add).then_inc(*S.did("res", b))
            dve.wait_ge(*S.at("res", B - 1))

            S, P, A = x1["dve"], x1["pe"], x1["act"]
            for s in range(2):
                dve.memset(slot[s]["va"][:, :, HD1:HD1 + 1], 1.0)
                ins = dve.memset(slot[s]["vb"][:, :, HD1:HD1 + 1], 1.0)
            ins.then_inc(*S.did("ones", 0))
            for i in range(B // 2):
                ln_stats(S, i, lambda s: X[:, 2 * i + s, :], ("stats", "mv", "var"))
                for s in range(2):
                    b = 2 * i + s
                    dve.wait_ge(*x1["pool"].at("rstd", b))
                    dve.tensor_scalar(slot[s]["xn"], X[:, b, :], slot[s]["mv"][:, 0:1], slot[s]["rs"],
                                      ALU.subtract, ALU.mult).then_inc(*S.did("xn", b))
                for s in range(2):
                    dve.wait_ge(*S.at("xn", 2 * i + s))
                ln_stats(S, i, lambda s: slot[s]["xn"], ("stats2", "mv2", "var2"), "st2", "mv2", "var2")
                for s in range(2):
                    b, v = 2 * i + s, slot[s]
                    dve.wait_ge(*x1["pool"].at("rstd2", b))
                    dve.tensor_scalar(v["l1"], v["xn"], v["mv2"][:, 0:1], v["rs2"], ALU.subtract, ALU.mult)\
                       .then_inc(*S.did("l0", b))
                for s in range(2):
                    b, v = 2 * i + s, slot[s]
                    dve.wait_ge(*S.at("l0", b))
                    dve.tensor_tensor(v["l1"], v["l1"], row("gl"), ALU.mult).then_inc(*S.did("l1", b))
                for s in range(2):
                    b, v = 2 * i + s, slot[s]
                    dve.wait_ge(*S.at("l1", b))
                    dve.tensor_tensor(v["l2"], v["l1"], row("bl"), ALU.add).then_inc(*S.did("l2", b))
                for s in range(2):
                    b, v = 2 * i + s, slot[s]
                    dve.wait_ge(*P.at("v", b))
                    dve.tensor_copy(v["va"][0:M, :, 0:HD1], bank(4 * s + 2)[0:M, :].rearrange("p (h d) -> p h d", h=H1))
                    dve.tensor_copy(v["vb"][:, :, 0:HD1], bank(4 * s + 3).rearrange("p (h d) -> p h d", h=H1))\
                       .then_inc(*S.did("v", b))
                for s in range(2):
                    b, v = 2 * i + s, slot[s]
                    dve.wait_ge(*P.at("s", b))
                    sc = PS[:, 4 * s:4 * s + 4, 0:2 * J1].rearrange("p g (h m) -> p g h m", h=2)
                    dve.tensor_reduce(v["mx"][:, 0:H1].rearrange("p (g h) -> p g h", g=4), sc, AX, ALU.max)\
                       .then_inc(*S.did("mx", b))
                for s in range(2):
                    b, v = 2 * i + s, slot[s]
                    dve.wait_ge(*S.at("mx", b))
                    for g in range(4):
                        ins = dve.tensor_tensor(
                            v["p1"][:, 2 * g * J1:2 * (g + 1) * J1].rearrange("p (h m) -> p h m", h=2),
                            PS[:, 4 * s + g, 0:2 * J1].rearrange("p (h m) -> p h m", h=2),
                            v["mx"][:, 2 * g:2 * g + 2].unsqueeze(2).to_broadcast([128, 2, J1]), ALU.subtract)
                    ins.then_inc(*S.did("sub", b))
                for s in range(2):
                    b, v = 2 * i + s, slot[s]
                    dve.wait_ge(*P.at("pt", b))
                    dve.tensor_copy(v["ptb"].rearrange("p h t -> p (h t)"), bank(4 * s + 2, 2)).then_inc(*S.did("ptb", b))
                for s in range(2):
                    b, v = 2 * i + s, slot[s]
                    o = PS[:, 4 * s:4 * s + 2, 0:4 * (HD1 + 1)].rearrange("p g (h d) -> p g h d", h=4)
                    dve.wait_ge(*P.at("o", b))
                    for g in range(2):
                        ins = dve.reciprocal(v["rz"][:, 4 * g:4 * g + 4].unsqueeze(2), o[:, g, :, HD1:HD1 + 1])
                    ins.then_inc(*S.did("rz", b))
                for s in range(2):
                    b, v = 2 * i + s, slot[s]
                    o = PS[:, 4 * s:4 * s + 2, 0:4 * (HD1 + 1)].rearrange("p g (h d) -> p g h d", h=4)
                    dve.wait_ge(*S.at("rz", b))
                    for g in range(2):
                        ins = dve.tensor_tensor(
                            v["o"][:, 256 * g:256 * g + 256].rearrange("p (h d) -> p h d", h=4), o[:, g, :, 0:HD1],
                            v["rz"][:, 4 * g:4 * g + 4].unsqueeze(2).to_broadcast([128, 4, HD1]), ALU.mult)
                    ins.then_inc(*S.did("o", b))
                for s in range(2):
                    b = 2 * i + s
                    dve.wait_ge(*P.at("out", b))
                    dve.tensor_tensor(X[:, b, :], X[:, b, :], PS[:, 4 * s + 3, 0:D], ALU.add)\
                       .then_inc(*S.did("res", b))
            dve.wait_ge(*S.at("res", B - 1))

            S, P, A = g1["dve"], g1["pe"], g1["act"]
            for s in range(2):
                dve.memset(slot[s]["xp"][:, 0:1], 0.0)
                dve.memset(slot[s]["xp"][:, T + 1:T + 2], 0.0)
                ins = dve.memset(slot[s]["v1"][:, :, HD0:HD0 + 1], 1.0)
            ins.then_inc(*S.did("ones", 0))
            for i in range(B // 2):
                ln_stats(S, i, lambda s: X[:, 2 * i + s, :], ("stats", "mv", "var"))
                for s in range(2):
                    b = 2 * i + s
                    dve.wait_ge(*g1["pool"].at("rstd", b))
                    dve.tensor_scalar(slot[s]["xn"], X[:, b, :], slot[s]["mv"][:, 0:1], slot[s]["rs"],
                                      ALU.subtract, ALU.mult).then_inc(*S.did("xn", b))
                for s in range(2):
                    b, v = 2 * i + s, slot[s]
                    dve.wait_ge(*P.at("y", b))
                    dve.tensor_copy(v["y"], PS[:, 4 * s, 0:D]).then_inc(*S.did("y", b))
                for s in range(2):
                    b, v = 2 * i + s, slot[s]
                    dve.wait_ge(*P.at("v", b))
                    dve.tensor_copy(v["v1"][:, :, 0:HD0], PS[:, 4 * s + 2, D:2 * D].rearrange("p (h d) -> p h d", h=H0))\
                       .then_inc(*S.did("v", b))
                heads_softmax(S, P, i, T)
                heads_out(S, P, i, T)
                for s in range(2):
                    b, v = 2 * i + s, slot[s]
                    dve.wait_ge(*P.at("wo", b))
                    dve.tensor_tensor(v["y"], v["y"], PS[:, 4 * s + 2, 0:D], ALU.add).then_inc(*S.did("h", b))
                for s in range(2):
                    dve.wait_ge(*S.at("h", 2 * i + s))
                ln_stats(S, i, lambda s: slot[s]["y"], ("stats2", "mv2", "var2"), "st2", "mv2", "var2")
                for s in range(2):
                    b, v = 2 * i + s, slot[s]
                    dve.wait_ge(*g1["pool"].at("rstd2", b))
                    dve.tensor_scalar(v["l1"], v["y"], v["mv2"][:, 0:1], v["rs2"], ALU.subtract, ALU.mult)\
                       .then_inc(*S.did("l0", b))
                for s in range(2):
                    b, v = 2 * i + s, slot[s]
                    dve.wait_ge(*S.at("l0", b))
                    dve.tensor_tensor(v["l1"], v["l1"], row("ln1_g"), ALU.mult).then_inc(*S.did("l1", b))
                for s in range(2):
                    b, v = 2 * i + s, slot[s]
                    dve.wait_ge(*S.at("l1", b))
                    dve.tensor_tensor(XN1[:, b, :], v["l1"], row("ln1_b"), ALU.add).then_inc(*S.did("xa", b))
                for s in range(2):
                    b = 2 * i + s
                    dve.wait_ge(*P.at("gate", b))
                    dve.tensor_copy(SMALL[:, 0, b, :], PS[:, 4 * s + 3, 0:E1]).then_inc(*S.did("lg", b))
            dve.wait_ge(*S.at("lg", B - 1))

            F = f1
            S, P = F["dve"], F["pe"]
            lg = SMALL[:, 0, :, :]
            dve.tensor_reduce(SMALL[:, 1, :, 0], lg, AX, ALU.max).then_inc(*S.did("gmx"))
            dve.wait_ge(*S.at("gmx"))
            dve.tensor_tensor(lg, lg, SMALL[:, 1, :, 0:1].to_broadcast([T, B, E1]), ALU.subtract).then_inc(*S.did("gsub"))
            dve.wait_ge(*F["act"].at("gexp"))
            dve.tensor_reduce(SMALL[:, 1, :, 1], lg, AX, ALU.add).then_inc(*S.did("gsum"))
            dve.wait_ge(*S.at("gsum"))
            dve.reciprocal(SMALL[:, 1, :, 2], SMALL[:, 1, :, 1]).then_inc(*S.did("grz"))
            dve.wait_ge(*S.at("grz"))
            dve.tensor_tensor(PROB, lg, SMALL[:, 1, :, 2:3].to_broadcast([T, B, E1]), ALU.mult).then_inc(*S.did("prob"))
            dve.wait_ge(*P.at("b2"))
            dve.tensor_tensor(XA.rearrange("p b c -> p (b c)"), XN1.rearrange("p b c -> p (b c)"), bank(4, 2), ALU.add)\
               .then_inc(*S.did("b2"))
            dve.wait_ge(*S.at("b2"))
            moe_units(f1, 4, False, XA)
            dve.wait_ge(*S.at("acc", 1, E0 - 1))
            stats_all(S, XA, 128, "stats", "mv", "var")
            dve.wait_ge(*F["pool"].at("rstd"))
            norm_all(S, XA, XA, 128, "xn")
            dve.wait_ge(*S.at("xn"))
            dve.tensor_tensor(XA, XA, row_b("ln2_g"), ALU.mult).then_inc(*S.did("g"))
            dve.wait_ge(*S.at("g"))
            dve.tensor_tensor(XA, XA, row_b("ln2_b"), ALU.add).then_inc(*S.did("b"))
            dve.wait_ge(*S.at("b"))
            dve.tensor_tensor(FIN, XA, X[:, :, :], ALU.add).then_inc(*S.did("fin"))

        @block.gpsimd
        def _(pool):
            def rsqrt_all(S, wait, p, step):
                pool.wait_ge(*wait)
                pool.tensor_tensor(RS[0:p, :], RS[0:p, :], HALFNEG[0:p, :], ALU.pow).then_inc(*S.did(step))

            rsqrt_all(mpool, mdve.at("var"), 128, "rstd")
            rsqrt_all(mpool, mdve.at("cvar"), M, "crstd")
            for k in ("bu1", "hc1"):
                pool.nop().then_inc(L[k], CREDIT)
            for d in range(2):
                base = d * DS + CREDIT

                def inputs_b(s, n):
                    pool.wait_ge(L["b_sb"], n + 1)
                    pool.wait_ge(L["yacc"], n - 3)
                    pool.tensor_tensor(HB[s % 4][:, 1, :], U[d][:, 1, :], BS[:, s % 2, :], ALU.mult).then_inc(L["bu1"], 1)

                def states_c(s, n):
                    pool.wait_ge(L["c_sb"], n + 1)
                    pool.wait_ge(L["h1"], n + 1)
                    pool.tensor_tensor(HB[s][:, 1, :], HB[s][:, 1, :], CS[:, s % 2, :], ALU.mult).then_inc(L["hc1"], 1)

                pool.wait_ge(*mdve.at("du", d))
                inputs_b(0, base)
                with pool.Fori(0, DS // 4 - 1) as it:
                    for s in range(4):
                        inputs_b(s + 1, it * 4 + (s + 1 + base))
                        states_c(s, it * 4 + (s + base))
                for s in range(4):
                    if s < 3:
                        inputs_b(s + 1, base + DS - 4 + s + 1)
                    states_c(s, base + DS - 4 + s)
            rsqrt_all(mpool, mdve.at("hvar"), 128, "hrstd")

            def rstd(S, D_, i, var="var", rs="rs", wait="var", step="rstd"):
                for s in range(2):
                    b = 2 * i + s
                    pool.wait_ge(*D_.at(wait, b))
                    pool.tensor_tensor(slot[s][rs], slot[s][var], HALFNEG[:, 0:1], ALU.pow).then_inc(*S.did(step, b))

            def spread_keys(S, P, i, keys, src, waits):
                for s in range(2):
                    b = 2 * i + s
                    for w_ in waits(b):
                        pool.wait_ge(*w_)
                    kx = slot[s]["kx"][:, 0:H0 * keys].rearrange("p (h m) -> p h m", h=H0)
                    pool.tensor_tensor(kx, src(s, b).unsqueeze(1).to_broadcast([128, H0, keys]),
                                       MASK.unsqueeze(2).to_broadcast([128, H0, keys]), ALU.mult)\
                        .then_inc(*S.did("kx", b))

            for i in range(B // 2):
                rstd(x0["pool"], x0["dve"], i)
                spread_keys(x0["pool"], x0["pe"], i, M, lambda s, b: KT0[:, b, :], lambda b: [x0["pe"].at("q", b)])
            rsqrt_all(f0["pool"], f0["dve"].at("var"), 128, "rstd")
            for i in range(B // 2):
                rstd(a1["pool"], a1["dve"], i)
            for i in range(B // 2):
                rstd(x1["pool"], x1["dve"], i)
                rstd(x1["pool"], x1["dve"], i, "var2", "rs2", "var2", "rstd2")
            for i in range(B // 2):
                rstd(g1["pool"], g1["dve"], i)
                spread_keys(g1["pool"], g1["pe"], i, T, lambda s, b: slot[s]["kt"], lambda b: [g1["act"].at("k", b)])
                rstd(g1["pool"], g1["dve"], i, "var2", "rs2", "var2", "rstd2")
            rsqrt_all(f1["pool"], f1["dve"].at("var"), 128, "rstd")

        @block.scalar
        def _(act):
            act.wait_ge(ld_c, 48)
            act.activation(NEGA[:, :, :, :].rearrange("p a b c -> p (a b c)"), ALOG, ACT.Exp)\
               .then_inc(*mact.did("nega"))
            act.wait_ge(*mpe.at("kt0"))
            for g in range(2):
                i = act.activation(KT0[:, 4 * g:4 * g + 4, :].rearrange("p b m -> p (b m)"), bank(g)[:, 0:4 * M],
                                   ACT.Identity, bias=X0BK)
            i.then_inc(*mact.did("kt0"))
            act.wait_ge(*mdve.at("rope7"))
            act.activation(SMALL[:, 3, :, 0:4], SMALL[:, 1, :, 0:4], ACT.Abs).then_inc(*mact.did("sin_abs"))
            act.activation(SMALL[:, 6, :, 0:4], SMALL[:, 1, :, 0:4], ACT.Sin)
            act.wait_ge(*mdve.at("rope8"))
            act.activation(SMALL[:, 5, :, 0:4], SMALL[:, 3, :, 0:4], ACT.Sin).then_inc(*mact.did("sin"))
            act.wait_ge(*mpe.at("ct"))
            act.activation(KVT[:, :, 0:M], bank(4, 2).rearrange("p (b t) -> p b t", b=B)[:, :, 0:M], ACT.Copy)\
               .then_inc(*mact.did("ct"))
            act.wait_ge(*mpe.at("xnt"))
            act.activation(XNT[:, :, :].rearrange("p b t -> p (b t)"), bank(6, 2), ACT.Copy).then_inc(*mact.did("xnt"))
            for k in ("b_sb", "c_sb", "da0", "da1"):
                act.nop().then_inc(L[k], CREDIT)
            for d in range(2):
                off = DC - 1 if d == 0 else 0
                for c in range(NC):
                    act.wait_ge(*mpe.at(f"xz{c}", d))
                    i = act.activation(XP[d][:, c, :, off:off + T], bank(2 * c, 2).rearrange("p (b t) -> p b t", b=B),
                                       ACT.Copy)
                i.then_inc(*mact.did("xp", d))
                for c in range(NC):
                    act.wait_ge(*mpe.at(f"xz{2 + c}", d))
                    i = act.activation(ZS[:, d, c, :], bank(4 + 2 * c, 2), ACT.Silu)
                i.then_inc(*mact.did("zs", d))
            for d in range(2):
                act.wait_ge(*mdve.at("conv", d))
                for c in range(NC):
                    i = act.activation(U[d][:, c, :], U[d][:, c, :], ACT.Silu)
                i.then_inc(*mact.did("u", d))
            for d in range(2):
                act.wait_ge(*mpe.at("dbc", d))
                if d:
                    act.wait_ge(*mdve.at("delta", 0))
                act.activation(DTS[0:DR, :], bank(0, 2)[0:DR, :], ACT.Copy).then_inc(*mact.did("dts", d))
                for c in range(NC):
                    act.wait_ge(*mpe.at(f"dt{c}", d))
                    act.activation(SPR[:, c, :], bank(4 + 2 * c, 2), ACT.Relu, bias=DTB[d][:, c:c + 1])\
                       .then_inc(*mact.did(f"relu{c}", d))
                    act.activation(SPE[:, c, :], bank(4 + 2 * c, 2), ACT.Abs, bias=DTB[d][:, c:c + 1])\
                       .then_inc(*mact.did(f"abs{c}", d))
                act.wait_ge(*mact.at("abs1", d))
                for c in range(NC):
                    i = act.activation(SPE[:, c, :], SPE[:, c, :], ACT.Exp, scale=-1.0)
                i.then_inc(*mact.did("exp", d))
                act.wait_ge(*mact.at("exp", d))
                act.wait_ge(*mdve.at("s3", d))
                for c in range(NC):
                    i = act.activation(SPL[:, c, :], SPE[:, c, :], ACT.Ln, bias=ONES[:, 0:1])
                i.then_inc(*mact.did("ln", d))
            for d in range(2):
                act.wait_ge(*mdve.at("edge", d))
                cols_ = slice(1, T) if d == 0 else slice(0, T - 1)
                with act.Fori(0, DS // 4) as it:
                    for s in range(4):
                        n = it * 4 + (s + d * DS + CREDIT)
                        act.wait_ge(L["b_ps"], it * 4 + (s + d * DS + 1))
                        act.wait_ge(L["bu0"], n - 1)
                        act.wait_ge(L["bu1"], n - 1)
                        act.activation(BS[:, s % 2, :], bank(0, 2), ACT.Copy).then_inc(L["b_sb"], 1)
                        for c in (1, 0):
                            act.wait_ge(L[f"h{c}"], n - 1)
                            act.activation(DA[:, s % 2, c, :].rearrange("p (b t) -> p b t", b=B)[:, :, cols_],
                                           DELTA[d][:, c, :].rearrange("p (b t) -> p b t", b=B)[:, :, cols_], ACT.Exp,
                                           scale=NEGA[:, d, c, bass.ds(it * 4 + s, 1)]).then_inc(L[f"da{c}"], 1)
                        act.wait_ge(L["c_ps"], it * 4 + (s + d * DS + 1))
                        act.wait_ge(L["hc0"], n - 1)
                        act.wait_ge(L["hc1"], n - 1)
                        act.activation(CS[:, s % 2, :], bank(2, 2), ACT.Copy).then_inc(L["c_sb"], 1)

            def copy(S, P, step, pstep, dst, src, i, func=ACT.Copy, bias=None, scale=1.0):
                for s in range(2):
                    b = 2 * i + s
                    act.wait_ge(*P.at(pstep, b))
                    if bias is None:
                        act.activation(dst(s, b), src(s), func, scale=scale).then_inc(*S.did(step, b))
                    else:
                        act.activation(dst(s, b), src(s), func, bias=bias, scale=scale).then_inc(*S.did(step, b))

            S, P = x0["act"], x0["pe"]
            act.wait_ge(*mdve.at("x"))
            for i in range(B // 2):
                copy(S, P, "xt", "xt", lambda s, b: slot[s]["xt"], lambda s: PS[:, 4 * s + 3, 384:512], i)
                copy(S, P, "qt", "qt", lambda s, b: slot[s]["qt"], lambda s: PS[:, 4 * s + 3, 384:512], i)
                copy(S, x0["dve"], "p", "sub", lambda s, b: slot[s]["p"][:, 0:H0 * M],
                     lambda s: slot[s]["p"][:, 0:H0 * M], i, ACT.Exp, scale=float(1 / np.sqrt(HD0)))
                copy(S, P, "pt0", "pt0", lambda s, b: slot[s]["pt"][0:M, 0:1024], lambda s: bank(4 * s, 2)[0:M, :], i)
                copy(S, P, "ot", "ot", lambda s, b: slot[s]["ot"][:, 0, :], lambda s: PS[:, 4 * s + 1, 0:T], i)
            S, P = f0["act"], f0["pe"]
            act.wait_ge(*P.at("xnt"))
            act.activation(XNT[:, :, :].rearrange("p b t -> p (b t)"), bank(0, 2), ACT.Copy).then_inc(*S.did("xnt"))
            act.wait_ge(*f0["dve"].at("dif"))
            act.activation(SMALL[:, 3, :, 1:2], SMALL[:, 3, :, 0:1], ACT.Exp).then_inc(*S.did("top_exp"))
            for k, u in enumerate(units(2)):
                act.wait_ge(*P.at("hg", *u))
                if k >= 3:
                    act.wait_ge(*f0["dve"].at("act", *units(2)[k - 3]))
                act.activation(ACTS[:, k % 3, :], bank(2 * (k % 3)), ACT.Silu).then_inc(*S.did("silu", *u))
            S, P = a1["act"], a1["pe"]
            for i in range(B // 2):
                copy(S, P, "xt", "xt", lambda s, b: slot[s]["xt"], lambda s: PS[:, 4 * s, 0:T], i)
                copy(S, P, "q", "q", lambda s, b: slot[s]["qt"], lambda s: PS[:, 4 * s + 1, 0:T], i, ACT.Identity, A1B[:, 0:1])
                copy(S, P, "k", "k", lambda s, b: slot[s]["kt"], lambda s: PS[:, 4 * s + 2, 0:T], i, ACT.Identity, A1B[:, 1:2])
                for s in range(2):
                    b, v = 2 * i + s, slot[s]
                    act.wait_ge(*a1["dve"].at("nmx", b))
                    act.activation(v["p"][:, 0:T], v["q"], ACT.Exp, bias=v["mx1"], accum_out=v["rz"][:, 0:1])\
                       .then_inc(*S.did("p", b))
                copy(S, P, "pt", "pt", lambda s, b: slot[s]["pt"][:, 0:T], lambda s: PS[:, 4 * s + 1, 0:T], i)
                copy(S, P, "o", "o", lambda s, b: slot[s]["ot"][:, 0, :], lambda s: PS[:, 4 * s + 2, 0:T], i)
            S, P = x1["act"], x1["pe"]
            for i in range(B // 2):
                copy(S, P, "lt", "lt", lambda s, b: KVT[:, b, M:J1], lambda s: PS[:, 4 * s, 0:T], i)
                copy(S, P, "q", "q", lambda s, b: slot[s]["qt1"].rearrange("p c t -> p (c t)"), lambda s: bank(4 * s + 1), i)
                for s in range(2):
                    b = 2 * i + s
                    act.wait_ge(*P.at("k", b))
                    for g, bk in enumerate((4 * s, 4 * s + 1)):
                        ins = act.activation(slot[s]["kt1"][:, 2 * g:2 * g + 2, :].rearrange("p c j -> p (c j)"),
                                             bank(bk)[:, 0:2 * J1], ACT.Copy)
                    ins.then_inc(*S.did("k", b))
                copy(S, x1["dve"], "p", "sub", lambda s, b: slot[s]["p1"], lambda s: slot[s]["p1"], i, ACT.Exp,
                     scale=float(HD1 ** 0.5))
                copy(S, P, "pta", "pt", lambda s, b: slot[s]["pta"].rearrange("p h t -> p (h t)")[0:M, :],
                     lambda s: bank(4 * s, 2)[0:M, :], i)
                copy(S, P, "ot", "ot", lambda s, b: slot[s]["ot"].rearrange("p c t -> p (c t)"), lambda s: bank(4 * s + 2), i)
            S, P = g1["act"], g1["pe"]
            act.wait_ge(*x1["pe"].at("out", B - 1))
            for i in range(B // 2):
                copy(S, P, "xt", "xt", lambda s, b: slot[s]["xp"][:, 1:T + 1], lambda s: PS[:, 4 * s, 0:T], i)
                copy(S, P, "yt", "yt", lambda s, b: slot[s]["yt"], lambda s: PS[:, 4 * s + 1, 0:T], i)
                copy(S, P, "q", "q", lambda s, b: slot[s]["qt"], lambda s: PS[:, 4 * s, 0:T], i, ACT.Identity, F1B[:, 0:1])
                copy(S, P, "k", "k", lambda s, b: slot[s]["kt"], lambda s: PS[:, 4 * s + 1, 0:T], i, ACT.Identity, F1B[:, 1:2])
                copy(S, g1["dve"], "p", "sub", lambda s, b: slot[s]["p"], lambda s: slot[s]["p"], i, ACT.Exp,
                     scale=float(1 / np.sqrt(HD0)))
                copy(S, P, "pt0", "pt0", lambda s, b: slot[s]["pt"][:, 0:1024], lambda s: bank(4 * s, 2), i)
                copy(S, P, "ot", "ot", lambda s, b: slot[s]["ot"][:, 0, :], lambda s: PS[:, 4 * s + 1, 0:T], i)
                copy(S, P, "xat", "xat", lambda s, b: XAT1[:, b, :], lambda s: PS[:, 4 * s + 1, 0:T], i)
            S, P = f1["act"], f1["pe"]
            act.wait_ge(*f1["dve"].at("gsub"))
            act.activation(SMALL[:, 0, :, :], SMALL[:, 0, :, :], ACT.Exp).then_inc(*S.did("gexp"))
            act.wait_ge(*P.at("pt"))
            act.activation(PROBT[0:E1, :, :].rearrange("p b t -> p (b t)"), bank(0, 2)[0:E1, :], ACT.Copy).then_inc(*S.did("pt"))
            act.wait_ge(*f1["dve"].at("b2"))
            for k, (h, e, c) in enumerate(units(4)):
                act.wait_ge(*P.at("hg", h, e, c))
                if k >= 4:
                    ub = units(4)[k - 4]
                    act.wait_ge(*P.at("y" if ub[2] == 3 else "yp", *(ub[:2] if ub[2] == 3 else ub)))
                act.activation(ACTB[:, k % 4, :], bank(k % 4), ACT.Relu, bias=B1[:, e, c:c + 1])\
                   .then_inc(*S.did("relu", h, e, c))

        @block.tensor
        def _(pe):
            def mm(out_, lhs, rhs, start=True, stop=True, **k):
                return pe.matmul(out_, lhs, rhs, start=start, stop=stop, **k)

            def bias(out_, name, n=D, p=128):
                mm(out_, ONES[0:1, 0:p], row(name, n, 1), True, False)

            pe.wait_ge(ld_ctx, 48)
            for g in range(2):
                i = mm(bank(g)[:, 0:4 * M], X0K, CTXT[:, 4 * g:4 * g + 4, :].rearrange("p b m -> p (b m)"))
            i.then_inc(*mpe.did("kt0"))
            pe.wait_ge(ld_c, 48)
            pe.wait_ge(*mdve.at("const"))
            for b in range(B):
                o = PS[0:M, 2 + b // 4, (b % 4) * D:(b % 4 + 1) * D]
                bias(o, "x0_bv", p=M)
                i = mm(o, CTXT[:, b, :], X0V, False, True)
            i.then_inc(*mpe.did("v0"))
            pe.wait_ge(ld_x, 32)
            pe.wait_ge(*mdve.at("cb"))
            for b in range(B):
                i = pe.transpose(PS[:, 4 + b // 4, (b % 4) * T:(b % 4) * T + M], CTX[:, b, :], IDN[0:M, 0:M])
            i.then_inc(*mpe.did("ct"))
            pe.wait_ge(*mdve.at("xn"))
            for b in range(B):
                i = pe.transpose(PS[:, 6 + b // 4, (b % 4) * T:(b % 4 + 1) * T], XN[:, b, :], IDN)
            i.then_inc(*mpe.did("xnt"))
            pe.wait_ge(ld_m, 32)
            pe.wait_ge(*mdve.at("diag"))
            pe.wait_ge(*mact.at("xnt"))
            pe.nop().then_inc(L["yacc"], CREDIT)
            xnt = XNT[:, :, :].rearrange("p b t -> p (b t)")
            for d in range(2):
                for c in range(4):
                    if d:
                        pe.wait_ge(*mact.at("xp" if c < NC else "zs", 0))
                    for h in range(2):
                        i = mm(bank(2 * c + h), WIN[:, d, c * 128:(c + 1) * 128], xnt[:, h * HALF:(h + 1) * HALF])
                    i.then_inc(*mpe.did(f"xz{c}", d))
            for d in range(2):
                pe.wait_ge(*mact.at("u", d))
                pe.wait_ge(*mact.at("xp", 1))
                if d:
                    pe.wait_ge(*mact.at("dts", 0))
                    pe.wait_ge(*mdve.at("s3", 0))
                for h in range(2):
                    for c in range(NC):
                        mm(bank(h)[0:DR, :], WDT[:, d, c, :], U[d][:, c, h * HALF:(h + 1) * HALF], c == 0, c == NC - 1)
                    for c in range(NC):
                        i = mm(bank(2 + h)[0:96, :], WBC[:, d, c, :], U[d][:, c, h * HALF:(h + 1) * HALF],
                               c == 0, c == NC - 1)
                i.then_inc(*mpe.did("dbc", d))
                pe.wait_ge(*mact.at("dts", d))
                if d == 0:
                    pe.wait_ge(*mact.at("zs", 1))
                for c in range(NC):
                    for h in range(2):
                        i = mm(bank(4 + 2 * c + h), DTW[:, d, c * 128:(c + 1) * 128], DTS[0:DR, h * HALF:(h + 1) * HALF])
                    i.then_inc(*mpe.did(f"dt{c}", d))
            pe.wait_ge(*mact.at("abs1", 1))
            pe.wait_ge(*mdve.at("s3", 1))
            for d in range(2):
                if d:
                    pe.wait_ge(*mdve.at("y", 0))
                for c in range(NC):
                    for h in range(2):
                        i = mm(bank(4 + 2 * c + h), DIAG[:, d, c, :], U[d][:, c, h * HALF:(h + 1) * HALF], True, False)
                i.then_inc(*mpe.did("y0", d))
                base = d * DS + CREDIT

                def rows_bc(st, n):
                    for k, off, ps in (("b", 0, 0), ("c", DS, 2)):
                        pe.wait_ge(L[f"{k}_sb"], n)
                        for h in range(2):
                            ins = mm(bank(ps + h), SEL[:, bass.ds(st + off, 1)].to_broadcast([128, 128]),
                                     S3[d][:, h * HALF:(h + 1) * HALF])
                        ins.then_inc(L[f"{k}_ps"], 1)

                def sum_y(s, n, stop=False):
                    for c in range(NC):
                        pe.wait_ge(L[f"hc{c}"], n + 1)
                        for h in range(2):
                            ins = mm(bank(4 + 2 * c + h), IDN, HB[s][:, c, h * HALF:(h + 1) * HALF], False, stop)
                    ins.then_inc(L["yacc"], 1)

                rows_bc(0, base)
                rows_bc(1, base + 1)
                with pe.Fori(0, DS // 4 - 1) as it:
                    for s in range(4):
                        rows_bc(it * 4 + (s + 2), it * 4 + (s + 2 + base))
                        sum_y(s, it * 4 + (s + base))
                for s in range(4):
                    if s < 2:
                        rows_bc(DS - 2 + s, base + DS - 2 + s)
                    sum_y(s, base + DS - 4 + s, s == 3)
            pe.wait_ge(*mdve.at("y", 1))
            for b in range(B):
                for d in range(2):
                    for c in range(NC):
                        i = mm(PS[:, b // 4, (b % 4) * D:(b % 4 + 1) * D], ZS[:, d, c, b * T:(b + 1) * T],
                               WOUT[:, d, c, :], d == c == 0, d == c == 1)
            i.then_inc(*mpe.did("out"))

            def turn(S, A, step, wait, out_, src, i):
                for s in range(2):
                    b = 2 * i + s
                    pe.wait_ge(*A.at(wait, b))
                    pe.transpose(out_(s), src(s), IDN).then_inc(*S.did(step, b))

            def attend(S, DV, A, i, keys, values, free0):
                for half in range(2):
                    for s in range(2):
                        b = 2 * i + s
                        if half == 0:
                            pe.wait_ge(*A.at("p", b))
                        for h in range(8 * half, 8 * half + 8):
                            ins = pe.transpose(PS[0:keys, 4 * s + h // 4, (h % 4) * T:(h % 4 + 1) * T],
                                               slot[s]["p"][:, h * keys:(h + 1) * keys], IDN)
                        ins.then_inc(*S.did(f"pt{half}", b))
                for s in range(2):
                    b = 2 * i + s
                    pe.wait_ge(*A.at("pt0", b))
                    pe.wait_ge(*DV.at("pt1", b))
                    for h in range(H0):
                        ins = mm(PS[:, 4 * s, h * (HD0 + 1):(h + 1) * (HD0 + 1)],
                                 slot[s]["pt"][0:keys, h * T:(h + 1) * T], values(s, b)[:, h, :])
                    ins.then_inc(*S.did("pv", b))
                turn(S, DV, "ot", "o", lambda s: PS[:, 4 * s + 1, 0:T], lambda s: slot[s]["o"][:, 0:D], i)

            S, A, DV = x0["pe"], x0["act"], x0["dve"]
            for i in range(B // 2):
                turn(S, DV, "xt", "xn", lambda s: PS[:, 4 * s + 3, 384:512], lambda s: slot[s]["xn"], i)
                for s in range(2):
                    b = 2 * i + s
                    o = PS[:, 4 * s + 3, 384:512]
                    pe.wait_ge(*A.at("xt", b))
                    bias(o, "x0_bq")
                    mm(o, slot[s]["xt"], X0Q, False, True).then_inc(*S.did("q", b))
                turn(S, DV, "qt", "rope", lambda s: PS[:, 4 * s + 3, 384:512], lambda s: slot[s]["qr"], i)
                for s in range(2):
                    b = 2 * i + s
                    pe.wait_ge(*A.at("qt", b))
                    pe.wait_ge(*x0["pool"].at("kx", b))
                    for g in range(4):
                        ins = mm(PS[:, 4 * s + g, 0:4 * M], slot[s]["qt"], slot[s]["kx"][:, 4 * g * M:4 * (g + 1) * M])
                    ins.then_inc(*S.did("sc", b))
                attend(S, DV, A, i, M, lambda s, b: V0[:, b, :, :], None)
                for s in range(2):
                    b = 2 * i + s
                    o = PS[:, 4 * s + 2, 0:D]
                    pe.wait_ge(*A.at("ot", b))
                    bias(o, "x0_bo")
                    mm(o, slot[s]["ot"][:, 0, :], X0O, False, True).then_inc(*S.did("wo", b))

            def moe_units(F, n, w_in, w_out, rhs):
                S = F["pe"]
                us = units(n)

                def hidden(k):
                    h, e, c = us[k]
                    if len(w_in) == 2:
                        if k >= 3:
                            pe.wait_ge(*F["dve"].at("act", *us[k - 3]))
                        for j in range(2):
                            ins = mm(bank(2 * (k % 3) + j), w_in[j][:, e, c * 128:(c + 1) * 128], rhs[:, h * HALF:(h + 1) * HALF])
                    else:
                        if k >= 4:
                            pe.wait_ge(*F["act"].at("relu", *us[k - 4]))
                        ins = mm(bank(k % 4), w_in[0][:, e, c * 128:(c + 1) * 128], rhs[:, h * HALF:(h + 1) * HALF])
                    ins.then_inc(*S.did("hg", h, e, c))

                hidden(0)
                for k, (h, e, c) in enumerate(us):
                    if k + 1 < len(us):
                        hidden(k + 1)
                    if len(w_in) == 2:
                        pe.wait_ge(*F["dve"].at("act", h, e, c))
                    else:
                        pe.wait_ge(*F["act"].at("relu", h, e, c))
                    ring = 3 if len(w_in) == 2 else 4
                    if c == 0 and h * E0 + e >= 2:
                        ph, pe_ = divmod(h * E0 + e - 2, E0)
                        pe.wait_ge(*F["dve"].at("acc", ph, pe_))
                    for j in range(4):
                        ins = mm(PS[:, 6 + e % 2, j * D:(j + 1) * D], ACTB[:, k % ring, j * T:(j + 1) * T],
                                 w_out[:, e, c, :], c == 0 and j == 0, c == n - 1 and j == 3, skip_group_check=True)
                    if c == n - 1:
                        ins.then_inc(*S.did("y", h, e))
                    else:
                        ins.then_inc(*S.did("yp", h, e, c))

            S, A, DV = f0["pe"], f0["act"], f0["dve"]
            pe.wait_ge(ld_w1, 32)
            pe.wait_ge(*DV.at("xn"))
            for b in range(B):
                i = pe.transpose(PS[:, b // 4, (b % 4) * T:(b % 4 + 1) * T], XA[:, b, :], IDN)
            i.then_inc(*S.did("xnt"))
            pe.wait_ge(*A.at("xnt"))
            for b in range(B):
                i = mm(bank(4)[:, b * E0:(b + 1) * E0], XNT[:, b, :], f_g)
            i.then_inc(*S.did("gate"))
            pe.wait_ge(*DV.at("lg"))
            moe_units(f0, 2, FW, FW3, xnt)

            S, A, DV = a1["pe"], a1["act"], a1["dve"]
            for i in range(B // 2):
                turn(S, DV, "xt", "xn", lambda s: PS[:, 4 * s, 0:T], lambda s: slot[s]["xn"], i)
                for k, (step, bk) in enumerate((("q", 1), ("k", 2))):
                    for s in range(2):
                        b = 2 * i + s
                        if k == 0:
                            pe.wait_ge(*A.at("xt", b))
                        mm(PS[:, 4 * s + bk, 0:T], A1W[:, k * D:(k + 1) * D], slot[s]["xt"]).then_inc(*S.did(step, b))
                for s in range(2):
                    o = PS[:, 4 * s + 3, 0:D]
                    bias(o, "a1_bv")
                    mm(o, slot[s]["xt"], A1W[:, 2 * D:3 * D], False, True).then_inc(*S.did("v", 2 * i + s))
                for s in range(2):
                    b = 2 * i + s
                    pe.wait_ge(*A.at("q", b))
                    pe.wait_ge(*A.at("k", b))
                    mm(PS[:, 4 * s, 0:T], slot[s]["qt"], slot[s]["kt"]).then_inc(*S.did("s", b))
                turn(S, A, "pt", "p", lambda s: PS[:, 4 * s + 1, 0:T], lambda s: slot[s]["p"][:, 0:T], i)
                for s in range(2):
                    b = 2 * i + s
                    pe.wait_ge(*A.at("pt", b))
                    pe.wait_ge(*DV.at("v", b))
                    mm(PS[:, 4 * s + 2, 0:T], slot[s]["y"], slot[s]["pt"][:, 0:T]).then_inc(*S.did("o", b))
                for s in range(2):
                    b = 2 * i + s
                    pe.wait_ge(*A.at("o", b))
                    mm(PS[:, 4 * s + 1, D:2 * D], slot[s]["ot"][:, 0, :], A1P).then_inc(*S.did("out", b))

            S, A, DV = x1["pe"], x1["act"], x1["dve"]
            pe.wait_ge(ld_x1, 16)
            for i in range(B // 2):
                turn(S, DV, "lt", "l2", lambda s: PS[:, 4 * s, 0:T], lambda s: slot[s]["l2"], i)
                for s in range(2):
                    b = 2 * i + s
                    pe.wait_ge(*A.at("lt", b))
                    for c in range(4):
                        ins = mm(PS[:, 4 * s + 1, c * T:(c + 1) * T], X1Q[:, c * 128:(c + 1) * 128], KVT[:, b, M:J1])
                    ins.then_inc(*S.did("q", b))
                for s in range(2):
                    b = 2 * i + s
                    for c in range(4):
                        if c == 2:
                            pe.wait_ge(*A.at("q", b))
                        ins = mm(PS[:, 4 * s + c // 2, (c % 2) * J1:(c % 2 + 1) * J1], X1KV[:, c * 128:(c + 1) * 128],
                                 KVT[:, b, :])
                    ins.then_inc(*S.did("k", b))
                for s in range(2):
                    b = 2 * i + s
                    mm(bank(4 * s + 2)[0:M, :], KVT[:, b, 0:M], X1KV[:, 512:1024])
                    mm(bank(4 * s + 3), KVT[:, b, M:J1], X1KV[:, 512:1024]).then_inc(*S.did("v", b))
                for s in range(2):
                    b = 2 * i + s
                    pe.wait_ge(*A.at("k", b))
                    pe.wait_ge(*DV.at("v", b))
                    for c in range(4):
                        for odd in range(2):
                            rows_ = slice(64 * odd, 64 * odd + 64)
                            ins = mm(PS[:, 4 * s + 2 * odd + c // 2, (c % 2) * J1:(c % 2 + 1) * J1],
                                     slot[s]["qt1"][rows_, c, :], slot[s]["kt1"][rows_, c, :])
                    ins.then_inc(*S.did("s", b))
                for s in range(2):
                    b = 2 * i + s
                    pe.wait_ge(*A.at("p", b))
                    for h in range(H1):
                        p1 = slot[s]["p1"][:, h * J1:(h + 1) * J1]
                        pe.transpose(PS[0:M, 4 * s + h // 4, (h % 4) * T:(h % 4 + 1) * T], p1[:, 0:M], IDN)
                        ins = pe.transpose(PS[:, 4 * s + 2 + h // 4, (h % 4) * T:(h % 4 + 1) * T], p1[:, M:J1], IDN)
                    ins.then_inc(*S.did("pt", b))
                for s in range(2):
                    b, v = 2 * i + s, slot[s]
                    pe.wait_ge(*A.at("pta", b))
                    pe.wait_ge(*DV.at("ptb", b))
                    for h in range(H1):
                        k = 4 * (h % 2) + h // 2
                        o = PS[:, 4 * s + h // 4, (h % 4) * (HD1 + 1):(h % 4 + 1) * (HD1 + 1)]
                        mm(o, v["pta"][0:M, k, :], v["va"][0:M, h, :], True, False)
                        ins = mm(o, v["ptb"][:, k, :], v["vb"][:, h, :], False, True)
                    ins.then_inc(*S.did("o", b))
                for s in range(2):
                    b, v = 2 * i + s, slot[s]
                    pe.wait_ge(*DV.at("o", b))
                    for c in range(4):
                        ins = pe.transpose(PS[:, 4 * s + 2, c * T:(c + 1) * T], v["o"][:, c * 128:(c + 1) * 128], IDN)
                    ins.then_inc(*S.did("ot", b))
                for s in range(2):
                    b, v = 2 * i + s, slot[s]
                    pe.wait_ge(*A.at("ot", b))
                    for c in range(4):
                        ins = mm(PS[:, 4 * s + 3, 0:D], v["ot"][:, c, :], X1O[:, c, :], c == 0, c == 3)
                    ins.then_inc(*S.did("out", b))

            S, A, DV = g1["pe"], g1["act"], g1["dve"]
            pe.wait_ge(ld_w2, 32)
            for i in range(B // 2):
                turn(S, DV, "xt", "xn", lambda s: PS[:, 4 * s, 0:T], lambda s: slot[s]["xn"], i)
                for s in range(2):
                    b = 2 * i + s
                    o = PS[:, 4 * s, 0:D]
                    pe.wait_ge(*A.at("xt", b))
                    bias(o, "conv_b")
                    for k in range(3):
                        ins = mm(o, slot[s]["xp"][:, k:k + T], GC[:, k, :], False, k == 2)
                    ins.then_inc(*S.did("y", b))
                turn(S, DV, "yt", "y", lambda s: PS[:, 4 * s + 1, 0:T], lambda s: slot[s]["y"], i)
                for k, step in enumerate(("q", "k")):
                    for s in range(2):
                        b = 2 * i + s
                        if k == 0:
                            pe.wait_ge(*A.at("yt", b))
                        mm(PS[:, 4 * s + k, 0:T], G_QKV[:, k * D:(k + 1) * D], slot[s]["yt"]).then_inc(*S.did(step, b))
                for s in range(2):
                    o = PS[:, 4 * s + 2, D:2 * D]
                    bias(o, "f1_bv")
                    mm(o, slot[s]["yt"], G_QKV[:, 2 * D:3 * D], False, True).then_inc(*S.did("v", 2 * i + s))
                for s in range(2):
                    b = 2 * i + s
                    pe.wait_ge(*A.at("q", b))
                    pe.wait_ge(*DV.at("v", b))
                    pe.wait_ge(*g1["pool"].at("kx", b))
                    for g in range(4):
                        ins = mm(bank(4 * s + g), slot[s]["qt"], slot[s]["kx"][:, 4 * g * T:4 * (g + 1) * T])
                    ins.then_inc(*S.did("s", b))
                attend(S, DV, A, i, T, lambda s, b: slot[s]["v1"], None)
                for s in range(2):
                    b = 2 * i + s
                    o = PS[:, 4 * s + 2, 0:D]
                    pe.wait_ge(*A.at("ot", b))
                    bias(o, "f1_bo")
                    mm(o, slot[s]["ot"][:, 0, :], G_O, False, True).then_inc(*S.did("wo", b))
                for s in range(2):
                    b = 2 * i + s
                    pe.wait_ge(*DV.at("xa", b))
                    pe.transpose(PS[:, 4 * s + 1, 0:T], XN1[:, b, :], IDN).then_inc(*S.did("xat", b))
                for s in range(2):
                    b = 2 * i + s
                    o = PS[:, 4 * s + 3, 0:E1]
                    pe.wait_ge(*A.at("xat", b))
                    bias(o, "gate_b", E1)
                    mm(o, XAT1[:, b, :], G_G, False, True).then_inc(*S.did("gate", b))

            S, A, DV = f1["pe"], f1["act"], f1["dve"]
            pe.wait_ge(*DV.at("prob"))
            for b in range(B):
                i = pe.transpose(PS[0:E1, b // 4, (b % 4) * T:(b % 4 + 1) * T], PROB[:, b, :], IDN)
            i.then_inc(*S.did("pt"))
            pe.wait_ge(*A.at("pt"))
            for b in range(B):
                i = mm(PS[:, 4 + b // 4, (b % 4) * D:(b % 4 + 1) * D], PROBT[0:E1, b, :], B2[:, :])
            i.then_inc(*S.did("b2"))
            moe_units(f1, 4, [G1], G2, XAT1.rearrange("p b t -> p (b t)"))


def _constants():
    c = np.zeros((128, 156 + 2 * DS), np.float32)
    c[:, 0:128] = np.eye(128)
    c[:, 128:144] = np.arange(128)[:, None] // HD0 == np.arange(H0)[None, :]
    c[:, 144:148] = 1.0 / 10000.0 ** (np.arange(0, HD0, 2, dtype=np.float32) / HD0)
    c[:, 148:156] = np.arange(8)
    for r in range(96):
        c[r, 156 + r % 32] = 1
    return c


def kernel(**inp):
    import concourse.bacc as bacc
    from concourse.bass_utils import run_bass_kernel_spmd

    a = {k: np.asarray(v) for k, v in inp.items()}
    m = {d: {k[len("L0_attn_"):-2]: v for k, v in a.items() if k.startswith("L0_attn_") and k.endswith("_" + d)} for d in "fb"}

    def flat(*parts):
        return np.ascontiguousarray(np.concatenate([p.reshape(p.shape[0], -1) for p in parts], axis=1))

    def chunks(w, n=128):
        return w.reshape(w.shape[0] // n, n, -1).transpose(1, 0, 2)

    consts = _constants()
    w_m = flat(*[m[d]["in_proj"].T for d in "fb"],
               *[chunks(m[d]["x_proj"][0:DR].T) for d in "fb"],
               *[np.concatenate([chunks(m[d]["x_proj"][DR:].T)] * 3, axis=2) for d in "fb"],
               *[chunks(m[d]["out_proj"].T) for d in "fb"])
    dtw_t = np.ascontiguousarray(np.stack([m[d]["dt_w"].T for d in "fb"], axis=1))
    rows = {"ln_w": a["L0_attn_ln_w"], "ln_b": a["L0_attn_ln_b"], "gm": a["L1_xattn_gm"], "bm": a["L1_xattn_bm"],
            "gl": a["L1_xattn_gl"], "bl": a["L1_xattn_bl"], "ln1_g": a["L1_ffn_ln1_g"], "ln1_b": a["L1_ffn_ln1_b"],
            "ln2_g": a["L1_ffn_ln2_g"], "ln2_b": a["L1_ffn_ln2_b"], "x0_bq": a["L0_xattn_bq"],
            "x0_bv": a["L0_xattn_bv"], "x0_bo": a["L0_xattn_bo"], "a1_bv": a["L1_attn_b_qkv"][2 * D:],
            "a1_bproj": a["L1_attn_b_proj"], "conv_b": a["L1_ffn_conv_b"], "f1_bv": a["L1_ffn_bqkv"][2 * D:],
            "f1_bo": a["L1_ffn_bo"], "gate_b": a["L1_ffn_gate_b"]}
    row = np.zeros((1, len(ROWS) * D), np.float32)
    for i, k in enumerate(ROWS):
        row[0, i * D:i * D + rows[k].size] = rows[k]
    both = "fb"
    cols = flat(*[chunks(m[d]["conv_w"]) for d in both], *[chunks(m[d]["conv_b"][:, None]) for d in both],
                *[chunks(m[d]["dt_b"][:, None]) for d in both], *[chunks(m[d]["D"][:, None]) for d in both],
                *[chunks(m[d]["A_log"]) for d in both], a["L0_xattn_bk"][:, None],
                a["L1_attn_b_qkv"][0:2 * D].reshape(2, D).T, a["L1_ffn_bqkv"][0:2 * D].reshape(2, D).T,
                a["L1_ffn_b1"].reshape(E1, 4, 128).transpose(2, 0, 1))
    arrays = {
        "x": a["x"], "ctx": a["ctx_1024"], "ctx_t": np.ascontiguousarray(a["ctx_1024"].transpose(2, 0, 1)),
        "pos": np.ascontiguousarray(a["itok_BxS_1_4095"].T), "w_m": w_m, "dtw_t": dtw_t, "consts": consts,
        "rows": row, "cols": cols,
        "w_x0": flat(*[a[f"L0_xattn_W{k}"].T for k in "qkvo"]),
        "w_f0": flat(a["L0_ffn_Wg"], *[a[f"L0_ffn_W{k}"].transpose(1, 0, 2) for k in (1, 2)],
                     a["L0_ffn_W3"].reshape(E0, 2, 128, D).transpose(2, 0, 1, 3)),
        "w_a1": flat(a["L1_attn_W_qkv"], a["L1_attn_W_proj"]),
        "w_x1": flat(a["L1_xattn_Wq"], a["L1_xattn_Wkv"], chunks(a["L1_xattn_Wout"])),
        "w_f1": flat(a["L1_ffn_conv_w"].transpose(1, 2, 0), a["L1_ffn_wqkv"].T, a["L1_ffn_wo"].T, a["L1_ffn_gate_w"],
                     a["L1_ffn_w1"].transpose(1, 0, 2), a["L1_ffn_w2"].reshape(E1, 4, 128, D).transpose(2, 0, 1, 3)),
        "b2": a["L1_ffn_b2"],
    }
    nc = bacc.Bacc("TRN2", target_bir_lowering=False, num_devices=1)
    args = [nc.dram_tensor(f"in_{k}", v.shape, mybir.dt.from_np(v.dtype), kind="ExternalInput").ap()
            for k, v in arrays.items()]
    out = nc.dram_tensor("out_x", (B, T, D), F32, kind="ExternalOutput").ap()
    decoder_kernel(nc, *args, out)
    r = run_bass_kernel_spmd(nc, [{f"in_{k}": v for k, v in arrays.items()}], core_ids=[0])
    return r.results[0]["out_x"]
```

```python
from contextlib import ExitStack

import numpy as np

import concourse.bass as bass
from concourse import mybir

F32 = mybir.dt.float32
BF16 = mybir.dt.bfloat16
I32 = mybir.dt.int32
U32 = mybir.dt.uint32
ALU = mybir.AluOpType
ACT = mybir.ActivationFunctionType
AX = mybir.AxisListType.X

B, T, D = 8, 128, 128
N = B * T
M = 77
H0, HD0 = 16, 8
DI, DS, DC, DR = 256, 16, 4, 64
NC = DI // 128
E0, HID0 = 8, 256
H1, HD1 = 8, 64
J1 = M + T
E1, HID1 = 8, 512
EPS = 1e-5
MAGIC = 1.5 * 2.0 ** 23
TWO_PI = (6.28125, 0.0019350051879882812, 3.0198604e-07)
HALF = N // 2

ROWS = ["ln_w", "ln_b", "gm", "bm", "gl", "bl", "ln1_g", "ln1_b", "ln2_g", "ln2_b",
        "x0_bq", "x0_bv", "x0_bo", "a1_bv", "a1_bproj", "conv_b", "f1_bv", "f1_bo", "gate_b"]


class Steps:

    def __init__(self, sem, order):
        self.sem, self.order, self.n = sem, list(order), 0
        self.value = {k: i + 1 for i, k in enumerate(self.order)}
        assert len(self.value) == len(self.order)

    def at(self, *key):
        return self.sem, self.value[key]

    def did(self, *key):
        assert self.order[self.n] == key, (self.order[self.n], key)
        self.n += 1
        return self.sem, 1


def after(engine, steps, step, n):
    if n >= 0:
        engine.wait_ge(*steps.at(step, n))


def pipeline(sem, timeline, name, start, period, sequence, group=None, dve_turns=()):
    steps = {}
    for e in ("pe", "act", "dve", "pool"):
        places = [(round(start + b * period + t, 3), name, step, b) for step, t in sequence[e].items() for b in range(B)]
        places += [(round(start + k * period / 4 + t, 3), name, step, k)
                   for step, t in (group or {}).get(e, {}).items() for k in range(4 * B)
                   if not (step == "pt" and e in ("act", "dve") and (k % 4 in dve_turns) != (e == "dve"))]
        steps[e] = Steps(sem(f"{e}_{name}"), [key[2:] for key in sorted(places)])
        timeline[e] += places
    return steps


def decoder_kernel(nc, x, ctx, ctx_t, pos, w_m, dtw_t, consts, rows, cols, w_x0, w_f0, w_a1, w_x1, w_f1, b2, out):
    with ExitStack() as stack:
        def sb(name, shape, dt=F32):
            return stack.enter_context(nc.sbuf_tensor(name, shape, dt))

        def sem(name):
            return stack.enter_context(nc.semaphore(name))

        X = sb("residual", [T, B, D])
        XNT = sb("normed_t", [D, B, T])
        CTX = sb("context", [M, B, D])
        CTXT = sb("context_t", [D, B, M])
        KT0 = sb("x0_keys_t", [D, B, M])
        V0 = sb("x0_values", [M, B, H0, HD0 + 1])
        KVT = sb("x1_kv_input_t", [D, B, J1])
        WM = sb("w_m", [128, w_m.shape[1]])
        DTW = sb("dt_w_t", [DR, 2, DI])
        SEL = sb("row_selectors", [128, 2 * DS], BF16)
        CONST = sb("consts", [128, consts.shape[1]])
        ROW = sb("rows", [128, len(ROWS) * D])
        COL = sb("cols", [128, cols.shape[1]])
        WX0 = sb("w_x0", [128, w_x0.shape[1]])
        WF0 = sb("w_f0", [128, w_f0.shape[1]])
        WA1 = sb("w_a1", [128, w_a1.shape[1]])
        WX1 = WM[:, 0:w_x1.shape[1]]
        WF1 = sb("w_f1", [128, w_f1.shape[1]])
        B2 = sb("moe1_b2", [E1, D])
        POSI = sb("positions", [T, B], I32)
        ROPE = sb("rope_tables", [T, 2, B, 2, 4])
        ONES = sb("ones", [128, 128])
        HALFNEG = sb("minus_half", [128, B])
        DIAG = sb("diag_D", [128, 2, NC, 128])
        NEGA = sb("neg_A", [128, 2, NC, DS])
        ST6 = sb("bn_stats", [128, B, 6])
        MV = sb("mean_var", [128, B, 2])
        RS = sb("rstd", [128, B])
        SMALL = sb("small", [128, 8, B, 8])
        TOPI = sb("top_index", [128, B, 8], U32)
        PS = stack.enter_context(nc.psum_tensor("ps", [128, 8, 512], F32))

        ARENA_N = 22016
        ARENA = sb("arena", [128, ARENA_N])

        class Region:
            def __init__(self, start=0, of=None):
                self.o, self.of = start, ARENA if of is None else of

            def take(self, *shape):
                n = int(np.prod(shape))
                v = self.of[:, self.o:self.o + n]
                self.o += n
                assert self.o <= self.of.shape[1], self.o
                if len(shape) > 1:
                    names = "abcd"[:len(shape)]
                    v = v.rearrange(f"p ({' '.join(names)}) -> p {' '.join(names)}",
                                    **{k: s for k, s in zip(names[1:], shape[1:])})
                return v

        r = Region()
        XN = r.take(B, D)
        ZS = r.take(2, NC, N)
        U = [r.take(NC, N)]
        DELTA = [r.take(NC, N)]
        S3 = [r.take(N // 2).bitcast(BF16)]
        DU = [U[0]]
        m_shared = r.o
        DA = r.take(2, NC, N)
        HB = [r.take(NC, N) for _ in range(2)]
        BS = r.take(2, N)
        CS = r.take(2, N)
        q = Region(m_shared)
        DTS, RES = [q.take(N)], [q.take(N)]
        SPR, SPE = [q.take(NC, N)], [q.take(NC, N)]
        XP = [q.take(NC, B, T + DC - 1)]
        SMALLE = [q.take(NC * N).bitcast(I32)]
        f = Region(0, WF0)
        DTS.append(f.take(N))
        RES.append(f.take(N))
        SPR.append(f.take(NC, N))
        f0_end = f.o
        DU.append(WF0[:, f.o - NC * N:f.o].rearrange("p (c n) -> p c n", c=NC))
        f = Region(0, WF1)
        XP.append(f.take(NC, B, T + DC - 1))
        SMALLE.append(f.take(NC * N).bitcast(I32))
        second_u = f.o
        f = Region(0, WF1)
        HB += [f.take(NC, N) for _ in range(2)]
        f = Region(max(second_u, f.o), WF1)
        U.append(f.take(NC, N))
        DELTA.append(f.take(NC, N))
        S3.append(f.take(N // 2).bitcast(BF16))
        SPE.append(Region(f0_end, WF0).take(NC, N))
        SPL = [t[:, o:o + NC * N].rearrange("p (c n) -> p c n", c=NC) for t, o in ((ARENA, m_shared), (WF0, 0))]
        SPT = [XP[d].rearrange("p c b t -> p (c b t)")[:, 0:NC * N] for d in range(2)]

        def slots(n, **sizes):
            return [{k: region.take(*(size if isinstance(size, tuple) else (size,))) for k, size in sizes.items()}
                    for _ in range(n)]

        small = dict(xn=D, st=6, mv=2, var=1, rs=1)
        second = dict(st2=6, mv2=2, var2=1, rs2=1)
        region = Region()
        X0S = slots(4, xt=D, r1=D, r2=D, qr=D, qt=D, o=D, ot=D, xn2=D, rz=H0, **small, **second)
        X0U = slots(3, kx=(4, M), mx=4, p=4 * M, pt=4 * T)
        region = Region()
        X1S = slots(2, qt=(4, T), kt=(4, J1), va=(H1, HD1 + 1), vb=(H1, HD1 + 1), l1=D, l2=D, o=H1 * HD1, ot=(4, T),
                    rz=H1, **small, **second)
        X1U = slots(3, mx=2, p=(2, J1), pta=(2, T), ptb=(2, T))
        after_x1 = region.o
        A1S = slots(6, xt=D, qt=D, kt=D, v=D, a=D, r1=D, r2=D, p=D, pt=D, ot=D, y=D, mx=1, z=1, rz=1, **small)
        region = Region(after_x1)
        G1S = slots(4, xp=T + 2, y=D, yt=D, qt=D, kt=D, v=(H0, HD0 + 1), o=D, ot=D, l1=D, rz=H0, **small, **second)
        G1U = slots(3, kx=(4, T), mx=4, p=4 * T, pt=4 * T)
        r = Region()
        ACTS = r.take(4, HALF)
        ACTB = r.take(4, HALF)
        XA = r.take(B, D)
        XAT = r.take(B, T)
        PROB = r.take(B, E1)
        PROBT = r.take(B, T)
        FIN = r.take(B, D)
        XN1 = XNT[:, :, :]
        XAT1 = KVT[:, :, :].rearrange("p b j -> p (b j)")[:, 0:N].rearrange("p (b t) -> p b t", b=B)

        def row(name, n=D, p=128):
            i = ROWS.index(name)
            return ROW[0:p, i * D:i * D + n]

        def row_b(name, p=128):
            return row(name, D, p).unsqueeze(1).to_broadcast([p, B, D])

        IDN = CONST[:, 0:128]
        MASK = CONST[:, 128:128 + H0]
        FREQ = CONST[:, 144:148]
        IOTA = CONST[:, 148:156]
        c0 = [0]

        def col(n):
            c0[0] += n
            return COL[:, c0[0] - n:c0[0]]

        CONVW = [col(NC * DC).rearrange("p (c k) -> p c k", c=NC) for _ in range(2)]
        CONVB = [col(NC) for _ in range(2)]
        DTB = [col(NC) for _ in range(2)]
        DSK = [col(NC) for _ in range(2)]
        ALOG = col(2 * NC * DS)
        X0BK = col(1)
        A1B = col(2)
        F1B = col(2)
        B1 = col(E1 * 4).rearrange("p (e c) -> p e c", e=E1)

        def split(t, *sizes):
            o, parts = 0, []
            for n in sizes:
                parts.append(t[:, o:o + n])
                o += n
            return parts

        m_in, m_dt, m_bc, m_out = split(WM, 2 * 512, 2 * NC * DR, 2 * NC * 96, 2 * NC * 128)
        WIN = m_in.rearrange("p (d n) -> p d n", d=2)
        WDT = m_dt.rearrange("p (d c n) -> p d c n", d=2, c=NC)
        WBC = m_bc.rearrange("p (d c n) -> p d c n", d=2, c=NC)
        WOUT = m_out.rearrange("p (d c n) -> p d c n", d=2, c=NC)
        X0Q, X0K, X0V, X0O = split(WX0, D, D, D, D)
        f_1, f_2, f_3 = split(WF0, E0 * HID0, E0 * HID0, E0 * 2 * D)
        FW = [f_1.rearrange("p (e n) -> p e n", e=E0), f_2.rearrange("p (e n) -> p e n", e=E0)]
        FW3 = f_3.rearrange("p (e c n) -> p e c n", e=E0, c=2)
        A1W, A1P, f_g = split(WA1, 3 * D, D, E0)
        X1Q, X1KV, x1_o = split(WX1, 512, 1024, 4 * D)
        X1O = x1_o.rearrange("p (c n) -> p c n", c=4)
        g_c, G_QKV, G_O, G_G, g_1, g_2 = split(WF1, 3 * D, 3 * D, D, E1, E1 * HID1, E1 * 4 * D)
        GC = g_c.rearrange("p (k n) -> p k n", k=3)
        G1 = g_1.rearrange("p (e n) -> p e n", e=E1)
        G2 = g_2.rearrange("p (e c n) -> p e c n", e=E1, c=4)

        def bank(i, n=1):
            v = PS[:, i:i + n, :]
            return v.rearrange("p a b -> p (a b)")

        ld_x, ld_m, ld_c, ld_ctx, ld_w1, ld_f0, ld_x1, ld_w2 = (
            sem(f"loaded_{n}") for n in ("x", "m", "c", "ctx", "w1", "f0", "x1", "w2"))
        stored = sem("stored")
        ones = sem("ones_of_layer")

        both = range(2)
        mpe = Steps(sem("pe_mamba"), [("xnt",)] + [(k, d) for d in both for k in ("xz0", "xz1", "xz2", "xz3")] + [
            ("kt0",), ("v0",)] + [(k, d) for d in both for k in ("dbc", "dt0", "dt1")] + [
            ("ct",), ("y0", 0), ("y0", 1), ("out", 0), ("out", 1)])
        mact = Steps(sem("act_mamba"), [("nega",), ("xnt",), ("sin_abs",), ("sin",)] + [
            (k, d) for d in both for k in ("xp", "zs")] + [("kt0",), ("v0",), ("u", 0), ("u", 1)] + [
            (k, d) for d in both for k in ("dts", "relu0", "abs0", "relu1", "abs1", "exp")] + [
            ("ct",), ("ln", 0), ("ln", 1)])
        mdve = Steps(sem("dve_mamba"), [("const",), ("stats",), ("mv",), ("var",), ("xn",)]
                     + [(f"rope{i}",) for i in range(9)] + [("rope",), ("nega",), ("diag",), ("cstats",), ("cmv",), ("cvar",)]
                     + [(k, d) for d in both for k in ("pad", "tap0", "tap1", "tap2", "conv")]
                     + [(k, 0) for k in ("s3a", "s3b", "s3c", "s3d", "s3")] + [("cn",), ("cg",), ("cb",)]
                     + [(k, 1) for k in ("s3a", "s3b", "s3c", "s3d", "s3")]
                     + [(k, d) for d in both for k in ("poly0", "poly1", "poly", "small", "pick", "delta0", "delta")]
                     + [("du", 1), ("du", 0), ("edge", 0), ("edge", 1), ("xb",), ("y", 0), ("y", 1)]
                     + [(k, h) for h in both for k in ("h", "hstats", "hmv", "hvar")]
                     + [(k, h) for h in both for k in ("hn", "hg", "x")])
        mpool = Steps(sem("pool_mamba"), [("rstd",), ("crstd",), ("hrstd", 0), ("hrstd", 1)])
        CREDIT = 4
        names = ["b_ps", "c_ps", "b_sb", "c_sb", "da0", "da1", "bu0", "bu1", "h0", "h1", "hc0", "hc1", "yacc"]
        L = {k: sem("state_" + k) for k in names}

        def timelines():
            return {e: [] for e in ("pe", "act", "dve", "pool")}

        x0 = pipeline(sem, timelines(), "x0", 0, 8.186, {
            "pe": {"xt": -10.75, "q": -9.08, "qt": -5.37, "ot": 12.88, "wo": 13.64, "xt2": 18.24, "gate": 18.67},
            "act": {"xt": -9.4, "qt": -5.53, "ot": 12.28, "xt2": 15.62},
            "dve": {"stats": -17.58, "mv": -15.75, "var": -14.5, "xn": -10.81, "rope_a": -5.17, "rope": -4.82,
                    "rz": 13.78, "o": 13.87, "res": 16.17, "stats2": 16.74, "mv2": 16.96, "var2": 18.41,
                    "xn2": 18.97, "lg": 21.26, "max": 21.49, "index": 23.71},
            "pool": {"rstd": -5.28, "rstd2": 23.78}}, {
            "pe": {"sc": -3.33, "pt": 1.04, "pv": 4.09},
            "act": {"p": -0.79, "pt": 1.51},
            "dve": {"mx": 0.58, "sub": 1, "pt": 4.35},
            "pool": {"kx": -0.26}}, (3,))

        def units(n):
            return [(h, e, c) for h in range(2) for e in range(E0) for c in range(n)]

        def moe_steps(name, n, ahead, first, act_unit, gated, second=None, half=()):
            us = units(n)
            second = second or {"pe": [], "act": []}
            hidden = [("hg",) + u for u in us]
            pe = list(first["pe"]) + hidden[:ahead] + second["pe"]
            dv = list(first["dve"])
            for i, u in enumerate(us):
                pe += hidden[i + ahead:i + ahead + 1]
                pe.append(("y",) + u[:2] if u[2] == n - 1 else ("yp",) + u)
            a = [(act_unit,) + u for u in us]
            prev = None
            for u in us:
                if gated:
                    dv.append(("act",) + u)
                if u[2] == n - 1:
                    if prev is not None:
                        dv.append(("acc",) + prev)
                        if prev[1] == E0 - 1:
                            dv += [(k, 0) for k in half]
                    prev = u[:2]
            dv.append(("acc",) + prev)
            dv += [(k, 1) for k in half]
            return {"pe": Steps(sem(f"pe_{name}"), pe),
                    "act": Steps(sem(f"act_{name}"), list(first["act"]) + a[:ahead] + second["act"] + a[ahead:]),
                    "dve": Steps(sem(f"dve_{name}"), dv),
                    "pool": Steps(sem(f"pool_{name}"), first["pool"])}

        f0 = moe_steps("f0", 2, 1, {
            "pe": [], "act": [("top_exp",)],
            "dve": [(k,) for k in ("top_i", "dif", "den", "w1", "w2", "s1", "s2", "s1w", "s2w", "comb")],
            "pool": []}, "silu", True)
        later = timelines()
        a1 = pipeline(sem, later, "a1", -35.75, 2.097, {
            "pe": {"xt": 2.67, "qkv": 4.08, "s": 5.69, "pt": 9.65, "o": 11.59, "out": 13.8},
            "act": {"xt": 4.17, "v": 5.29, "k": 5.38, "q": 5.54, "p": 8.87, "pt": 9.97, "o": 12.99},
            "dve": {"stats": -5.49, "mv": -2.27, "var": -1.8, "xn": 1.78, "a": 6.65, "l1": 6.73, "g1": 6.77,
                    "l": 7.09, "g": 7.43, "ls": 7.8, "m": 8.04, "am": 8.13, "mx": 8.64, "nmx": 8.77, "rz": 12.19,
                    "y": 15.03, "res": 16.59},
            "pool": {"rstd": -3.66}})
        x1 = pipeline(sem, later, "x1", 4.04, 14.667, {
            "pe": {"lt": -14.39, "q": -11.28, "k0": -8.95, "k1": -7.54, "va": -4.68, "vb": -4.46, "ot": 19.76,
                   "out": 23.59},
            "act": {"lt": -13.92, "q": -8.36, "k0": -7.67, "k1": -5.45, "ot": 20.79},
            "dve": {"stats": -22.19, "mv": -20.41, "var": -18.45, "xn": -15.95, "stats2": -15.76, "mv2": -15.38,
                    "var2": -14.94, "l0": -13.78, "l1": -13.52, "l2": -13.42, "vb": 3.25, "va": 4.1, "rz0": 15.79,
                    "o0": 20.24, "rz1": 21.39, "o1": 22.41, "res": 29.36},
            "pool": {"rstd": -24.92, "rstd2": -13.35}}, {
            "pe": {"s": -4.52, "pt": 0.76, "o": 5.66},
            "act": {"p": -2.56, "pt": 2.57},
            "dve": {"mx": 1.57, "sub": 1.9},
            "pool": {}})
        g1 = pipeline(sem, later, "g1", 128.98, 10.958, {
            "pe": {"xt": -13.49, "y": -10.74, "yt": -9.46, "qkv": -8.02, "ot": 16.49, "wo": 18.93, "xat": 26.77,
                   "gate": 27.79},
            "act": {"xt": -14.15, "yt": -9.76, "k": -8.37, "v": -6.56, "q": -5.59, "ot": 16.32, "xat": 25.01},
            "dve": {"stats": -22.97, "mv": -18.43, "var": -16.21, "xn": -14.06, "y": -8.06, "rz": 17.06, "o": 17.26,
                    "h": 22.42, "stats2": 23.3, "mv2": 23.59, "var2": 23.62, "l0": 25.72, "l1": 26.4, "xa": 26.86,
                    "lg": 29.43},
            "pool": {"rstd": -17.31, "rstd2": 24.49}}, {
            "pe": {"sc": -0.56, "pt": 3.37, "pv": 6.89},
            "act": {"p": 0.72, "pt": 4.17},
            "dve": {"mx": 2.1, "sub": 2.3, "pt": 5.82},
            "pool": {"kx": -5.31}}, (3,))
        f1 = moe_steps("f1", 4, 3, {
            "pe": [], "act": [("gexp",)],
            "dve": [(k,) for k in ("gmx", "gsub", "gsum", "grz", "prob", "b", "b2")],
            "pool": [("rstd", 0), ("rstd", 1)]}, "relu", False, {"pe": [("pt",), ("b2",)], "act": [("pt",)]},
            ("stats", "mv", "var", "xn", "g", "fin"))

        def overlapped(e, functions):
            for _, name, step, n in sorted(later[e]):
                functions[name](step, n)

        block = stack.enter_context(nc.Block())

        @block.sync
        def _(sp):
            sp.dma_start(X[:, :, :], x.rearrange("b t c -> t b c")).then_inc(ld_x, 16)
            sp.dma_start(CONST[:, :], consts).then_inc(ld_x, 16)
            sp.dma_start(WM[:, :], w_m).then_inc(ld_m, 16)
            sp.dma_start(DTW[:, :, :], dtw_t).then_inc(ld_m, 16)
            sp.dma_start(COL[:, :], cols).then_inc(ld_c, 16)
            sp.dma_start(POSI[:, :], pos).then_inc(ld_c, 16)
            sp.dma_start(ROW[:, :], rows.to_broadcast([128, rows.shape[1]])).then_inc(ld_c, 16)
            sp.dma_start(CTXT[:, :, :], ctx_t).then_inc(ld_ctx, 16)
            sp.dma_start(CTX[:, :, :], ctx.rearrange("b t c -> t b c")).then_inc(ld_ctx, 16)
            sp.dma_start(WX0[:, :], w_x0).then_inc(ld_ctx, 16)
            sp.dma_start(WA1[:, :], w_a1).then_inc(ld_w1, 16)
            sp.dma_start(B2[:, :], b2).then_inc(ld_w2, 16)
            sp.wait_ge(*mpe.at("out", 1))
            sp.dma_start(WF0[:, :], w_f0).then_inc(ld_f0, 16)
            sp.dma_start(WX1, w_x1).then_inc(ld_x1, 16)
            sp.dma_start(WF1[:, :], w_f1).then_inc(ld_w2, 16)
            for h in range(2):
                sp.wait_ge(*f1["dve"].at("fin", h))
                sp.dma_start(out[4 * h:4 * h + 4].rearrange("b t c -> t b c"), FIN[:, 4 * h:4 * h + 4, :]).then_inc(stored, 16)
            sp.wait_ge(stored, 32)

        @block.vector
        def _(dve):
            def stats_all(S, src, p, a, b_, c, half=None):
                bs, key = (range(B), ()) if half is None else (range(4 * half, 4 * half + 4), (half,))
                for b in bs:
                    i = dve.bn_stats(ST6[0:p, b, :], src[0:p, b, :])
                i.then_inc(*S.did(a, *key))
                dve.wait_ge(*S.at(a, *key))
                for b in bs:
                    i = dve.bn_aggr(MV[0:p, b, :], ST6[0:p, b, :])
                i.then_inc(*S.did(b_, *key))
                dve.wait_ge(*S.at(b_, *key))
                cols_ = slice(bs[0], bs[-1] + 1)
                dve.tensor_scalar(RS[0:p, cols_], MV[0:p, cols_, 1], EPS, None, ALU.add).then_inc(*S.did(c, *key))

            def norm_all(S, dst, src, p, step, half=None):
                bs, key = (range(B), ()) if half is None else (range(4 * half, 4 * half + 4), (half,))
                for b in bs:
                    i = dve.tensor_scalar(dst[0:p, b, :], src[0:p, b, :], MV[0:p, b, 0:1], RS[0:p, b:b + 1],
                                          ALU.subtract, ALU.mult)
                i.then_inc(*S.did(step, *key))

            dve.memset(ONES[:, :], 1.0)
            dve.memset(HALFNEG[:, :], -0.5)
            dve.memset(V0[:, :, :, HD0:HD0 + 1], 1.0)
            dve.memset(S3[0][96:128, :], 0.0)
            dve.memset(S3[1][96:128, :], 0.0).then_inc(*mdve.did("const"))
            dve.wait_ge(ld_x, 32)
            dve.tensor_copy(SEL[:, :], CONST[:, 156:156 + 2 * DS])
            stats_all(mdve, X, 128, "stats", "mv", "var")
            dve.wait_ge(*mpool.at("rstd"))
            norm_all(mdve, XN, X, 128, "xn")
            dve.wait_ge(ld_c, 48)
            posf, ang, k, rr = (SMALL[:, i, :, 0:4] for i in range(4))
            dve.tensor_copy(SMALL[:, 4, :, 0:1], POSI[:, :].unsqueeze(2)).then_inc(*mdve.did("rope0"))
            dve.wait_ge(*mdve.at("rope0"))
            dve.tensor_tensor(ang, SMALL[:, 4, :, 0:1].to_broadcast([T, B, 4]),
                              FREQ.unsqueeze(1).to_broadcast([T, B, 4]), ALU.mult).then_inc(*mdve.did("rope1"))
            dve.wait_ge(*mdve.at("rope1"))
            dve.tensor_scalar(k, ang, float(1 / (2 * np.pi)), MAGIC, ALU.mult, ALU.add).then_inc(*mdve.did("rope2"))
            dve.wait_ge(*mdve.at("rope2"))
            dve.tensor_scalar(k, k, -MAGIC, None, ALU.add).then_inc(*mdve.did("rope3"))
            for i, part in enumerate(TWO_PI):
                dve.wait_ge(*mdve.at(f"rope{3 + i}"))
                dve.scalar_tensor_tensor(ang, k, -part, ang, ALU.mult, ALU.add).then_inc(*mdve.did(f"rope{4 + i}"))
            dve.wait_ge(*mdve.at("rope6"))
            pi = float(np.float32(3.1415925))
            dve.tensor_scalar(ang, ang, pi, -pi, ALU.min, ALU.max).then_inc(*mdve.did("rope7"))
            dve.wait_ge(*mact.at("sin_abs"))
            dve.tensor_scalar(rr, rr, -1.0, float(np.pi / 2), ALU.mult, ALU.add).then_inc(*mdve.did("rope8"))
            dve.wait_ge(*mact.at("sin"))
            for g in range(2):
                dve.tensor_copy(ROPE[:, 0, :, g, :], SMALL[:, 5, :, 0:4])
            dve.tensor_scalar(ROPE[:, 1, :, 0, :], SMALL[:, 6, :, 0:4], -1.0, None, ALU.mult)
            dve.tensor_copy(ROPE[:, 1, :, 1, :], SMALL[:, 6, :, 0:4]).then_inc(*mdve.did("rope"))
            dve.wait_ge(*mact.at("nega"))
            na = NEGA[:, :, :, :].rearrange("p a b c -> p (a b c)")
            dve.tensor_scalar(na, na, -1.0, None, ALU.mult).then_inc(*mdve.did("nega"))
            for d in range(2):
                for c in range(NC):
                    i = dve.tensor_scalar(DIAG[:, d, c, :], IDN, DSK[d][:, c:c + 1], None, ALU.mult)
            i.then_inc(*mdve.did("diag"))
            dve.wait_ge(ld_ctx, 48)
            dve.wait_ge(*mdve.at("xn"))
            stats_all(mdve, CTX, M, "cstats", "cmv", "cvar")

            for d in range(2):
                pad = slice(0, DC - 1) if d == 0 else slice(T, T + DC - 1)
                dve.memset(XP[d][:, :, :, pad], 0.0).then_inc(*mdve.did("pad", d))
                dve.wait_ge(*mact.at("xp", d))
                dve.wait_ge(*mdve.at("pad", d))
                for kk in range(DC):
                    shift = kk if d == 0 else DC - 1 - kk
                    for c in range(NC):
                        src = XP[d][:, c, :, shift:shift + T]
                        dst = U[d][:, c, :].rearrange("p (b t) -> p b t", b=B)
                        if kk == 0:
                            i = dve.tensor_scalar(dst, src, CONVW[d][:, c, 0:1], CONVB[d][:, c:c + 1], ALU.mult, ALU.add)
                        else:
                            i = dve.scalar_tensor_tensor(dst, src, CONVW[d][:, c, kk:kk + 1], dst, ALU.mult, ALU.add)
                    i.then_inc(*mdve.did(("tap0", "tap1", "tap2", "conv")[kk], d))
                    dve.wait_ge(*mdve.at(("tap0", "tap1", "tap2", "conv")[kk], d))

            def parts(d):
                src, s3, res = bank(2, 2), S3[d], RES[d]
                dve.wait_ge(*mpe.at("dbc", d))
                dve.tensor_copy(s3[0:96, :], src[0:96, :]).then_inc(*mdve.did("s3a", d))
                dve.wait_ge(*mdve.at("s3a", d))
                dve.tensor_tensor(res[0:64, :], src[0:64, :], s3[0:64, :], ALU.subtract).then_inc(*mdve.did("s3b", d))
                dve.wait_ge(*mdve.at("s3b", d))
                dve.tensor_copy(s3[0:64, :], res[0:64, :]).then_inc(*mdve.did("s3c", d))
                dve.wait_ge(*mdve.at("s3c", d))
                dve.tensor_tensor(res[0:32, :], res[0:32, :], s3[0:32, :], ALU.subtract).then_inc(*mdve.did("s3d", d))
                dve.wait_ge(*mdve.at("s3d", d))
                dve.tensor_copy(s3[0:32, :], res[0:32, :]).then_inc(*mdve.did("s3", d))

            parts(0)
            dve.wait_ge(*mpool.at("crstd"))
            norm_all(mdve, CTX, CTX, M, "cn")
            dve.wait_ge(*mdve.at("cn"))
            dve.tensor_tensor(CTX[:, :, :], CTX[:, :, :], row_b("gm", M), ALU.mult).then_inc(*mdve.did("cg"))
            dve.wait_ge(*mdve.at("cg"))
            dve.tensor_tensor(CTX[:, :, :], CTX[:, :, :], row_b("bm", M), ALU.add).then_inc(*mdve.did("cb"))
            parts(1)
            for d in range(2):
                e_ = SPE[d].rearrange("p c n -> p (c n)")
                dve.wait_ge(*mact.at("exp", d))
                dve.tensor_scalar(SPT[d], e_, 1.0 / 3.0, -0.5, ALU.mult, ALU.add).then_inc(*mdve.did("poly0", d))
                dve.wait_ge(*mdve.at("poly0", d))
                dve.tensor_tensor(SPT[d], SPT[d], e_, ALU.mult).then_inc(*mdve.did("poly1", d))
                dve.wait_ge(*mdve.at("poly1", d))
                dve.scalar_tensor_tensor(SPT[d], SPT[d], 1.0, e_, ALU.add, ALU.mult).then_inc(*mdve.did("poly", d))
                dve.tensor_scalar(SMALLE[d], e_, 2.0 ** -6, None, ALU.is_lt).then_inc(*mdve.did("small", d))
                dve.wait_ge(*mact.at("ln", d))
                dve.wait_ge(*mdve.at("small", d))
                dve.copy_predicated(SPL[d].rearrange("p c n -> p (c n)"), SMALLE[d], SPT[d]).then_inc(*mdve.did("pick", d))
                dve.wait_ge(*mdve.at("pick", d))
                for c in range(NC):
                    i = dve.tensor_tensor(DELTA[d][:, c, :], SPR[d][:, c, :], SPL[d][:, c, :], ALU.add)
                    i.then_inc(*mdve.did("delta0" if c == 0 else "delta", d))
            dve.wait_ge(*mdve.at("delta", 1))
            for d in (1, 0):
                if d == 0:
                    dve.wait_ge(*mpe.at("y0", 0))
                for c in range(NC):
                    i = dve.tensor_tensor(DU[d][:, c, :], DELTA[d][:, c, :], U[d][:, c, :], ALU.mult)
                i.then_inc(*mdve.did("du", d))

            dav = DA.rearrange("p s c (b t) -> p (s c b) t", b=B)
            dve.memset(dav[:, :, 0:1], 0.0).then_inc(*mdve.did("edge", 0))
            for kx in ("bu0", "h0", "h1", "hc0"):
                dve.nop().then_inc(L[kx], CREDIT)
            for d in range(2):
                dve.wait_ge(*mdve.at("edge", d))
                order = slice(None) if d == 0 else slice(None, None, -1)
                with dve.Fori(0, DS // 4) as it:
                    for s in range(4):
                        n = it * 4 + (s + d * DS + CREDIT)
                        h0, h1 = HB[s][:, 0, :], HB[s][:, 1, :]
                        dve.wait_ge(L["b_sb"], n + 1)
                        dve.wait_ge(L["yacc"], n - 3)
                        dve.tensor_tensor(h0, DU[d][:, 0, :], BS[:, s % 2, :], ALU.mult).then_inc(L["bu0"], 1)
                        dve.wait_ge(L["bu1"], n + 1)
                        dve.wait_ge(L["da1"], n + 1)
                        dve.tensor_tensor_scan(h1[:, order], DA[:, s % 2, 1, order], h1[:, order], 0.0,
                                               ALU.mult, ALU.add).then_inc(L["h1"], 1)
                        dve.wait_ge(L["bu0"], n + 1)
                        dve.wait_ge(L["da0"], n + 1)
                        dve.tensor_tensor_scan(h0[:, order], DA[:, s % 2, 0, order], h0[:, order], 0.0,
                                               ALU.mult, ALU.add).then_inc(L["h0"], 1)
                        dve.wait_ge(L["c_sb"], n + 1)
                        dve.wait_ge(L["h0"], n + 1)
                        dve.tensor_tensor(h0, h0, CS[:, s % 2, :], ALU.mult).then_inc(L["hc0"], 1)
                if d == 0:
                    dve.wait_ge(L["h0"], CREDIT + DS)
                    dve.wait_ge(L["h1"], CREDIT + DS)
                    dve.memset(dav[:, :, T - 1:T], 0.0).then_inc(*mdve.did("edge", 1))
                    dve.tensor_tensor(X[:, :, :], X[:, :, :], row_b("ln_b"), ALU.add).then_inc(*mdve.did("xb"))
                dve.wait_ge(L["yacc"], CREDIT + (d + 1) * DS)
                for c in range(NC):
                    i = dve.tensor_tensor(ZS[:, d, c, :], bank(4 + 2 * c, 2), ZS[:, d, c, :], ALU.mult)
                i.then_inc(*mdve.did("y", d))

            for h in range(2):
                hs = slice(4 * h, 4 * h + 4)
                dve.wait_ge(*mpe.at("out", h))
                dve.tensor_tensor(XN[:, hs, :], XN[:, hs, :], bank(h).rearrange("p (b c) -> p b c", b=4), ALU.add)\
                   .then_inc(*mdve.did("h", h))
                dve.wait_ge(*mdve.at("h", h))
                stats_all(mdve, XN, 128, "hstats", "hmv", "hvar", h)
            for h in range(2):
                hs = slice(4 * h, 4 * h + 4)
                dve.wait_ge(*mpool.at("hrstd", h))
                norm_all(mdve, XN, XN, 128, "hn", h)
                dve.wait_ge(*mdve.at("hn", h))
                dve.tensor_tensor(XN[:, hs, :], XN[:, hs, :], row("ln_w").unsqueeze(1).to_broadcast([128, 4, D]),
                                  ALU.mult).then_inc(*mdve.did("hg", h))
                dve.wait_ge(*mdve.at("hg", h))
                dve.tensor_tensor(X[:, hs, :], X[:, hs, :], XN[:, hs, :], ALU.add).then_inc(*mdve.did("x", h))
            dve.wait_ge(*mdve.at("x", 1))

            def ln_step(S, W, step, b, v, src, before=None):
                if step == "stats":
                    if before is not None:
                        dve.wait_ge(*before.at("res", b))
                    dve.bn_stats(v["st"], src).then_inc(*S.did("stats", b))
                elif step == "mv":
                    dve.wait_ge(*S.at("stats", b))
                    dve.bn_aggr(v["mv"], v["st"]).then_inc(*S.did("mv", b))
                elif step == "var":
                    dve.wait_ge(*S.at("mv", b))
                    dve.tensor_scalar(v["var"], v["mv"][:, 1:2], EPS, None, ALU.add).then_inc(*S.did("var", b))
                elif step == "xn":
                    dve.wait_ge(*W.at("rstd", b))
                    dve.tensor_scalar(v["xn"], src, v["mv"][:, 0:1], v["rs"], ALU.subtract, ALU.mult)\
                       .then_inc(*S.did("xn", b))

            def ln2_step(S, W, step, b, v, src, before, dst=None, g=None, b_=None, last=None):
                if step == "stats2":
                    dve.wait_ge(*S.at(before, b))
                    dve.bn_stats(v["st2"], src).then_inc(*S.did("stats2", b))
                elif step == "mv2":
                    dve.wait_ge(*S.at("stats2", b))
                    dve.bn_aggr(v["mv2"], v["st2"]).then_inc(*S.did("mv2", b))
                elif step == "var2":
                    dve.wait_ge(*S.at("mv2", b))
                    dve.tensor_scalar(v["var2"], v["mv2"][:, 1:2], EPS, None, ALU.add).then_inc(*S.did("var2", b))
                elif step == "xn2":
                    dve.wait_ge(*W.at("rstd2", b))
                    dve.tensor_scalar(v["xn2"], src, v["mv2"][:, 0:1], v["rs2"], ALU.subtract, ALU.mult)\
                       .then_inc(*S.did("xn2", b))
                elif step == "l0":
                    dve.wait_ge(*W.at("rstd2", b))
                    dve.tensor_scalar(v["l1"], src, v["mv2"][:, 0:1], v["rs2"], ALU.subtract, ALU.mult)\
                       .then_inc(*S.did("l0", b))
                elif step == "l1":
                    dve.wait_ge(*S.at("l0", b))
                    dve.tensor_tensor(v["l1"], v["l1"], row(g), ALU.mult).then_inc(*S.did("l1", b))
                elif step == last:
                    dve.wait_ge(*S.at("l1", b))
                    dve.tensor_tensor(dst, v["l1"], row(b_), ALU.add).then_inc(*S.did(last, b))

            def softmax_step(S, P, A, step, k, w, ps, scores):
                heads, keys = ps.shape[1:]
                if step == "mx":
                    dve.wait_ge(*P.at(scores, k))
                    dve.tensor_reduce(w["mx"], ps, AX, ALU.max).then_inc(*S.did("mx", k))
                elif step == "sub":
                    dve.wait_ge(*S.at("mx", k))
                    after(dve, P, "pt", k - 3)
                    dve.tensor_tensor(w["p"] if len(w["p"].shape) == 3 else w["p"].rearrange("p (h m) -> p h m", h=heads),
                                      ps, w["mx"].unsqueeze(2).to_broadcast([128, heads, keys]), ALU.subtract)\
                       .then_inc(*S.did("sub", k))

            def narrow_heads(L_, step, n, v, w, keys):
                S, P = L_["dve"], L_["pe"]
                if step in ("mx", "sub"):
                    ps = PS[:, n % 3, 0:4 * keys].rearrange("p (h m) -> p h m", h=4)
                    softmax_step(S, P, L_["act"], step, n, w, ps, "sc")
                elif step == "pt":
                    dve.wait_ge(*P.at("pt", n))
                    after(dve, P, "pv", n - 3)
                    dve.tensor_copy(w["pt"][0:keys, :], bank(3 + n % 2)[0:keys, :]).then_inc(*S.did("pt", n))
                else:
                    o = bank(5 + n % 2)[:, 0:H0 * (HD0 + 1)].rearrange("p (h d) -> p h d", h=H0)
                    if step == "rz":
                        dve.wait_ge(*P.at("pv", 4 * n + 3))
                        dve.reciprocal(v["rz"].unsqueeze(2), o[:, :, HD0:HD0 + 1]).then_inc(*S.did("rz", n))
                    elif step == "o":
                        dve.wait_ge(*S.at("rz", n))
                        dve.tensor_tensor(v["o"].rearrange("p (h d) -> p h d", h=H0), o[:, :, 0:HD0],
                                          v["rz"].unsqueeze(2).to_broadcast([128, H0, HD0]), ALU.mult)\
                           .then_inc(*S.did("o", n))

            S, P = x0["dve"], x0["pe"]
            lg, top = SMALL[:, 0, :, :], SMALL[:, 1, :, :]
            for step, n in S.order:
                v, w = X0S[n % 4], X0U[n % 3]
                if step in ("stats", "mv", "var", "xn"):
                    ln_step(S, x0["pool"], step, n, v, X[:, n, :])
                elif step == "rope_a":
                    q_ps = PS[:, 7, 0:D].rearrange("p (h g d) -> p h g d", h=H0, g=2)
                    r1 = v["r1"].rearrange("p (h g d) -> p h g d", h=H0, g=2)
                    r2 = v["r2"].rearrange("p (h g d) -> p h g d", h=H0, g=2)
                    dve.wait_ge(*P.at("q", n))
                    for g in range(2):
                        cos = ROPE[:, 0, n, g, :].unsqueeze(1).to_broadcast([T, H0, 4])
                        sin = ROPE[:, 1, n, g, :].unsqueeze(1).to_broadcast([T, H0, 4])
                        dve.tensor_tensor(r1[:, :, g, :], q_ps[:, :, g, :], cos, ALU.mult)
                        ins = dve.tensor_tensor(r2[:, :, g, :], q_ps[:, :, 1 - g, :], sin, ALU.mult)
                    ins.then_inc(*S.did("rope_a", n))
                elif step == "rope":
                    dve.wait_ge(*S.at("rope_a", n))
                    dve.tensor_tensor(v["qr"], v["r1"], v["r2"], ALU.add).then_inc(*S.did("rope", n))
                elif step == "res":
                    dve.wait_ge(*P.at("wo", n))
                    dve.tensor_tensor(X[:, n, :], X[:, n, :], PS[:, 5 + n % 2, 384:512], ALU.add)\
                       .then_inc(*S.did("res", n))
                elif step in ("stats2", "mv2", "var2", "xn2"):
                    ln2_step(S, x0["pool"], step, n, v, X[:, n, :], "res")
                elif step == "lg":
                    dve.wait_ge(*P.at("gate", n))
                    dve.tensor_copy(lg[:, n, :], PS[:, 5 + n % 2, 0:E0]).then_inc(*S.did("lg", n))
                elif step == "max":
                    dve.wait_ge(*S.at("lg", n))
                    dve.max(top[:, n, :], lg[:, n, :]).then_inc(*S.did("max", n))
                elif step == "index":
                    dve.wait_ge(*S.at("max", n))
                    dve.max_index(TOPI[:, n, :], top[:, n, :], lg[:, n, :]).then_inc(*S.did("index", n))
                else:
                    narrow_heads(x0, step, n, v, w, M)
            dve.wait_ge(*S.at("index", B - 1))

            S, P = f0["dve"], f0["pe"]
            ti = SMALL[:, 2, :, :]
            dve.tensor_copy(ti, TOPI[:, :, :]).then_inc(*S.did("top_i"))
            w = SMALL[:, 3, :, :]
            dve.tensor_tensor(w[:, :, 0:1], top[:, :, 1:2], top[:, :, 0:1], ALU.subtract).then_inc(*S.did("dif"))
            dve.wait_ge(*f0["act"].at("top_exp"))
            dve.tensor_scalar(w[:, :, 2:3], w[:, :, 1:2], 1.0, None, ALU.add).then_inc(*S.did("den"))
            dve.wait_ge(*S.at("den"))
            dve.reciprocal(w[:, :, 3:4], w[:, :, 2:3]).then_inc(*S.did("w1"))
            dve.wait_ge(*S.at("w1"))
            dve.tensor_tensor(w[:, :, 4:5], w[:, :, 1:2], w[:, :, 3:4], ALU.mult).then_inc(*S.did("w2"))
            iota = IOTA.unsqueeze(1).to_broadcast([T, B, E0])
            for j, (step, stepw) in enumerate((("s1", "s1w"), ("s2", "s2w"))):
                dve.tensor_tensor(SMALL[:, 4 + j, :, :], iota, ti[:, :, j:j + 1].to_broadcast([T, B, E0]),
                                  ALU.is_equal).then_inc(*S.did(step))
            for j, (step, stepw) in enumerate((("s1", "s1w"), ("s2", "s2w"))):
                dve.wait_ge(*S.at("s2"))
                dve.tensor_tensor(SMALL[:, 4 + j, :, :], SMALL[:, 4 + j, :, :],
                                  w[:, :, 3 + j:4 + j].to_broadcast([T, B, E0]), ALU.mult).then_inc(*S.did(stepw))
            dve.wait_ge(*S.at("s2w"))
            dve.tensor_tensor(PROB, SMALL[:, 4, :, :], SMALL[:, 5, :, :], ALU.add).then_inc(*S.did("comb"))

            def moe_units(F, n, gated, last_step, finish=None):
                S, P = F["dve"], F["pe"]

                def acc(h, e):
                    dve.wait_ge(*P.at("y", h, e))
                    if (h, e) != (0, 0):
                        dve.wait_ge(*S.at("acc", *divmod(h * E0 + e - 1, E0)))
                    for j in range(4):
                        b = 4 * h + j
                        ins = dve.scalar_tensor_tensor(last_step[:, b, :], PS[:, 6 + e % 2, j * D:(j + 1) * D],
                                                       PROB[:, b, e:e + 1], last_step[:, b, :], ALU.mult, ALU.add)
                    ins.then_inc(*S.did("acc", h, e))

                prev = None
                for k_, (h, e, c) in enumerate(units(n)):
                    if gated:
                        if k_ >= 3:
                            ub = units(n)[k_ - 3]
                            dve.wait_ge(*P.at("y" if ub[2] == n - 1 else "yp", *(ub[:2] if ub[2] == n - 1 else ub)))
                        dve.wait_ge(*F["act"].at("silu", h, e, c))
                        dve.tensor_tensor(ACTB[:, k_ % 3, :], ACTS[:, k_ % 3, :], bank(2 * (k_ % 3) + 1), ALU.mult)\
                           .then_inc(*S.did("act", h, e, c))
                    if c == n - 1:
                        if prev is not None:
                            acc(*prev)
                            if finish and prev[1] == E0 - 1:
                                finish(0)
                        prev = (h, e)
                acc(*prev)

            dve.wait_ge(*S.at("comb"))
            moe_units(f0, 2, True, X)
            dve.wait_ge(*S.at("acc", 1, E0 - 1))

            bound = {p: float(np.log(p / (1 - p))) for p in (0.95, 0.85, 0.1, 0.25)}
            def a1_step(step, b):
                S, P, A = a1["dve"], a1["pe"], a1["act"]
                v = A1S[b % 6]
                if step in ("stats", "mv", "var", "xn"):
                    ln_step(S, a1["pool"], step, b, v, X[:, b, :])
                elif step == "a":
                    dve.wait_ge(*P.at("s", b))
                    dve.tensor_scalar(v["a"], PS[:, b % 6, 0:T], float(HD0 ** -0.5), None, ALU.mult).then_inc(*S.did("a", b))
                elif step == "g1":
                    dve.wait_ge(*S.at("a", b))
                    dve.tensor_scalar(v["r1"], v["a"], bound[0.95], None, ALU.is_gt).then_inc(*S.did("g1", b))
                elif step == "l1":
                    dve.wait_ge(*S.at("a", b))
                    dve.tensor_scalar(v["r2"], v["a"], bound[0.1], 2.0 / 7.0, ALU.is_lt, ALU.mult).then_inc(*S.did("l1", b))
                elif step == "g":
                    dve.wait_ge(*S.at("g1", b))
                    dve.scalar_tensor_tensor(v["r1"], v["a"], bound[0.85], v["r1"], ALU.is_gt, ALU.add)\
                       .then_inc(*S.did("g", b))
                elif step == "l":
                    dve.wait_ge(*S.at("l1", b))
                    dve.scalar_tensor_tensor(v["r2"], v["a"], bound[0.25], v["r2"], ALU.is_lt, ALU.add)\
                       .then_inc(*S.did("l", b))
                elif step == "ls":
                    dve.wait_ge(*S.at("l", b))
                    dve.tensor_scalar(v["r2"], v["r2"], -0.7, 1.0, ALU.mult, ALU.add).then_inc(*S.did("ls", b))
                elif step == "m":
                    dve.wait_ge(*S.at("g", b))
                    dve.wait_ge(*S.at("ls", b))
                    dve.scalar_tensor_tensor(v["r1"], v["r1"], 0.5, v["r2"], ALU.mult, ALU.add).then_inc(*S.did("m", b))
                elif step == "am":
                    dve.wait_ge(*S.at("m", b))
                    dve.tensor_tensor(v["a"], v["a"], v["r1"], ALU.mult).then_inc(*S.did("am", b))
                elif step == "mx":
                    dve.wait_ge(*S.at("am", b))
                    dve.tensor_reduce(v["mx"], v["a"], AX, ALU.max).then_inc(*S.did("mx", b))
                elif step == "nmx":
                    dve.wait_ge(*S.at("mx", b))
                    dve.tensor_scalar(v["mx"], v["mx"], -1.0, None, ALU.mult).then_inc(*S.did("nmx", b))
                elif step == "rz":
                    dve.wait_ge(*A.at("p", b))
                    dve.reciprocal(v["rz"], v["z"]).then_inc(*S.did("rz", b))
                elif step == "y":
                    dve.wait_ge(*P.at("out", b))
                    dve.wait_ge(*S.at("rz", b))
                    dve.scalar_tensor_tensor(v["y"], PS[:, b % 6, 0:D], v["rz"], X[:, b, :], ALU.mult, ALU.add)\
                       .then_inc(*S.did("y", b))
                elif step == "res":
                    dve.wait_ge(*S.at("y", b))
                    dve.tensor_tensor(X[:, b, :], v["y"], row("a1_bproj"), ALU.add).then_inc(*S.did("res", b))

            def x1_step(step, n):
                S, P, A = x1["dve"], x1["pe"], x1["act"]
                v, w = X1S[n % 2], X1U[n % 3]
                if step in ("stats", "mv", "var", "xn"):
                    ln_step(S, x1["pool"], step, n, v, X[:, n, :], a1["dve"])
                elif step in ("stats2", "mv2", "var2", "l0", "l1", "l2"):
                    ln2_step(S, x1["pool"], step, n, v, v["xn"], "xn", v["l2"], "gl", "bl", "l2")
                elif step in ("va", "vb"):
                    p, bk = (M, 7) if step == "va" else (T, 6)
                    dve.wait_ge(*P.at(step, n))
                    after(dve, P, "o", 4 * (n - 2) + 3)
                    dve.tensor_copy(v[step][0:p, :, 0:HD1], bank(bk)[0:p, :].rearrange("p (h d) -> p h d", h=H1))\
                       .then_inc(*S.did(step, n))
                elif step in ("mx", "sub"):
                    ps = PS[:, n % 2, 0:2 * J1].rearrange("p (h m) -> p h m", h=2)
                    softmax_step(S, P, A, step, n, w, ps, "s")
                elif step in ("rz0", "o0", "rz1", "o1"):
                    g = int(step[-1])
                    o = PS[:, 4 + g, 0:4 * (HD1 + 1)].rearrange("p (h d) -> p h d", h=4)
                    rz = v["rz"][:, 4 * g:4 * g + 4].unsqueeze(2)
                    if step[0] == "r":
                        dve.wait_ge(*P.at("o", 4 * n + 2 * g + 1))
                        dve.reciprocal(rz, o[:, :, HD1:HD1 + 1]).then_inc(*S.did(step, n))
                    else:
                        dve.wait_ge(*S.at(f"rz{g}", n))
                        after(dve, P, "ot", n - 2)
                        dve.tensor_tensor(v["o"][:, 256 * g:256 * g + 256].rearrange("p (h d) -> p h d", h=4),
                                          o[:, :, 0:HD1], rz.to_broadcast([128, 4, HD1]), ALU.mult)\
                           .then_inc(*S.did(step, n))
                elif step == "res":
                    dve.wait_ge(*P.at("out", n))
                    dve.tensor_tensor(X[:, n, :], X[:, n, :], PS[:, 5, 0:D], ALU.add).then_inc(*S.did("res", n))

            def g1_step(step, n):
                S, P, A = g1["dve"], g1["pe"], g1["act"]
                if (step, n) == ("stats", 0):
                    for v in G1S:
                        dve.memset(v["xp"][:, 0:1], 0.0)
                        dve.memset(v["xp"][:, T + 1:T + 2], 0.0)
                        ins = dve.memset(v["v"][:, :, HD0:HD0 + 1], 1.0)
                    ins.then_inc(ones, 1)
                v, w = G1S[n % 4], G1U[n % 3]
                if step in ("stats", "mv", "var", "xn"):
                    ln_step(S, g1["pool"], step, n, v, X[:, n, :], x1["dve"])
                elif step == "y":
                    dve.wait_ge(*P.at("y", n))
                    dve.tensor_copy(v["y"], PS[:, 7, 0:D]).then_inc(*S.did("y", n))
                elif step == "h":
                    dve.wait_ge(*P.at("wo", n))
                    dve.tensor_tensor(v["y"], v["y"], PS[:, 5 + n % 2, 384:512], ALU.add).then_inc(*S.did("h", n))
                elif step in ("stats2", "mv2", "var2", "l0", "l1", "xa"):
                    ln2_step(S, g1["pool"], step, n, v, v["y"], "h", XN1[:, n, :], "ln1_g", "ln1_b", "xa")
                elif step == "lg":
                    dve.wait_ge(*P.at("gate", n))
                    dve.tensor_copy(SMALL[:, 0, n, :], PS[:, 5 + n % 2, 0:E1]).then_inc(*S.did("lg", n))
                else:
                    narrow_heads(g1, step, n, v, w, T)
            for v in X1S:
                dve.memset(v["va"][:, :, HD1:HD1 + 1], 1.0)
                ins = dve.memset(v["vb"][:, :, HD1:HD1 + 1], 1.0)
            ins.then_inc(ones, 1)
            overlapped("dve", {"a1": a1_step, "x1": x1_step, "g1": g1_step})
            dve.wait_ge(*g1["dve"].at("lg", B - 1))

            F = f1
            S, P = F["dve"], F["pe"]
            lg = SMALL[:, 0, :, :]
            dve.tensor_reduce(SMALL[:, 1, :, 0], lg, AX, ALU.max).then_inc(*S.did("gmx"))
            dve.wait_ge(*S.at("gmx"))
            dve.tensor_tensor(lg, lg, SMALL[:, 1, :, 0:1].to_broadcast([T, B, E1]), ALU.subtract).then_inc(*S.did("gsub"))
            dve.wait_ge(*F["act"].at("gexp"))
            dve.tensor_reduce(SMALL[:, 1, :, 1], lg, AX, ALU.add).then_inc(*S.did("gsum"))
            dve.wait_ge(*S.at("gsum"))
            dve.reciprocal(SMALL[:, 1, :, 2], SMALL[:, 1, :, 1]).then_inc(*S.did("grz"))
            dve.wait_ge(*S.at("grz"))
            dve.tensor_tensor(PROB, lg, SMALL[:, 1, :, 2:3].to_broadcast([T, B, E1]), ALU.mult).then_inc(*S.did("prob"))
            dve.tensor_tensor(X[:, :, :], X[:, :, :], row_b("ln2_b"), ALU.add).then_inc(*S.did("b"))
            dve.wait_ge(*P.at("b2"))
            dve.tensor_tensor(XA.rearrange("p b c -> p (b c)"), XN1.rearrange("p b c -> p (b c)"), bank(4, 2), ALU.add)\
               .then_inc(*S.did("b2"))
            dve.wait_ge(*S.at("b2"))

            def finish(h):
                dve.wait_ge(*S.at("acc", h, E0 - 1))
                stats_all(S, XA, 128, "stats", "mv", "var", h)
                dve.wait_ge(*F["pool"].at("rstd", h))
                norm_all(S, XA, XA, 128, "xn", h)
                xa, x_ = (t[:, 4 * h:4 * h + 4, :] for t in (XA, X))
                dve.wait_ge(*S.at("xn", h))
                dve.tensor_tensor(xa, xa, row("ln2_g").unsqueeze(1).to_broadcast([T, 4, D]), ALU.mult)\
                   .then_inc(*S.did("g", h))
                dve.wait_ge(*S.at("g", h))
                dve.tensor_tensor(FIN[:, 4 * h:4 * h + 4, :], xa, x_, ALU.add).then_inc(*S.did("fin", h))

            moe_units(f1, 4, False, XA, finish)
            finish(1)

        @block.gpsimd
        def _(pool):
            def rsqrt_all(S, wait, p, step, cols_=slice(0, B), *key):
                pool.wait_ge(*wait)
                pool.tensor_tensor(RS[0:p, cols_], RS[0:p, cols_], HALFNEG[0:p, cols_], ALU.pow).then_inc(*S.did(step, *key))

            rsqrt_all(mpool, mdve.at("var"), 128, "rstd")
            rsqrt_all(mpool, mdve.at("cvar"), M, "crstd")
            for k in ("bu1", "hc1"):
                pool.nop().then_inc(L[k], CREDIT)
            for d in range(2):
                base = d * DS + CREDIT

                def inputs_b(s, n):
                    pool.wait_ge(L["b_sb"], n + 1)
                    pool.wait_ge(L["yacc"], n - 3)
                    pool.tensor_tensor(HB[s % 4][:, 1, :], DU[d][:, 1, :], BS[:, s % 2, :], ALU.mult).then_inc(L["bu1"], 1)

                def states_c(s, n):
                    pool.wait_ge(L["c_sb"], n + 1)
                    pool.wait_ge(L["h1"], n + 1)
                    pool.tensor_tensor(HB[s][:, 1, :], HB[s][:, 1, :], CS[:, s % 2, :], ALU.mult).then_inc(L["hc1"], 1)

                pool.wait_ge(*mdve.at("du", d))
                inputs_b(0, base)
                with pool.Fori(0, DS // 4 - 1) as it:
                    for s in range(4):
                        inputs_b(s + 1, it * 4 + (s + 1 + base))
                        states_c(s, it * 4 + (s + base))
                for s in range(4):
                    if s < 3:
                        inputs_b(s + 1, base + DS - 4 + s + 1)
                    states_c(s, base + DS - 4 + s)
            for h in range(2):
                rsqrt_all(mpool, mdve.at("hvar", h), 128, "hrstd", slice(4 * h, 4 * h + 4), h)

            def layer(L_, slots_, groups=None, keys=None, keys_src=None):
                S, DV = L_["pool"], L_["dve"]

                def take(step, n):
                    v = slots_[n % len(slots_)]
                    if step == "rstd":
                        pool.wait_ge(*DV.at("var", n))
                        pool.tensor_tensor(v["rs"], v["var"], HALFNEG[:, 0:1], ALU.pow).then_inc(*S.did("rstd", n))
                    elif step == "rstd2":
                        pool.wait_ge(*DV.at("var2", n))
                        pool.tensor_tensor(v["rs2"], v["var2"], HALFNEG[:, 0:1], ALU.pow).then_inc(*S.did("rstd2", n))
                    elif step == "kx":
                        b, g = divmod(n, 4)
                        if keys == T and g == 0:
                            pool.wait_ge(*L_["act"].at("k", b))
                        after(pool, L_["pe"], "sc", n - 3)
                        pool.tensor_tensor(groups[n % 3]["kx"], keys_src(b).unsqueeze(1).to_broadcast([128, 4, keys]),
                                           MASK[:, 4 * g:4 * g + 4].unsqueeze(2).to_broadcast([128, 4, keys]), ALU.mult)\
                            .then_inc(*S.did("kx", n))
                return take

            x0_step = layer(x0, X0S, X0U, M, lambda b: KT0[:, b, :])
            for step, n in x0["pool"].order:
                x0_step(step, n)
            overlapped("pool", {"a1": layer(a1, A1S), "x1": layer(x1, X1S),
                                "g1": layer(g1, G1S, G1U, T, lambda b: G1S[b % 4]["kt"])})
            S = f1["pool"]
            for h in range(2):
                rsqrt_all(S, f1["dve"].at("var", h), 128, "rstd", slice(4 * h, 4 * h + 4), h)

        @block.scalar
        def _(act):
            act.wait_ge(ld_c, 48)
            act.activation(NEGA[:, :, :, :].rearrange("p a b c -> p (a b c)"), ALOG, ACT.Exp)\
               .then_inc(*mact.did("nega"))
            act.wait_ge(*mpe.at("xnt"))
            act.activation(XNT[:, :, :].rearrange("p b t -> p (b t)"), bank(6, 2), ACT.Copy).then_inc(*mact.did("xnt"))
            act.wait_ge(*mdve.at("rope7"))
            act.activation(SMALL[:, 3, :, 0:4], SMALL[:, 1, :, 0:4], ACT.Abs).then_inc(*mact.did("sin_abs"))
            act.activation(SMALL[:, 6, :, 0:4], SMALL[:, 1, :, 0:4], ACT.Sin)
            act.wait_ge(*mdve.at("rope8"))
            act.activation(SMALL[:, 5, :, 0:4], SMALL[:, 3, :, 0:4], ACT.Sin).then_inc(*mact.did("sin"))
            for k in ("b_sb", "c_sb", "da0", "da1"):
                act.nop().then_inc(L[k], CREDIT)
            for d in range(2):
                off = DC - 1 if d == 0 else 0
                for c in range(NC):
                    act.wait_ge(*mpe.at(f"xz{c}", d))
                    i = act.activation(XP[d][:, c, :, off:off + T], bank(2 * c, 2).rearrange("p (b t) -> p b t", b=B),
                                       ACT.Copy)
                i.then_inc(*mact.did("xp", d))
                for c in range(NC):
                    act.wait_ge(*mpe.at(f"xz{2 + c}", d))
                    i = act.activation(ZS[:, d, c, :], bank(4 + 2 * c, 2), ACT.Silu)
                i.then_inc(*mact.did("zs", d))
            act.wait_ge(*mpe.at("kt0"))
            for g in range(2):
                i = act.activation(KT0[:, 4 * g:4 * g + 4, :].rearrange("p b m -> p (b m)"), bank(g)[:, 0:4 * M],
                                   ACT.Identity, bias=X0BK)
            i.then_inc(*mact.did("kt0"))
            act.wait_ge(*mpe.at("v0"))
            for g in range(2):
                i = act.activation(V0[:, 4 * g:4 * g + 4, :, 0:HD0].rearrange("p b h d -> p (b h) d"),
                                   bank(2 + g)[0:M, :].rearrange("p (h d) -> p h d", d=HD0), ACT.Copy)
            i.then_inc(*mact.did("v0"))
            for d in range(2):
                act.wait_ge(*mdve.at("conv", d))
                for c in range(NC):
                    i = act.activation(U[d][:, c, :], U[d][:, c, :], ACT.Silu)
                i.then_inc(*mact.did("u", d))
            for d in range(2):
                act.wait_ge(*mpe.at("dbc", d))
                act.activation(DTS[d][0:DR, :], bank(0, 2)[0:DR, :], ACT.Copy).then_inc(*mact.did("dts", d))
                for c in range(NC):
                    act.wait_ge(*mpe.at(f"dt{c}", d))
                    act.activation(SPR[d][:, c, :], bank(4 + 2 * c, 2), ACT.Relu, bias=DTB[d][:, c:c + 1])\
                       .then_inc(*mact.did(f"relu{c}", d))
                    act.activation(SPE[d][:, c, :], bank(4 + 2 * c, 2), ACT.Abs, bias=DTB[d][:, c:c + 1])\
                       .then_inc(*mact.did(f"abs{c}", d))
                act.wait_ge(*mact.at("abs1", d))
                for c in range(NC):
                    i = act.activation(SPE[d][:, c, :], SPE[d][:, c, :], ACT.Exp, scale=-1.0)
                i.then_inc(*mact.did("exp", d))
            act.wait_ge(*mpe.at("ct"))
            act.activation(KVT[:, :, 0:M], bank(0, 2).rearrange("p (b t) -> p b t", b=B)[:, :, 0:M], ACT.Copy)\
               .then_inc(*mact.did("ct"))
            for d in range(2):
                act.wait_ge(*mact.at("exp", d))
                act.wait_ge(*mdve.at("s3", d))
                for c in range(NC):
                    i = act.activation(SPL[d][:, c, :], SPE[d][:, c, :], ACT.Ln, bias=ONES[:, 0:1])
                i.then_inc(*mact.did("ln", d))
            for d in range(2):
                act.wait_ge(*mdve.at("edge", d))
                cols_ = slice(1, T) if d == 0 else slice(0, T - 1)
                with act.Fori(0, DS // 4) as it:
                    for s in range(4):
                        n = it * 4 + (s + d * DS + CREDIT)
                        act.wait_ge(L["b_ps"], it * 4 + (s + d * DS + 1))
                        act.wait_ge(L["bu0"], n - 1)
                        act.wait_ge(L["bu1"], n - 1)
                        act.activation(BS[:, s % 2, :], bank(0, 2), ACT.Copy).then_inc(L["b_sb"], 1)
                        for c in (1, 0):
                            act.wait_ge(L[f"h{c}"], n - 1)
                            act.activation(DA[:, s % 2, c, :].rearrange("p (b t) -> p b t", b=B)[:, :, cols_],
                                           DELTA[d][:, c, :].rearrange("p (b t) -> p b t", b=B)[:, :, cols_], ACT.Exp,
                                           scale=NEGA[:, d, c, bass.ds(it * 4 + s, 1)]).then_inc(L[f"da{c}"], 1)
                        act.wait_ge(L["c_ps"], it * 4 + (s + d * DS + 1))
                        act.wait_ge(L["hc0"], n - 1)
                        act.wait_ge(L["hc1"], n - 1)
                        act.activation(CS[:, s % 2, :], bank(2, 2), ACT.Copy).then_inc(L["c_sb"], 1)

            def copy(L_, step, n, dst, src, func=ACT.Copy, wait=None, **k):
                act.wait_ge(*L_["pe"].at(wait or step, n))
                act.activation(dst, src, func, **k).then_inc(*L_["act"].did(step, n))

            def exp(L_, k, p, scale):
                act.wait_ge(*L_["dve"].at("sub", k))
                act.activation(p, p, ACT.Exp, scale=scale).then_inc(*L_["act"].did("p", k))

            act.wait_ge(*mdve.at("x", 1))
            for step, n in x0["act"].order:
                v, w = X0S[n % 4], X0U[n % 3]
                if step == "p":
                    exp(x0, n, w["p"], float(1 / np.sqrt(HD0)))
                elif step == "pt":
                    after(act, x0["pe"], "pv", n - 3)
                    copy(x0, step, n, w["pt"][0:M, :], bank(3 + n % 2)[0:M, :])
                elif step == "ot":
                    copy(x0, step, n, v["ot"], PS[:, 5 + n % 2, 256:384])
                elif step == "xt2":
                    copy(x0, step, n, XNT[:, n, :], PS[:, 5 + n % 2, 0:T])
                else:
                    copy(x0, step, n, v[step], PS[:, 7, 0:T])
            S, P = f0["act"], f0["pe"]
            act.wait_ge(*f0["dve"].at("dif"))
            act.activation(SMALL[:, 3, :, 1:2], SMALL[:, 3, :, 0:1], ACT.Exp).then_inc(*S.did("top_exp"))
            for k, u in enumerate(units(2)):
                act.wait_ge(*P.at("hg", *u))
                if k >= 3:
                    act.wait_ge(*f0["dve"].at("act", *units(2)[k - 3]))
                act.activation(ACTS[:, k % 3, :], bank(2 * (k % 3)), ACT.Silu).then_inc(*S.did("silu", *u))
            def a1_step(step, b):
                v = A1S[b % 6]
                if step == "xt":
                    copy(a1, step, b, v["xt"], PS[:, b % 6, 0:T])
                elif step in ("q", "k"):
                    i = "qk".index(step)
                    copy(a1, step, b, v[step + "t"], PS[:, b % 6, i * T:(i + 1) * T], ACT.Identity, "qkv", bias=A1B[:, i:i + 1])
                elif step == "v":
                    copy(a1, step, b, v["v"], PS[:, b % 6, 2 * D:3 * D], wait="qkv")
                elif step == "p":
                    act.wait_ge(*a1["dve"].at("nmx", b))
                    act.activation(v["p"], v["a"], ACT.Exp, bias=v["mx"], accum_out=v["z"]).then_inc(*a1["act"].did("p", b))
                elif step == "pt":
                    copy(a1, step, b, v["pt"], PS[:, b % 6, 0:T])
                elif step == "o":
                    copy(a1, step, b, v["ot"], PS[:, b % 6, 0:T])
            def x1_step(step, n):
                v, w = X1S[n % 2], X1U[n % 3]
                if step == "lt":
                    copy(x1, step, n, KVT[:, n, M:J1], PS[:, 6, 0:T])
                elif step == "q":
                    after(act, x1["pe"], "s", 4 * (n - 2) + 3)
                    copy(x1, step, n, v["qt"].rearrange("p c t -> p (c t)"), bank(6))
                elif step in ("k0", "k1"):
                    g = int(step[-1])
                    after(act, x1["pe"], "s", 4 * (n - 2) + 3)
                    copy(x1, step, n, v["kt"][:, 2 * g:2 * g + 2, :].rearrange("p c j -> p (c j)"), bank(7 - g)[:, 0:2 * J1])
                elif step == "p":
                    exp(x1, n, w["p"].rearrange("p h j -> p (h j)"), float(HD1 ** 0.5))
                elif step == "pt":
                    act.wait_ge(*x1["pe"].at("pt", n))
                    after(act, x1["pe"], "o", n - 3)
                    act.activation(w["pta"].rearrange("p h t -> p (h t)")[0:M, :], bank(2 + n % 2)[0:M, 0:2 * T], ACT.Copy)
                    copy(x1, step, n, w["ptb"].rearrange("p h t -> p (h t)"), bank(2 + n % 2)[:, 2 * T:4 * T])
                elif step == "ot":
                    after(act, x1["pe"], "out", n - 2)
                    copy(x1, step, n, v["ot"].rearrange("p c t -> p (c t)"), bank(5))
            def g1_step(step, n):
                v, w = G1S[n % 4], G1U[n % 3]
                if step == "xt":
                    copy(g1, step, n, v["xp"][:, 1:T + 1], PS[:, 7, 0:T])
                elif step == "yt":
                    copy(g1, step, n, v["yt"], PS[:, 7, 0:T])
                elif step in ("q", "k"):
                    i = "qk".index(step)
                    copy(g1, step, n, v[step + "t"], PS[:, 7, i * T:(i + 1) * T], ACT.Identity, "qkv", bias=F1B[:, i:i + 1])
                elif step == "v":
                    copy(g1, step, n, v["v"][:, :, 0:HD0], PS[:, 7, 2 * D:3 * D].rearrange("p (h d) -> p h d", h=H0), wait="qkv")
                elif step == "p":
                    exp(g1, n, w["p"], float(1 / np.sqrt(HD0)))
                elif step == "pt":
                    after(act, g1["pe"], "pv", n - 3)
                    copy(g1, step, n, w["pt"], bank(3 + n % 2))
                elif step == "ot":
                    copy(g1, step, n, v["ot"], PS[:, 5 + n % 2, 256:384])
                elif step == "xat":
                    copy(g1, step, n, XAT1[:, n, :], PS[:, 5 + n % 2, 0:T])
            overlapped("act", {"a1": a1_step, "x1": x1_step, "g1": g1_step})
            S, P = f1["act"], f1["pe"]
            act.wait_ge(*f1["dve"].at("gsub"))
            act.activation(SMALL[:, 0, :, :], SMALL[:, 0, :, :], ACT.Exp).then_inc(*S.did("gexp"))
            for k, (h, e, c) in enumerate(units(4)):
                if k == 3:
                    act.wait_ge(*P.at("pt"))
                    act.activation(PROBT[0:E1, :, :].rearrange("p b t -> p (b t)"), bank(4, 2)[0:E1, :], ACT.Copy)\
                       .then_inc(*S.did("pt"))
                act.wait_ge(*P.at("hg", h, e, c))
                if k >= 4:
                    ub = units(4)[k - 4]
                    act.wait_ge(*P.at("y" if ub[2] == 3 else "yp", *(ub[:2] if ub[2] == 3 else ub)))
                act.activation(ACTB[:, k % 4, :], bank(k % 4), ACT.Relu, bias=B1[:, e, c:c + 1])\
                   .then_inc(*S.did("relu", h, e, c))

        @block.tensor
        def _(pe):
            def mm(out_, lhs, rhs, start=True, stop=True, **k):
                return pe.matmul(out_, lhs, rhs, start=start, stop=stop, **k)

            def bias(out_, name, n=D, p=128):
                mm(out_, ONES[0:1, 0:p], row(name, n, 1), True, False)

            pe.wait_ge(ld_x, 32)
            pe.wait_ge(*mdve.at("xn"))
            for b in range(B):
                i = pe.transpose(PS[:, 6 + b // 4, (b % 4) * T:(b % 4 + 1) * T], XN[:, b, :], IDN)
            i.then_inc(*mpe.did("xnt"))
            pe.wait_ge(ld_m, 32)
            pe.wait_ge(*mact.at("xnt"))
            pe.nop().then_inc(L["yacc"], CREDIT)
            xnt = XNT[:, :, :].rearrange("p b t -> p (b t)")
            for d in range(2):
                for c in range(4):
                    if d:
                        pe.wait_ge(*mact.at("xp" if c < NC else "zs", 0))
                    for h in range(2):
                        i = mm(bank(2 * c + h), WIN[:, d, c * 128:(c + 1) * 128], xnt[:, h * HALF:(h + 1) * HALF])
                    i.then_inc(*mpe.did(f"xz{c}", d))
            pe.wait_ge(ld_ctx, 48)
            pe.wait_ge(ld_c, 48)
            pe.wait_ge(*mdve.at("const"))
            pe.wait_ge(*mact.at("xp", 1))
            for g in range(2):
                i = mm(bank(g)[:, 0:4 * M], X0K, CTXT[:, 4 * g:4 * g + 4, :].rearrange("p b m -> p (b m)"))
            i.then_inc(*mpe.did("kt0"))
            for b in range(B):
                o = PS[0:M, 2 + b // 4, (b % 4) * D:(b % 4 + 1) * D]
                bias(o, "x0_bv", p=M)
                i = mm(o, CTXT[:, b, :], X0V, False, True)
            i.then_inc(*mpe.did("v0"))
            for d in range(2):
                pe.wait_ge(*mact.at("u", d))
                if d:
                    pe.wait_ge(*mact.at("dts", 0))
                    pe.wait_ge(*mdve.at("s3", 0))
                else:
                    pe.wait_ge(*mact.at("v0"))
                for h in range(2):
                    for c in range(NC):
                        mm(bank(h)[0:DR, :], WDT[:, d, c, :], U[d][:, c, h * HALF:(h + 1) * HALF], c == 0, c == NC - 1)
                    for c in range(NC):
                        i = mm(bank(2 + h)[0:96, :], WBC[:, d, c, :], U[d][:, c, h * HALF:(h + 1) * HALF],
                               c == 0, c == NC - 1)
                i.then_inc(*mpe.did("dbc", d))
                pe.wait_ge(*mact.at("dts", d))
                if d == 0:
                    pe.wait_ge(*mact.at("zs", 1))
                for c in range(NC):
                    if d:
                        pe.wait_ge(*mact.at(f"abs{c}", 0))
                    for h in range(2):
                        i = mm(bank(4 + 2 * c + h), DTW[:, d, c * 128:(c + 1) * 128], DTS[d][0:DR, h * HALF:(h + 1) * HALF])
                    i.then_inc(*mpe.did(f"dt{c}", d))
            pe.wait_ge(*mdve.at("cb"))
            for b in range(B):
                i = pe.transpose(PS[:, b // 4, (b % 4) * T:(b % 4) * T + M], CTX[:, b, :], IDN[0:M, 0:M])
            i.then_inc(*mpe.did("ct"))
            pe.wait_ge(*mact.at("abs1", 1))
            pe.wait_ge(*mdve.at("diag"))
            for d in range(2):
                base = d * DS + CREDIT

                def start_y():
                    for c in range(NC):
                        for h in range(2):
                            i = mm(bank(4 + 2 * c + h), DIAG[:, d, c, :], U[d][:, c, h * HALF:(h + 1) * HALF], True, False)
                    i.then_inc(*mpe.did("y0", d))

                def rows_bc(st, n):
                    for k, off, ps in (("b", 0, 0), ("c", DS, 2)):
                        pe.wait_ge(L[f"{k}_sb"], n)
                        for h in range(2):
                            ins = mm(bank(ps + h), SEL[:, bass.ds(st + off, 1)].to_broadcast([128, 128]),
                                     S3[d][:, h * HALF:(h + 1) * HALF])
                        ins.then_inc(L[f"{k}_ps"], 1)

                def sum_y(s, n, stop=False):
                    for c in range(NC):
                        pe.wait_ge(L[f"hc{c}"], n + 1)
                        for h in range(2):
                            ins = mm(bank(4 + 2 * c + h), IDN, HB[s][:, c, h * HALF:(h + 1) * HALF], False, stop)
                    ins.then_inc(L["yacc"], 1)

                if d == 0:
                    start_y()
                    pe.wait_ge(*mact.at("ct"))
                    pe.wait_ge(*mdve.at("s3", 1))
                rows_bc(0, base)
                rows_bc(1, base + 1)
                if d == 1:
                    pe.wait_ge(*mdve.at("y", 0))
                    start_y()
                with pe.Fori(0, DS // 4 - 1) as it:
                    for s in range(4):
                        rows_bc(it * 4 + (s + 2), it * 4 + (s + 2 + base))
                        sum_y(s, it * 4 + (s + base))
                for s in range(4):
                    if s < 2:
                        rows_bc(DS - 2 + s, base + DS - 2 + s)
                    if d == 1 and s == 2:
                        pe.wait_ge(L["b_sb"], base + DS)
                        for b in range(B):
                            for c in range(NC):
                                mm(PS[:, b // 4, (b % 4) * D:(b % 4 + 1) * D], ZS[:, 0, c, b * T:(b + 1) * T], WOUT[:, 0, c, :],
                                   b % 4 == 0 and c == 0, False, skip_group_check=True)
                    sum_y(s, base + DS - 4 + s, s == 3)
            pe.wait_ge(*mdve.at("y", 1))
            for b in range(B):
                for c in range(NC):
                    i = mm(PS[:, b // 4, (b % 4) * D:(b % 4 + 1) * D], ZS[:, 1, c, b * T:(b + 1) * T], WOUT[:, 1, c, :],
                           False, b % 4 == 3 and c == NC - 1, skip_group_check=True)
                if b % 4 == 3:
                    i.then_inc(*mpe.did("out", b // 4))

            def turn(S, step, n, out_, src, wait):
                pe.wait_ge(*wait)
                pe.transpose(out_, src, IDN).then_inc(*S.did(step, n))

            def narrow_heads(L_, step, n, v, w, keys, values, w_out, b_out, bank_free):
                S, A, DV = L_["pe"], L_["act"], L_["dve"]

                def turned(k):
                    return (DV if ("pt", k) in DV.value else A).at("pt", k)

                if step == "sc":
                    if n % 4 == 0:
                        for k in ("qt",) if keys == M else ("q", "k", "v"):
                            pe.wait_ge(*A.at(k, n // 4))
                    pe.wait_ge(*L_["pool"].at("kx", n))
                    after(pe, DV, "sub", n - 3)
                    mm(bank(n % 3)[:, 0:4 * keys], v["qt"], w["kx"].rearrange("p h m -> p (h m)")).then_inc(*S.did("sc", n))
                elif step == "pt":
                    pe.wait_ge(*A.at("p", n))
                    if n >= 2:
                        pe.wait_ge(*turned(n - 2))
                    for h in range(4):
                        ins = pe.transpose(PS[0:keys, 3 + n % 2, h * T:(h + 1) * T], w["p"][:, h * keys:(h + 1) * keys], IDN)
                    ins.then_inc(*S.did("pt", n))
                elif step == "pv":
                    b, g = divmod(n, 4)
                    if g == 0:
                        after(pe, DV, bank_free, b - 2)
                    pe.wait_ge(*turned(n))
                    for h in range(4):
                        o = (4 * g + h) * (HD0 + 1)
                        ins = mm(PS[:, 5 + b % 2, o:o + HD0 + 1], w["pt"][0:keys, h * T:(h + 1) * T], values[:, 4 * g + h, :])
                    ins.then_inc(*S.did("pv", n))
                elif step == "ot":
                    turn(S, "ot", n, PS[:, 5 + n % 2, 256:384], v["o"], DV.at("o", n))
                elif step == "wo":
                    pe.wait_ge(*A.at("ot", n))
                    bias(PS[:, 5 + n % 2, 384:512], b_out)
                    mm(PS[:, 5 + n % 2, 384:512], v["ot"], w_out, False, True).then_inc(*S.did("wo", n))

            S, A, DV = x0["pe"], x0["act"], x0["dve"]
            for step, n in S.order:
                group = step in ("sc", "pt", "pv")
                b = n // 4 if group else n
                v, w = X0S[b % 4], X0U[n % 3]
                if step == "xt":
                    after(pe, A, "qt", b - 1)
                    turn(S, "xt", b, PS[:, 7, 0:T], v["xn"], DV.at("xn", b))
                elif step == "q":
                    pe.wait_ge(*A.at("xt", b))
                    bias(PS[:, 7, 0:D], "x0_bq")
                    mm(PS[:, 7, 0:D], v["xt"], X0Q, False, True).then_inc(*S.did("q", b))
                elif step == "qt":
                    turn(S, "qt", b, PS[:, 7, 0:T], v["qr"], DV.at("rope", b))
                elif step == "xt2":
                    turn(S, "xt2", b, PS[:, 5 + b % 2, 0:T], v["xn2"], DV.at("xn2", b))
                elif step == "gate":
                    if b == 0:
                        pe.wait_ge(ld_w1, 16)
                    pe.wait_ge(*A.at("xt2", b))
                    mm(PS[:, 5 + b % 2, 0:E0], XNT[:, b, :], f_g).then_inc(*S.did("gate", b))
                else:
                    narrow_heads(x0, step, n, v, w, M, V0[:, b, :, :], X0O, "x0_bo", "lg")

            def moe_units(F, n, ahead, w_in, w_out, rhs, second=None):
                S = F["pe"]
                us = units(n)

                def hidden(k):
                    h, e, c = us[k]
                    if len(w_in) == 2:
                        if k >= 3:
                            pe.wait_ge(*F["dve"].at("act", *us[k - 3]))
                        for j in range(2):
                            ins = mm(bank(2 * (k % 3) + j), w_in[j][:, e, c * 128:(c + 1) * 128], rhs[:, h * HALF:(h + 1) * HALF])
                    else:
                        if k >= 4:
                            pe.wait_ge(*F["act"].at("relu", *us[k - 4]))
                        ins = mm(bank(k % 4), w_in[0][:, e, c * 128:(c + 1) * 128], rhs[:, h * HALF:(h + 1) * HALF])
                    ins.then_inc(*S.did("hg", h, e, c))

                for k in range(ahead):
                    hidden(k)
                if second:
                    second()
                for k, (h, e, c) in enumerate(us):
                    if k + ahead < len(us):
                        hidden(k + ahead)
                    if len(w_in) == 2:
                        pe.wait_ge(*F["dve"].at("act", h, e, c))
                    else:
                        pe.wait_ge(*F["act"].at("relu", h, e, c))
                    ring = 3 if len(w_in) == 2 else 4
                    if c == 0 and h * E0 + e >= 2:
                        ph, pe_ = divmod(h * E0 + e - 2, E0)
                        pe.wait_ge(*F["dve"].at("acc", ph, pe_))
                    for j in range(4):
                        ins = mm(PS[:, 6 + e % 2, j * D:(j + 1) * D], ACTB[:, k % ring, j * T:(j + 1) * T],
                                 w_out[:, e, c, :], c == 0 and j == 0, c == n - 1 and j == 3, skip_group_check=True)
                    if c == n - 1:
                        ins.then_inc(*S.did("y", h, e))
                    else:
                        ins.then_inc(*S.did("yp", h, e, c))

            S, A, DV = f0["pe"], f0["act"], f0["dve"]
            pe.wait_ge(ld_f0, 16)
            pe.wait_ge(*x0["dve"].at("lg", B - 1))
            moe_units(f0, 2, 1, FW, FW3, xnt)

            def a1_step(step, b):
                S, A, DV = a1["pe"], a1["act"], a1["dve"]
                v, ps = A1S[b % 6], PS[:, b % 6, 0:T]
                if step == "xt":
                    after(pe, DV, "y", b - 6)
                    turn(S, "xt", b, ps, v["xn"], DV.at("xn", b))
                elif step == "qkv":
                    pe.wait_ge(*A.at("xt", b))
                    for k in range(2):
                        mm(PS[:, b % 6, k * T:(k + 1) * T], A1W[:, k * D:(k + 1) * D], v["xt"])
                    bias(PS[:, b % 6, 2 * D:3 * D], "a1_bv")
                    mm(PS[:, b % 6, 2 * D:3 * D], v["xt"], A1W[:, 2 * D:3 * D], False, True).then_inc(*S.did("qkv", b))
                elif step == "s":
                    for k in "qkv":
                        pe.wait_ge(*A.at(k, b))
                    mm(ps, v["qt"], v["kt"]).then_inc(*S.did("s", b))
                elif step == "pt":
                    turn(S, "pt", b, ps, v["p"], A.at("p", b))
                elif step == "o":
                    pe.wait_ge(*A.at("pt", b))
                    mm(ps, v["v"], v["pt"]).then_inc(*S.did("o", b))
                elif step == "out":
                    pe.wait_ge(*A.at("o", b))
                    mm(ps, v["ot"], A1P).then_inc(*S.did("out", b))

            def x1_step(step, n):
                S, A, DV = x1["pe"], x1["act"], x1["dve"]
                group = step in ("s", "pt", "o")
                b, g = divmod(n, 4) if group else (n, 0)
                v, w = X1S[b % 2], X1U[n % 3]
                rows_ = slice(64 * (g % 2), 64 * (g % 2) + 64)
                if (step, n) == ("lt", 0):
                    pe.wait_ge(ld_x1, 16)
                    pe.wait_ge(ones, 1)
                if (step, n) == ("s", 0):
                    pe.wait_ge(*a1["dve"].at("y", B - 1))
                if step == "lt":
                    after(pe, DV, "vb", b - 1)
                    turn(S, "lt", b, PS[:, 6, 0:T], v["l2"], DV.at("l2", b))
                elif step == "q":
                    pe.wait_ge(*A.at("lt", b))
                    for c in range(4):
                        ins = mm(PS[:, 6, c * T:(c + 1) * T], X1Q[:, c * 128:(c + 1) * 128], KVT[:, b, M:J1])
                    ins.then_inc(*S.did("q", b))
                elif step in ("k0", "k1"):
                    if step == "k0":
                        pe.wait_ge(*A.at("lt", b))
                        after(pe, DV, "va", b - 1)
                    else:
                        pe.wait_ge(*A.at("q", b))
                    bk, c0_ = (7, 0) if step == "k0" else (6, 2)
                    for c in range(2):
                        ins = mm(PS[:, bk, c * J1:(c + 1) * J1], X1KV[:, (c0_ + c) * 128:(c0_ + c + 1) * 128], KVT[:, b, :])
                    ins.then_inc(*S.did(step, b))
                elif step == "va":
                    pe.wait_ge(*A.at("k0", b))
                    mm(bank(7)[0:M, :], KVT[:, b, 0:M], X1KV[:, 512:1024]).then_inc(*S.did("va", b))
                elif step == "vb":
                    pe.wait_ge(*A.at("k1", b))
                    mm(bank(6), KVT[:, b, M:J1], X1KV[:, 512:1024]).then_inc(*S.did("vb", b))
                elif step == "s":
                    if g == 0:
                        pe.wait_ge(*A.at("k0", b))
                        pe.wait_ge(*A.at("k1", b))
                    after(pe, DV, "sub", n - 2)
                    for j in range(2):
                        c = 2 * (g // 2) + j
                        ins = mm(PS[:, n % 2, j * J1:(j + 1) * J1], v["qt"][rows_, c, :], v["kt"][rows_, c, :])
                    ins.then_inc(*S.did("s", n))
                elif step == "pt":
                    pe.wait_ge(*A.at("p", n))
                    after(pe, A, "pt", n - 2)
                    for j in range(2):
                        pe.transpose(PS[0:M, 2 + n % 2, j * T:(j + 1) * T], w["p"][:, j, 0:M], IDN)
                        ins = pe.transpose(PS[:, 2 + n % 2, (2 + j) * T:(3 + j) * T], w["p"][:, j, M:J1], IDN)
                    ins.then_inc(*S.did("pt", n))
                elif step == "o":
                    if g == 0:
                        pe.wait_ge(*DV.at("va", b))
                        pe.wait_ge(*DV.at("vb", b))
                        after(pe, DV, "o0", b - 1)
                    if g == 2:
                        after(pe, DV, "res", b - 1)
                    pe.wait_ge(*A.at("pt", n))
                    for j in range(2):
                        h = 4 * (g // 2) + g % 2 + 2 * j
                        o = PS[:, 4 + g // 2, (h % 4) * (HD1 + 1):(h % 4 + 1) * (HD1 + 1)]
                        mm(o, w["pta"][0:M, j, :], v["va"][0:M, h, :], True, False)
                        ins = mm(o, w["ptb"][:, j, :], v["vb"][:, h, :], False, True)
                    ins.then_inc(*S.did("o", n))
                elif step == "ot":
                    pe.wait_ge(*DV.at("o0", b))
                    pe.wait_ge(*DV.at("o1", b))
                    for c in range(4):
                        ins = pe.transpose(PS[:, 5, c * T:(c + 1) * T], v["o"][:, c * 128:(c + 1) * 128], IDN)
                    ins.then_inc(*S.did("ot", b))
                elif step == "out":
                    pe.wait_ge(*A.at("ot", b))
                    for c in range(4):
                        ins = mm(PS[:, 5, 0:D], v["ot"][:, c, :], X1O[:, c, :], c == 0, c == 3)
                    ins.then_inc(*S.did("out", b))

            def g1_step(step, n):
                S, A, DV = g1["pe"], g1["act"], g1["dve"]
                if (step, n) == ("xt", 0):
                    pe.wait_ge(ld_w2, 32)
                    pe.wait_ge(ones, 2)
                    pe.wait_ge(*x1["dve"].at("va", B - 1))
                elif (step, n) == ("sc", 0):
                    pe.wait_ge(*x1["dve"].at("sub", 4 * B - 1))
                    pe.wait_ge(*x1["act"].at("pt", 4 * B - 1))
                elif (step, n) == ("pt", 0):
                    pe.wait_ge(*x1["dve"].at("o0", B - 1))
                elif (step, n) == ("pv", 0):
                    pe.wait_ge(*x1["dve"].at("res", B - 1))
                group = step in ("sc", "pt", "pv")
                b = n // 4 if group else n
                v, w = G1S[b % 4], G1U[n % 3]
                if step == "xt":
                    for k in "qkv":
                        after(pe, A, k, b - 1)
                    turn(S, "xt", b, PS[:, 7, 0:T], v["xn"], DV.at("xn", b))
                elif step == "y":
                    pe.wait_ge(*A.at("xt", b))
                    bias(PS[:, 7, 0:D], "conv_b")
                    for k in range(3):
                        ins = mm(PS[:, 7, 0:D], v["xp"][:, k:k + T], GC[:, k, :], False, k == 2)
                    ins.then_inc(*S.did("y", b))
                elif step == "yt":
                    turn(S, "yt", b, PS[:, 7, 0:T], v["y"], DV.at("y", b))
                elif step == "qkv":
                    pe.wait_ge(*A.at("yt", b))
                    for k in range(2):
                        mm(PS[:, 7, k * T:(k + 1) * T], G_QKV[:, k * D:(k + 1) * D], v["yt"])
                    bias(PS[:, 7, 2 * D:3 * D], "f1_bv")
                    mm(PS[:, 7, 2 * D:3 * D], v["yt"], G_QKV[:, 2 * D:3 * D], False, True).then_inc(*S.did("qkv", b))
                elif step == "xat":
                    turn(S, "xat", b, PS[:, 5 + b % 2, 0:T], XN1[:, b, :], DV.at("xa", b))
                elif step == "gate":
                    pe.wait_ge(*A.at("xat", b))
                    bias(PS[:, 5 + b % 2, 0:E1], "gate_b", E1)
                    mm(PS[:, 5 + b % 2, 0:E1], XAT1[:, b, :], G_G, False, True).then_inc(*S.did("gate", b))
                else:
                    narrow_heads(g1, step, n, v, w, T, v["v"], G_O, "f1_bo", "lg")

            overlapped("pe", {"a1": a1_step, "x1": x1_step, "g1": g1_step})

            S, A, DV = f1["pe"], f1["act"], f1["dve"]

            def second():
                pe.wait_ge(*DV.at("prob"))
                for b in range(B):
                    i = pe.transpose(PS[0:E1, 4 + b // 4, (b % 4) * T:(b % 4 + 1) * T], PROB[:, b, :], IDN)
                i.then_inc(*S.did("pt"))
                pe.wait_ge(*A.at("pt"))
                for b in range(B):
                    i = mm(PS[:, 4 + b // 4, (b % 4) * D:(b % 4 + 1) * D], PROBT[0:E1, b, :], B2[:, :])
                i.then_inc(*S.did("b2"))

            moe_units(f1, 4, 3, [G1], G2, XAT1.rearrange("p b t -> p (b t)"), second)


def _constants():
    c = np.zeros((128, 156 + 2 * DS), np.float32)
    c[:, 0:128] = np.eye(128)
    c[:, 128:144] = np.arange(128)[:, None] // HD0 == np.arange(H0)[None, :]
    c[:, 144:148] = 1.0 / 10000.0 ** (np.arange(0, HD0, 2, dtype=np.float32) / HD0)
    c[:, 148:156] = np.arange(8)
    for r in range(96):
        c[r, 156 + r % 32] = 1
    return c


def kernel(**inp):
    import concourse.bacc as bacc
    from concourse.bass_utils import run_bass_kernel_spmd

    a = {k: np.asarray(v) for k, v in inp.items()}
    m = {d: {k[len("L0_attn_"):-2]: v for k, v in a.items() if k.startswith("L0_attn_") and k.endswith("_" + d)} for d in "fb"}

    def flat(*parts):
        return np.ascontiguousarray(np.concatenate([p.reshape(p.shape[0], -1) for p in parts], axis=1))

    def chunks(w, n=128):
        return w.reshape(w.shape[0] // n, n, -1).transpose(1, 0, 2)

    consts = _constants()
    w_m = flat(*[m[d]["in_proj"].T for d in "fb"],
               *[chunks(m[d]["x_proj"][0:DR].T) for d in "fb"],
               *[np.concatenate([chunks(m[d]["x_proj"][DR:].T)] * 3, axis=2) for d in "fb"],
               *[chunks(m[d]["out_proj"].T) for d in "fb"])
    dtw_t = np.ascontiguousarray(np.stack([m[d]["dt_w"].T for d in "fb"], axis=1))
    rows = {"ln_w": a["L0_attn_ln_w"], "ln_b": a["L0_attn_ln_b"], "gm": a["L1_xattn_gm"], "bm": a["L1_xattn_bm"],
            "gl": a["L1_xattn_gl"], "bl": a["L1_xattn_bl"], "ln1_g": a["L1_ffn_ln1_g"], "ln1_b": a["L1_ffn_ln1_b"],
            "ln2_g": a["L1_ffn_ln2_g"], "ln2_b": a["L1_ffn_ln2_b"], "x0_bq": a["L0_xattn_bq"],
            "x0_bv": a["L0_xattn_bv"], "x0_bo": a["L0_xattn_bo"], "a1_bv": a["L1_attn_b_qkv"][2 * D:],
            "a1_bproj": a["L1_attn_b_proj"], "conv_b": a["L1_ffn_conv_b"], "f1_bv": a["L1_ffn_bqkv"][2 * D:],
            "f1_bo": a["L1_ffn_bo"], "gate_b": a["L1_ffn_gate_b"]}
    row = np.zeros((1, len(ROWS) * D), np.float32)
    for i, k in enumerate(ROWS):
        row[0, i * D:i * D + rows[k].size] = rows[k]
    both = "fb"
    cols = flat(*[chunks(m[d]["conv_w"]) for d in both], *[chunks(m[d]["conv_b"][:, None]) for d in both],
                *[chunks(m[d]["dt_b"][:, None]) for d in both], *[chunks(m[d]["D"][:, None]) for d in both],
                *[chunks(m[d]["A_log"]) for d in both], a["L0_xattn_bk"][:, None],
                a["L1_attn_b_qkv"][0:2 * D].reshape(2, D).T, a["L1_ffn_bqkv"][0:2 * D].reshape(2, D).T,
                a["L1_ffn_b1"].reshape(E1, 4, 128).transpose(2, 0, 1))
    arrays = {
        "x": a["x"], "ctx": a["ctx_1024"], "ctx_t": np.ascontiguousarray(a["ctx_1024"].transpose(2, 0, 1)),
        "pos": np.ascontiguousarray(a["itok_BxS_1_4095"].T), "w_m": w_m, "dtw_t": dtw_t, "consts": consts,
        "rows": row, "cols": cols,
        "w_x0": flat(*[a[f"L0_xattn_W{k}"].T for k in "qkvo"]),
        "w_f0": flat(*[a[f"L0_ffn_W{k}"].transpose(1, 0, 2) for k in (1, 2)],
                     a["L0_ffn_W3"].reshape(E0, 2, 128, D).transpose(2, 0, 1, 3)),
        "w_a1": flat(a["L1_attn_W_qkv"], a["L1_attn_W_proj"], a["L0_ffn_Wg"]),
        "w_x1": flat(a["L1_xattn_Wq"], a["L1_xattn_Wkv"], chunks(a["L1_xattn_Wout"])),
        "w_f1": flat(a["L1_ffn_conv_w"].transpose(1, 2, 0), a["L1_ffn_wqkv"].T, a["L1_ffn_wo"].T, a["L1_ffn_gate_w"],
                     a["L1_ffn_w1"].transpose(1, 0, 2), a["L1_ffn_w2"].reshape(E1, 4, 128, D).transpose(2, 0, 1, 3)),
        "b2": a["L1_ffn_b2"],
    }
    nc = bacc.Bacc("TRN2", target_bir_lowering=False, num_devices=1)
    args = [nc.dram_tensor(f"in_{k}", v.shape, mybir.dt.from_np(v.dtype), kind="ExternalInput").ap()
            for k, v in arrays.items()]
    out = nc.dram_tensor("out_x", (B, T, D), F32, kind="ExternalOutput").ap()
    decoder_kernel(nc, *args, out)
    r = run_bass_kernel_spmd(nc, [{f"in_{k}": v for k, v in arrays.items()}], core_ids=[0])
    return r.results[0]["out_x"]
```

```python
from contextlib import ExitStack

import numpy as np

import concourse.bass as bass
from concourse import mybir

F32 = mybir.dt.float32
BF16 = mybir.dt.bfloat16
I32 = mybir.dt.int32
U32 = mybir.dt.uint32
ALU = mybir.AluOpType
ACT = mybir.ActivationFunctionType
AX = mybir.AxisListType.X

B, T, D = 8, 128, 128
N = B * T
M = 77
H0, HD0 = 16, 8
DI, DS, DC, DR = 256, 16, 4, 64
NC = DI // 128
E0, HID0 = 8, 256
H1, HD1 = 8, 64
J1 = M + T
E1, HID1 = 8, 512
EPS = 1e-5
MAGIC = 1.5 * 2.0 ** 23
TWO_PI = (6.28125, 0.0019350051879882812, 3.0198604e-07)
HALF = N // 2

ROWS = ["ln_w", "ln_b", "gm", "bm", "gl", "bl", "ln1_g", "ln1_b", "ln2_g", "ln2_b",
        "x0_bq", "x0_bv", "x0_bo", "a1_bv", "a1_bproj", "conv_b", "f1_bv", "f1_bo", "gate_b"]


class Steps:

    def __init__(self, sem, order):
        self.sem, self.order, self.n = sem, list(order), 0
        self.value = {k: i + 1 for i, k in enumerate(self.order)}
        assert len(self.value) == len(self.order)

    def at(self, *key):
        return self.sem, self.value[key]

    def did(self, *key):
        assert self.order[self.n] == key, (self.order[self.n], key)
        self.n += 1
        return self.sem, 1


def after(engine, steps, step, n):
    if n >= 0:
        engine.wait_ge(*steps.at(step, n))


def pipeline(sem, timeline, name, start, period, sequence, group=None, dve_turns=(), second=None):
    begin = [b * period for b in range(B)]
    if second:
        begin[B // 2:] = [second[0] + b * second[1] for b in range(B // 2)]
    steps = {}
    for e in ("pe", "act", "dve", "pool"):
        places = [(round(start + begin[b] + t, 3), name, step, b) for step, t in sequence[e].items() for b in range(B)]
        places += [(round(start + k * period / 4 + t, 3), name, step, k)
                   for step, t in (group or {}).get(e, {}).items() for k in range(4 * B)
                   if not (step == "pt" and e in ("act", "dve") and (k % 4 in dve_turns) != (e == "dve"))]
        steps[e] = Steps(sem(f"{e}_{name}"), [key[2:] for key in sorted(places)])
        timeline[e] += places
    return steps


def decoder_kernel(nc, x, ctx, ctx_t, pos, w_m, dtw_t, consts, rows, cols, w_x0, w_f0, w_a1, w_x1, w_f1, b2, out):
    with ExitStack() as stack:
        def sb(name, shape, dt=F32):
            return stack.enter_context(nc.sbuf_tensor(name, shape, dt))

        def sem(name):
            return stack.enter_context(nc.semaphore(name))

        X = sb("residual", [T, B, D])
        XNT = sb("normed_t", [D, B, T])
        CTX = sb("context", [M, B, D])
        CTXT = sb("context_t", [D, B, M])
        KT0 = sb("x0_keys_t", [D, B, M])
        V0 = sb("x0_values", [M, B, H0, HD0 + 1])
        KVT = sb("x1_kv_input_t", [D, B, J1])
        WM = sb("w_m", [128, w_m.shape[1]])
        DTW = sb("dt_w_t", [DR, 2, DI])
        SEL = sb("row_selectors", [128, 2 * DS], BF16)
        CONST = sb("consts", [128, consts.shape[1]])
        ROW = sb("rows", [128, len(ROWS) * D])
        COL = sb("cols", [128, cols.shape[1]])
        WX0 = sb("w_x0", [128, w_x0.shape[1]])
        WF0 = sb("w_f0", [128, w_f0.shape[1]])
        WA1 = sb("w_a1", [128, w_a1.shape[1]])
        WX1 = WM[:, 0:w_x1.shape[1]]
        WF1 = sb("w_f1", [128, w_f1.shape[1]])
        B2 = sb("moe1_b2", [E1, D])
        POSI = sb("positions", [T, B], I32)
        ROPE = sb("rope_tables", [T, 2, B, 2, 4])
        ONES = sb("ones", [128, 128])
        HALFNEG = sb("minus_half", [128, B])
        DIAG = sb("diag_D", [128, 2, NC, 128])
        NEGA = sb("neg_A", [128, 2, NC, DS])
        ST6 = sb("bn_stats", [128, B, 6])
        MV = sb("mean_var", [128, B, 2])
        RS = sb("rstd", [128, B])
        SMALL = sb("small", [128, 8, B, 8])
        TOPI = sb("top_index", [128, B, 8], U32)
        PS = stack.enter_context(nc.psum_tensor("ps", [128, 8, 512], F32))

        ARENA_N = 22016
        ARENA = sb("arena", [128, ARENA_N])

        class Region:
            def __init__(self, start=0, of=None):
                self.o, self.of = start, ARENA if of is None else of

            def take(self, *shape):
                n = int(np.prod(shape))
                v = self.of[:, self.o:self.o + n]
                self.o += n
                assert self.o <= self.of.shape[1], self.o
                if len(shape) > 1:
                    names = "abcd"[:len(shape)]
                    v = v.rearrange(f"p ({' '.join(names)}) -> p {' '.join(names)}",
                                    **{k: s for k, s in zip(names[1:], shape[1:])})
                return v

        r = Region()
        XN = r.take(B, D)
        ZS = r.take(2, NC, N)
        U = [r.take(NC, N)]
        DELTA = [r.take(NC, N)]
        S3 = [r.take(N // 2).bitcast(BF16)]
        DU = [U[0]]
        m_shared = r.o
        DA = r.take(2, NC, N)
        HB = [r.take(NC, N) for _ in range(2)]
        BS = r.take(2, N)
        CS = r.take(2, N)
        q = Region(m_shared)
        DTS, RES = [q.take(N)], [q.take(N)]
        SPR, SPE = [q.take(NC, N)], [q.take(NC, N)]
        XP = [q.take(NC, B, T + DC - 1)]
        SMALLE = [q.take(NC * N).bitcast(I32)]
        f = Region(0, WF0)
        DTS.append(f.take(N))
        RES.append(f.take(N))
        SPR.append(f.take(NC, N))
        f0_end = f.o
        DU.append(WF0[:, f.o - NC * N:f.o].rearrange("p (c n) -> p c n", c=NC))
        f = Region(0, WF1)
        XP.append(f.take(NC, B, T + DC - 1))
        SMALLE.append(f.take(NC * N).bitcast(I32))
        second_u = f.o
        f = Region(0, WF1)
        HB += [f.take(NC, N) for _ in range(2)]
        f = Region(max(second_u, f.o), WF1)
        U.append(f.take(NC, N))
        DELTA.append(f.take(NC, N))
        S3.append(f.take(N // 2).bitcast(BF16))
        SPE.append(Region(f0_end, WF0).take(NC, N))
        SPL = [t[:, o:o + NC * N].rearrange("p (c n) -> p c n", c=NC) for t, o in ((ARENA, m_shared), (WF0, 0))]
        EXPV = [SPE[d].rearrange("p c n -> p (c n)") for d in range(2)]
        SPT = [XP[d].rearrange("p c b t -> p (c b t)")[:, 0:NC * N] for d in range(2)]

        def slots(n, **sizes):
            return [{k: region.take(*(size if isinstance(size, tuple) else (size,))) for k, size in sizes.items()}
                    for _ in range(n)]

        small = dict(xn=D, st=6, mv=2, var=1, rs=1)
        second = dict(st2=6, mv2=2, var2=1, rs2=1)
        region = Region()
        X0S = slots(4, xt=D, r1=D, r2=D, qr=D, qt=D, o=D, ot=D, xn2=D, rz=H0, **small, **second)
        X0U = slots(3, kx=(4, M), mx=4, p=4 * M, pt=4 * T)
        region = Region()
        X1S = slots(2, qt=(4, T), kt=(4, J1), va=(H1, HD1 + 1), vb=(H1, HD1 + 1), l1=D, l2=D, o=H1 * HD1, ot=(4, T),
                    rz=H1, **small, **second)
        X1U = slots(3, mx=2, p=(2, J1), pta=(2, T), ptb=(2, T))
        after_x1 = region.o
        A1BANK = (4, 5, 4, 5, 4, 5, 2, 3)
        A1S = slots(6, xt=D, qt=D, kt=D, v=D, a=D, r1=D, r2=D, p=D, pt=D, ot=D, y=D, mx=1, z=1, rz=1, **small)
        region = Region(after_x1)
        G1S = slots(4, xp=T + 2, y=D, yt=D, qt=D, kt=D, v=(H0, HD0 + 1), o=D, ot=D, l1=D, rz=H0, **small, **second)
        G1U = slots(3, kx=(4, T), mx=4, p=4 * T, pt=4 * T)
        r = Region()
        ACTS = r.take(4, HALF)
        ACTB = r.take(4, HALF)
        XA = r.take(B, D)
        XAT = r.take(B, T)
        PROB = r.take(B, E1)
        PROBT = r.take(B, T)
        FIN = r.take(B, D)
        XN1 = XNT[:, :, :]
        XAT1 = KVT[:, :, :].rearrange("p b j -> p (b j)")[:, 0:N].rearrange("p (b t) -> p b t", b=B)

        def row(name, n=D, p=128):
            i = ROWS.index(name)
            return ROW[0:p, i * D:i * D + n]

        def row_b(name, p=128):
            return row(name, D, p).unsqueeze(1).to_broadcast([p, B, D])

        IDN = CONST[:, 0:128]
        MASK = CONST[:, 128:128 + H0]
        FREQ = CONST[:, 144:148]
        IOTA = CONST[:, 148:156]
        c0 = [0]

        def col(n):
            c0[0] += n
            return COL[:, c0[0] - n:c0[0]]

        CONVW = [col(NC * DC).rearrange("p (c k) -> p c k", c=NC) for _ in range(2)]
        CONVB = [col(NC) for _ in range(2)]
        DTB = [col(NC) for _ in range(2)]
        DSK = [col(NC) for _ in range(2)]
        ALOG = col(2 * NC * DS)
        X0BK = col(1)
        A1B = col(2)
        F1B = col(2)
        B1 = col(E1 * 4).rearrange("p (e c) -> p e c", e=E1)

        def split(t, *sizes):
            o, parts = 0, []
            for n in sizes:
                parts.append(t[:, o:o + n])
                o += n
            return parts

        m_in, m_dt, m_bc, m_out = split(WM, 2 * 512, 2 * NC * DR, 2 * NC * 96, 2 * NC * 128)
        WIN = m_in.rearrange("p (d n) -> p d n", d=2)
        WDT = m_dt.rearrange("p (d c n) -> p d c n", d=2, c=NC)
        WBC = m_bc.rearrange("p (d c n) -> p d c n", d=2, c=NC)
        WOUT = m_out.rearrange("p (d c n) -> p d c n", d=2, c=NC)
        X0Q, X0K, X0V, X0O = split(WX0, D, D, D, D)
        f_1, f_2, f_3 = split(WF0, E0 * HID0, E0 * HID0, E0 * 2 * D)
        FW = [f_1.rearrange("p (e n) -> p e n", e=E0), f_2.rearrange("p (e n) -> p e n", e=E0)]
        FW3 = f_3.rearrange("p (e c n) -> p e c n", e=E0, c=2)
        A1W, A1P, f_g = split(WA1, 3 * D, D, E0)
        X1Q, X1KV, x1_o = split(WX1, 512, 1024, 4 * D)
        X1O = x1_o.rearrange("p (c n) -> p c n", c=4)
        g_c, G_QKV, G_O, G_G, g_1, g_2 = split(WF1, 3 * D, 3 * D, D, E1, E1 * HID1, E1 * 4 * D)
        GC = g_c.rearrange("p (k n) -> p k n", k=3)
        G1 = g_1.rearrange("p (e n) -> p e n", e=E1)
        G2 = g_2.rearrange("p (e c n) -> p e c n", e=E1, c=4)

        def bank(i, n=1):
            v = PS[:, i:i + n, :]
            return v.rearrange("p a b -> p (a b)")

        ld_x, ld_m, ld_c, ld_ctx, ld_w1, ld_f0, ld_x1, ld_w2 = (
            sem(f"loaded_{n}") for n in ("x", "m", "c", "ctx", "w1", "f0", "x1", "w2"))
        stored = sem("stored")
        ones = sem("ones_of_layer")

        both = range(2)
        mpe = Steps(sem("pe_mamba"), [("xnt",)] + [(k, d) for d in both for k in ("xz0", "xz1", "xz2", "xz3")] + [
            (k, d) for d in both for k in ("bc", "low", "dt0", "dt1")] + [
            ("ct",), ("kt0",), ("y0", 0), ("v0",), ("y0", 1), ("out", 0), ("out", 1)])
        mact = Steps(sem("act_mamba"), [("nega",), ("xnt",), ("sin_abs",), ("sin",)] + [
            (k, d) for d in both for k in ("xp", "zs")] + [("u", 0), ("u", 1)] + [
            (k, d) for d in both for k in ("dts", "relu0", "abs0", "relu1", "abs1", "exp")] + [
            ("ln", 0), ("ln", 1), ("ct",), ("kt0",), ("v0",)])
        mdve = Steps(sem("dve_mamba"), [("const",), ("stats",), ("mv",), ("var",), ("xn",)]
                     + [(f"rope{i}",) for i in range(9)] + [("rope",), ("nega",), ("diag",), ("cstats",), ("cmv",), ("cvar",)]
                     + [(k, d) for d in both for k in ("pad", "tap0", "tap1", "tap2", "conv")]
                     + [(k, 0) for k in ("s3a", "s3b", "s3c", "s3d", "s3")] + [("cn",), ("cg",), ("cb",)]
                     + [(k, 1) for k in ("s3a", "s3b", "s3c", "s3d", "s3")]
                     + [("poly0", 0), ("poly1", 0), ("poly", 0), ("small", 0), ("poly0", 1), ("pick", 0)]
                     + [("poly", 1), ("small", 1), ("pick", 1)]
                     + [("delta", 1), ("du", 1), ("du", 0), ("edge", 0), ("edge", 1), ("xb",), ("y", 0), ("y", 1)]
                     + [(k, h) for h in both for k in ("h", "hstats", "hmv", "hvar")]
                     + [(k, h) for h in both for k in ("hn", "hg", "x")])
        mpool = Steps(sem("pool_mamba"), [("rstd",), ("crstd",), ("poly1", 1), ("delta", 0), ("du", 1), ("hrstd", 0), ("hrstd", 1)])
        CREDIT = 4
        names = ["b_ps", "c_ps", "b_sb", "c_sb", "da0", "da1", "bu0", "bu1", "h0", "h1", "hc0", "hc1", "yacc"]
        L = {k: sem("state_" + k) for k in names}

        def timelines():
            return {e: [] for e in ("pe", "act", "dve", "pool")}

        x0 = pipeline(sem, timelines(), "x0", 0, 8.753, {
            "pe": {"xt": -12.21, "q": -9.69, "qt": -4.68, "ot": 12.46, "wo": 13.22, "xt2": 17.72, "gate": 19.64},
            "act": {"xt": -11.26, "qt": -4.42, "ot": 12.5, "xt2": 20.16},
            "dve": {"stats": -19.23, "mv": -18.5, "var": -14.86, "xn": -12.27, "rope_a": -5.59, "rope": -5.03,
                    "rz": 13.34, "o": 13.7, "res": 16.11, "stats2": 16.16, "mv2": 16.52, "var2": 17.33, "xn2": 19.18,
                    "lg": 22.24, "max": 29.45, "index": 32.89},
            "pool": {"rstd": 3.24, "rstd2": 37.87}}, {
            "pe": {"sc": -3.48, "pt": 1.16, "pv": 4.19},
            "act": {"p": 0.46, "pt": 3.16},
            "dve": {"mx": -0.44, "sub": 0.1, "pt": 5.37},
            "pool": {"kx": 11.72}}, (3,))

        def units(n):
            return [(h, e, c) for h in range(2) for e in range(E0) for c in range(n)]

        def moe_steps(name, n, ahead, first, act_unit, gated, second=None, half=()):
            us = units(n)
            second = second or {"pe": {}, "act": {}}
            hidden = [("hg",) + u for u in us]
            pe = list(first["pe"]) + hidden[:ahead]
            dv = list(first["dve"])
            for i, u in enumerate(us):
                pe += hidden[i + ahead:i + ahead + 1]
                pe.append(("y",) + u[:2] if u[2] == n - 1 else ("yp",) + u)
                pe += second["pe"].get(i, [])
            a = [k for i, u in enumerate(us) for k in second["act"].get(i, []) + [(act_unit,) + u]]
            prev = None
            for u in us:
                if gated:
                    dv.append(("act",) + u)
                if u[2] == n - 1:
                    if prev is not None:
                        dv.append(("acc",) + prev)
                        if prev[1] == E0 - 1:
                            dv += [(k, 0) for k in half]
                    prev = u[:2]
            dv.append(("acc",) + prev)
            dv += [(k, 1) for k in half]
            return {"pe": Steps(sem(f"pe_{name}"), pe),
                    "act": Steps(sem(f"act_{name}"), list(first["act"]) + a),
                    "dve": Steps(sem(f"dve_{name}"), dv),
                    "pool": Steps(sem(f"pool_{name}"), first["pool"])}

        f0 = moe_steps("f0", 2, 1, {
            "pe": [], "act": [("top_exp",)],
            "dve": [(k,) for k in ("top_i", "dif", "den", "w1", "w2", "s1", "s2", "s1w", "s2w", "comb")],
            "pool": []}, "silu", True)
        later = timelines()
        F0_START, F0_PERIOD = -135.88, 2.613
        for e in ("pe", "act", "dve"):
            later[e] += [(round(F0_START + k * F0_PERIOD, 3), "f0", "unit", k) for k in range(len(units(2)))]
        later["dve"].append((round(F0_START + len(units(2)) * F0_PERIOD + 1.5, 3), "f0", "end", 0))
        a1 = pipeline(sem, later, "a1", -85.99, 7.658, {
            "pe": {"xt": 0.7, "qkv": 1.76, "s": 4, "pt": 9.02, "o": 11.83, "out": 14.12},
            "act": {"xt": 0.55, "v": 3, "k": 3.2, "q": 3.26, "p": 8.19, "pt": 10.18, "o": 13.34},
            "dve": {"stats": -4.25, "mv": -2.75, "var": -1.82, "xn": 0.46, "a": 5.59, "l1": 5.85, "g1": 6.35,
                    "l": 6.76, "g": 6.9, "ls": 7.35, "m": 7.75, "am": 7.99, "mx": 8.03, "nmx": 8.45, "rz": 12.33,
                    "y": 17.17, "res": 22.42},
            "pool": {"rstd": -9.71}}, second=(40.63, 2.73))
        x1 = pipeline(sem, later, "x1", -25.66, 14.472, {
            "pe": {"lt": -15.29, "k0": -13.92, "q": -10.86, "k1": -8.56, "va": -7.12, "vb": -4.44, "ot": 24.14,
                   "out": 27.58},
            "act": {"lt": -15.07, "q": -10.89, "k0": -7.64, "k1": -5.31, "ot": 25.04},
            "dve": {"stats": -24.42, "mv": -23.44, "var": -22.63, "xn": -20.78, "stats2": -18.52, "mv2": -18.17,
                    "var2": -17.9, "l0": -16.87, "l1": -16.11, "l2": -14.63, "va": -2.51, "vb": -0.68, "rz0": 18.71,
                    "o0": 20.34, "rz1": 24.35, "o1": 25.2, "res": 31.19},
            "pool": {"rstd": -31.27, "rstd2": -27.39}}, {
            "pe": {"s": -5.47, "pt": 5.35, "o": 10.92},
            "act": {"p": 2.96, "pt": 7.42},
            "dve": {"mx": 1.71, "sub": 2.45},
            "pool": {}})
        g1 = pipeline(sem, later, "g1", 96.43, 11.893, {
            "pe": {"xt": -16.21, "y": -11.97, "yt": -10.42, "qkv": -9.8, "ot": 19.5, "wo": 22.22, "xat": 27.61,
                   "gate": 31.07},
            "act": {"xt": -12.7, "yt": -10.9, "v": -8.9, "q": -7.93, "k": -4.65, "ot": 21.42, "xat": 27.4},
            "dve": {"stats": -23.65, "mv": -22.26, "var": -21.12, "xn": -17.79, "y": -8.45, "rz": 20.88, "o": 21.82,
                    "h": 25.46, "stats2": 26.72, "mv2": 27.72, "var2": 28.05, "l0": 28.76, "l1": 28.86, "xa": 29.28,
                    "lg": 35.38},
            "pool": {"rstd": 6.55, "rstd2": 51.34}}, {
            "pe": {"sc": -1.4, "pt": 6.29, "pv": 9.63},
            "act": {"p": 2.38, "pt": 8},
            "dve": {"mx": 2.94, "sub": 4.54, "pt": 10.13},
            "pool": {"kx": 23.04}}, (3,))
        f1 = moe_steps("f1", 4, 3, {
            "pe": [], "act": [("gexp",)],
            "dve": [(k,) for k in ("gmx", "gsub", "gsum", "grz", "prob", "b", "b2")],
            "pool": [("rstd", 0), ("rstd", 1)]}, "relu", False, {"pe": {1: [("pt",)], 2: [("b2",)]}, "act": {5: [("pt",)]}},
            ("stats", "mv", "var", "xn", "g", "fin"))

        def overlapped(e, functions):
            for _, name, step, n in sorted(later[e]):
                functions[name](step, n)

        block = stack.enter_context(nc.Block())

        @block.sync
        def _(sp):
            sp.dma_start(X[:, :, :], x.rearrange("b t c -> t b c")).then_inc(ld_x, 16)
            sp.dma_start(CONST[:, :], consts).then_inc(ld_x, 16)
            sp.dma_start(WM[:, :], w_m).then_inc(ld_m, 16)
            sp.dma_start(DTW[:, :, :], dtw_t).then_inc(ld_m, 16)
            sp.dma_start(COL[:, :], cols).then_inc(ld_c, 16)
            sp.dma_start(POSI[:, :], pos).then_inc(ld_c, 16)
            sp.dma_start(ROW[:, :], rows.to_broadcast([128, rows.shape[1]])).then_inc(ld_c, 16)
            sp.dma_start(CTXT[:, :, :], ctx_t).then_inc(ld_ctx, 16)
            sp.dma_start(CTX[:, :, :], ctx.rearrange("b t c -> t b c")).then_inc(ld_ctx, 16)
            sp.dma_start(WX0[:, :], w_x0).then_inc(ld_ctx, 16)
            sp.dma_start(WA1[:, :], w_a1).then_inc(ld_w1, 16)
            sp.dma_start(B2[:, :], b2).then_inc(ld_w2, 16)
            sp.wait_ge(*mpe.at("out", 1))
            sp.dma_start(WF0[:, :], w_f0).then_inc(ld_f0, 16)
            sp.dma_start(WX1, w_x1).then_inc(ld_x1, 16)
            sp.dma_start(WF1[:, :], w_f1).then_inc(ld_w2, 16)
            for h in range(2):
                sp.wait_ge(*f1["dve"].at("fin", h))
                sp.dma_start(out[4 * h:4 * h + 4].rearrange("b t c -> t b c"), FIN[:, 4 * h:4 * h + 4, :]).then_inc(stored, 16)
            sp.wait_ge(stored, 32)

        @block.vector
        def _(dve):
            def stats_all(S, src, p, a, b_, c, half=None):
                bs, key = (range(B), ()) if half is None else (range(4 * half, 4 * half + 4), (half,))
                for b in bs:
                    i = dve.bn_stats(ST6[0:p, b, :], src[0:p, b, :])
                i.then_inc(*S.did(a, *key))
                dve.wait_ge(*S.at(a, *key))
                for b in bs:
                    i = dve.bn_aggr(MV[0:p, b, :], ST6[0:p, b, :])
                i.then_inc(*S.did(b_, *key))
                dve.wait_ge(*S.at(b_, *key))
                cols_ = slice(bs[0], bs[-1] + 1)
                dve.tensor_scalar(RS[0:p, cols_], MV[0:p, cols_, 1], EPS, None, ALU.add).then_inc(*S.did(c, *key))

            def norm_all(S, dst, src, p, step, half=None):
                bs, key = (range(B), ()) if half is None else (range(4 * half, 4 * half + 4), (half,))
                for b in bs:
                    i = dve.tensor_scalar(dst[0:p, b, :], src[0:p, b, :], MV[0:p, b, 0:1], RS[0:p, b:b + 1],
                                          ALU.subtract, ALU.mult)
                i.then_inc(*S.did(step, *key))

            dve.memset(ONES[:, :], 1.0)
            dve.memset(HALFNEG[:, :], -0.5)
            dve.memset(V0[:, :, :, HD0:HD0 + 1], 1.0)
            dve.memset(S3[0][96:128, :], 0.0)
            dve.memset(S3[1][96:128, :], 0.0).then_inc(*mdve.did("const"))
            dve.wait_ge(ld_x, 32)
            dve.tensor_copy(SEL[:, :], CONST[:, 156:156 + 2 * DS])
            stats_all(mdve, X, 128, "stats", "mv", "var")
            dve.wait_ge(*mpool.at("rstd"))
            norm_all(mdve, XN, X, 128, "xn")
            dve.wait_ge(ld_c, 48)
            posf, ang, k, rr = (SMALL[:, i, :, 0:4] for i in range(4))
            dve.tensor_copy(SMALL[:, 4, :, 0:1], POSI[:, :].unsqueeze(2)).then_inc(*mdve.did("rope0"))
            dve.wait_ge(*mdve.at("rope0"))
            dve.tensor_tensor(ang, SMALL[:, 4, :, 0:1].to_broadcast([T, B, 4]),
                              FREQ.unsqueeze(1).to_broadcast([T, B, 4]), ALU.mult).then_inc(*mdve.did("rope1"))
            dve.wait_ge(*mdve.at("rope1"))
            dve.tensor_scalar(k, ang, float(1 / (2 * np.pi)), MAGIC, ALU.mult, ALU.add).then_inc(*mdve.did("rope2"))
            dve.wait_ge(*mdve.at("rope2"))
            dve.tensor_scalar(k, k, -MAGIC, None, ALU.add).then_inc(*mdve.did("rope3"))
            for i, part in enumerate(TWO_PI):
                dve.wait_ge(*mdve.at(f"rope{3 + i}"))
                dve.scalar_tensor_tensor(ang, k, -part, ang, ALU.mult, ALU.add).then_inc(*mdve.did(f"rope{4 + i}"))
            dve.wait_ge(*mdve.at("rope6"))
            pi = float(np.float32(3.1415925))
            dve.tensor_scalar(ang, ang, pi, -pi, ALU.min, ALU.max).then_inc(*mdve.did("rope7"))
            dve.wait_ge(*mact.at("sin_abs"))
            dve.tensor_scalar(rr, rr, -1.0, float(np.pi / 2), ALU.mult, ALU.add).then_inc(*mdve.did("rope8"))
            dve.wait_ge(*mact.at("sin"))
            for g in range(2):
                dve.tensor_copy(ROPE[:, 0, :, g, :], SMALL[:, 5, :, 0:4])
            dve.tensor_scalar(ROPE[:, 1, :, 0, :], SMALL[:, 6, :, 0:4], -1.0, None, ALU.mult)
            dve.tensor_copy(ROPE[:, 1, :, 1, :], SMALL[:, 6, :, 0:4]).then_inc(*mdve.did("rope"))
            dve.wait_ge(*mact.at("nega"))
            na = NEGA[:, :, :, :].rearrange("p a b c -> p (a b c)")
            dve.tensor_scalar(na, na, -1.0, None, ALU.mult).then_inc(*mdve.did("nega"))
            for d in range(2):
                for c in range(NC):
                    i = dve.tensor_scalar(DIAG[:, d, c, :], IDN, DSK[d][:, c:c + 1], None, ALU.mult)
            i.then_inc(*mdve.did("diag"))
            dve.wait_ge(ld_ctx, 48)
            dve.wait_ge(*mdve.at("xn"))
            stats_all(mdve, CTX, M, "cstats", "cmv", "cvar")

            for d in range(2):
                pad = slice(0, DC - 1) if d == 0 else slice(T, T + DC - 1)
                dve.memset(XP[d][:, :, :, pad], 0.0).then_inc(*mdve.did("pad", d))
                dve.wait_ge(*mact.at("xp", d))
                dve.wait_ge(*mdve.at("pad", d))
                for kk in range(DC):
                    shift = kk if d == 0 else DC - 1 - kk
                    for c in range(NC):
                        src = XP[d][:, c, :, shift:shift + T]
                        dst = U[d][:, c, :].rearrange("p (b t) -> p b t", b=B)
                        if kk == 0:
                            i = dve.tensor_scalar(dst, src, CONVW[d][:, c, 0:1], CONVB[d][:, c:c + 1], ALU.mult, ALU.add)
                        else:
                            i = dve.scalar_tensor_tensor(dst, src, CONVW[d][:, c, kk:kk + 1], dst, ALU.mult, ALU.add)
                    i.then_inc(*mdve.did(("tap0", "tap1", "tap2", "conv")[kk], d))
                    dve.wait_ge(*mdve.at(("tap0", "tap1", "tap2", "conv")[kk], d))

            def parts(d):
                src, s3, res = bank(2, 2), S3[d], RES[d]
                dve.wait_ge(*mpe.at("bc", d))
                dve.tensor_copy(s3[0:96, :], src[0:96, :]).then_inc(*mdve.did("s3a", d))
                dve.wait_ge(*mdve.at("s3a", d))
                dve.tensor_tensor(res[0:64, :], src[0:64, :], s3[0:64, :], ALU.subtract).then_inc(*mdve.did("s3b", d))
                dve.wait_ge(*mdve.at("s3b", d))
                dve.tensor_copy(s3[0:64, :], res[0:64, :]).then_inc(*mdve.did("s3c", d))
                dve.wait_ge(*mdve.at("s3c", d))
                dve.tensor_tensor(res[0:32, :], res[0:32, :], s3[0:32, :], ALU.subtract).then_inc(*mdve.did("s3d", d))
                dve.wait_ge(*mdve.at("s3d", d))
                dve.tensor_copy(s3[0:32, :], res[0:32, :]).then_inc(*mdve.did("s3", d))

            parts(0)
            dve.wait_ge(*mpool.at("crstd"))
            norm_all(mdve, CTX, CTX, M, "cn")
            dve.wait_ge(*mdve.at("cn"))
            dve.tensor_tensor(CTX[:, :, :], CTX[:, :, :], row_b("gm", M), ALU.mult).then_inc(*mdve.did("cg"))
            dve.wait_ge(*mdve.at("cg"))
            dve.tensor_tensor(CTX[:, :, :], CTX[:, :, :], row_b("bm", M), ALU.add).then_inc(*mdve.did("cb"))
            parts(1)
            def poly0(d):
                dve.wait_ge(*mact.at("exp", d))
                dve.tensor_scalar(SPT[d], EXPV[d], 1.0 / 3.0, -0.5, ALU.mult, ALU.add).then_inc(*mdve.did("poly0", d))

            def poly(d):
                dve.wait_ge(*(mdve.at("poly1", 0) if d == 0 else mpool.at("poly1", 1)))
                dve.scalar_tensor_tensor(SPT[d], SPT[d], 1.0, EXPV[d], ALU.add, ALU.mult).then_inc(*mdve.did("poly", d))
                dve.tensor_scalar(SMALLE[d], EXPV[d], 2.0 ** -6, None, ALU.is_lt).then_inc(*mdve.did("small", d))

            def pick(d):
                dve.wait_ge(*mact.at("ln", d))
                dve.wait_ge(*mdve.at("small", d))
                dve.copy_predicated(SPL[d].rearrange("p c n -> p (c n)"), SMALLE[d], SPT[d])\
                   .then_inc(*mdve.did("pick", d))

            poly0(0)
            dve.wait_ge(*mdve.at("poly0", 0))
            dve.tensor_tensor(SPT[0], SPT[0], EXPV[0], ALU.mult).then_inc(*mdve.did("poly1", 0))
            poly(0)
            poly0(1)
            pick(0)
            poly(1)
            pick(1)
            dve.wait_ge(*mdve.at("pick", 1))
            for c in range(NC):
                i = dve.tensor_tensor(DELTA[1][:, c, :], SPR[1][:, c, :], SPL[1][:, c, :], ALU.add)
            i.then_inc(*mdve.did("delta", 1))
            dve.wait_ge(*mdve.at("delta", 1))
            dve.tensor_tensor(DU[1][:, 0, :], DELTA[1][:, 0, :], U[1][:, 0, :], ALU.mult).then_inc(*mdve.did("du", 1))
            dve.wait_ge(*mpe.at("y0", 0))
            dve.wait_ge(*mpool.at("delta", 0))
            for c in range(NC):
                i = dve.tensor_tensor(DU[0][:, c, :], DELTA[0][:, c, :], U[0][:, c, :], ALU.mult)
            i.then_inc(*mdve.did("du", 0))

            dav = DA.rearrange("p s c (b t) -> p (s c b) t", b=B)
            dve.memset(dav[:, :, 0:1], 0.0).then_inc(*mdve.did("edge", 0))
            for kx in ("bu0", "h0", "h1", "hc0"):
                dve.nop().then_inc(L[kx], CREDIT)
            for d in range(2):
                dve.wait_ge(*mdve.at("edge", d))
                order = slice(None) if d == 0 else slice(None, None, -1)
                base = d * DS + CREDIT

                def inputs_b(s, n, c=0):
                    dve.wait_ge(L["b_sb"], n + 1)
                    dve.wait_ge(L["yacc"], n - 3)
                    if c == 1:
                        dve.wait_ge(L["bu1"], n)
                    dve.tensor_tensor(HB[s % 4][:, c, :], DU[d][:, c, :], BS[:, s % 2, :], ALU.mult).then_inc(L[f"bu{c}"], 1)

                def recurrence(s, n):
                    for c in (1, 0):
                        h = HB[s][:, c, order]
                        dve.wait_ge(L[f"bu{c}"], n + 1)
                        dve.wait_ge(L[f"da{c}"], n + 1)
                        dve.tensor_tensor_scan(h, DA[:, s % 2, c, order], h, 0.0, ALU.mult, ALU.add).then_inc(L[f"h{c}"], 1)

                def states_c(s, n, c=0):
                    dve.wait_ge(L["c_sb"], n + 1)
                    dve.wait_ge(L[f"h{c}"], n + 1)
                    if c == 1:
                        dve.wait_ge(L["hc1"], n)
                    dve.tensor_tensor(HB[s][:, c, :], HB[s][:, c, :], CS[:, s % 2, :], ALU.mult).then_inc(L[f"hc{c}"], 1)

                inputs_b(0, base)
                with dve.Fori(0, DS // 4 - 1) as it:
                    for s in range(4):
                        recurrence(s, it * 4 + (s + base))
                        inputs_b(s + 1, it * 4 + (s + 1 + base))
                        states_c(s, it * 4 + (s + base))
                for s in range(4):
                    recurrence(s, base + DS - 4 + s)
                    if s < 3:
                        inputs_b(s + 1, base + DS - 4 + s + 1)
                    if s == 2:
                        inputs_b(3, base + DS - 1, 1)
                    states_c(s, base + DS - 4 + s)
                states_c(3, base + DS - 1, 1)
                if d == 0:
                    dve.wait_ge(L["h0"], CREDIT + DS)
                    dve.wait_ge(L["h1"], CREDIT + DS)
                    dve.memset(dav[:, :, T - 1:T], 0.0).then_inc(*mdve.did("edge", 1))
                    dve.tensor_tensor(X[:, :, :], X[:, :, :], row_b("ln_b"), ALU.add).then_inc(*mdve.did("xb"))
                dve.wait_ge(L["yacc"], CREDIT + (d + 1) * DS)
                for c in range(NC):
                    i = dve.tensor_tensor(ZS[:, d, c, :], bank(4 + 2 * c, 2), ZS[:, d, c, :], ALU.mult)
                i.then_inc(*mdve.did("y", d))

            for h in range(2):
                hs = slice(4 * h, 4 * h + 4)
                dve.wait_ge(*mpe.at("out", h))
                dve.tensor_tensor(XN[:, hs, :], XN[:, hs, :], bank(h).rearrange("p (b c) -> p b c", b=4), ALU.add)\
                   .then_inc(*mdve.did("h", h))
                dve.wait_ge(*mdve.at("h", h))
                stats_all(mdve, XN, 128, "hstats", "hmv", "hvar", h)
            for h in range(2):
                hs = slice(4 * h, 4 * h + 4)
                dve.wait_ge(*mpool.at("hrstd", h))
                norm_all(mdve, XN, XN, 128, "hn", h)
                dve.wait_ge(*mdve.at("hn", h))
                dve.tensor_tensor(XN[:, hs, :], XN[:, hs, :], row("ln_w").unsqueeze(1).to_broadcast([128, 4, D]),
                                  ALU.mult).then_inc(*mdve.did("hg", h))
                dve.wait_ge(*mdve.at("hg", h))
                dve.tensor_tensor(X[:, hs, :], X[:, hs, :], XN[:, hs, :], ALU.add).then_inc(*mdve.did("x", h))
            dve.wait_ge(*mdve.at("x", 1))

            def ln_step(S, W, step, b, v, src, before=None):
                if step == "stats":
                    if before is not None:
                        dve.wait_ge(*before.at("res", b))
                    dve.bn_stats(v["st"], src).then_inc(*S.did("stats", b))
                elif step == "mv":
                    dve.wait_ge(*S.at("stats", b))
                    dve.bn_aggr(v["mv"], v["st"]).then_inc(*S.did("mv", b))
                elif step == "var":
                    dve.wait_ge(*S.at("mv", b))
                    dve.tensor_scalar(v["var"], v["mv"][:, 1:2], EPS, None, ALU.add).then_inc(*S.did("var", b))
                elif step == "xn":
                    dve.wait_ge(*W.at("rstd", b))
                    dve.tensor_scalar(v["xn"], src, v["mv"][:, 0:1], v["rs"], ALU.subtract, ALU.mult)\
                       .then_inc(*S.did("xn", b))

            def ln2_step(S, W, step, b, v, src, before, dst=None, g=None, b_=None, last=None):
                if step == "stats2":
                    dve.wait_ge(*S.at(before, b))
                    dve.bn_stats(v["st2"], src).then_inc(*S.did("stats2", b))
                elif step == "mv2":
                    dve.wait_ge(*S.at("stats2", b))
                    dve.bn_aggr(v["mv2"], v["st2"]).then_inc(*S.did("mv2", b))
                elif step == "var2":
                    dve.wait_ge(*S.at("mv2", b))
                    dve.tensor_scalar(v["var2"], v["mv2"][:, 1:2], EPS, None, ALU.add).then_inc(*S.did("var2", b))
                elif step == "xn2":
                    dve.wait_ge(*W.at("rstd2", b))
                    dve.tensor_scalar(v["xn2"], src, v["mv2"][:, 0:1], v["rs2"], ALU.subtract, ALU.mult)\
                       .then_inc(*S.did("xn2", b))
                elif step == "l0":
                    dve.wait_ge(*W.at("rstd2", b))
                    dve.tensor_scalar(v["l1"], src, v["mv2"][:, 0:1], v["rs2"], ALU.subtract, ALU.mult)\
                       .then_inc(*S.did("l0", b))
                elif step == "l1":
                    dve.wait_ge(*S.at("l0", b))
                    dve.tensor_tensor(v["l1"], v["l1"], row(g), ALU.mult).then_inc(*S.did("l1", b))
                elif step == last:
                    dve.wait_ge(*S.at("l1", b))
                    dve.tensor_tensor(dst, v["l1"], row(b_), ALU.add).then_inc(*S.did(last, b))

            def softmax_step(S, P, A, step, k, w, ps, scores):
                heads, keys = ps.shape[1:]
                if step == "mx":
                    dve.wait_ge(*P.at(scores, k))
                    dve.tensor_reduce(w["mx"], ps, AX, ALU.max).then_inc(*S.did("mx", k))
                elif step == "sub":
                    dve.wait_ge(*S.at("mx", k))
                    after(dve, P, "pt", k - 3)
                    dve.tensor_tensor(w["p"] if len(w["p"].shape) == 3 else w["p"].rearrange("p (h m) -> p h m", h=heads),
                                      ps, w["mx"].unsqueeze(2).to_broadcast([128, heads, keys]), ALU.subtract)\
                       .then_inc(*S.did("sub", k))

            def narrow_heads(L_, step, n, v, w, keys):
                S, P = L_["dve"], L_["pe"]
                if step in ("mx", "sub"):
                    ps = PS[:, n % 3, 0:4 * keys].rearrange("p (h m) -> p h m", h=4)
                    softmax_step(S, P, L_["act"], step, n, w, ps, "sc")
                elif step == "pt":
                    dve.wait_ge(*P.at("pt", n))
                    after(dve, P, "pv", n - 3)
                    dve.tensor_copy(w["pt"][0:keys, :], bank(3 + n % 2)[0:keys, :]).then_inc(*S.did("pt", n))
                else:
                    o = bank(5 + n % 2)[:, 0:H0 * (HD0 + 1)].rearrange("p (h d) -> p h d", h=H0)
                    if step == "rz":
                        dve.wait_ge(*P.at("pv", 4 * n + 3))
                        dve.reciprocal(v["rz"].unsqueeze(2), o[:, :, HD0:HD0 + 1]).then_inc(*S.did("rz", n))
                    elif step == "o":
                        dve.wait_ge(*S.at("rz", n))
                        dve.tensor_tensor(v["o"].rearrange("p (h d) -> p h d", h=H0), o[:, :, 0:HD0],
                                          v["rz"].unsqueeze(2).to_broadcast([128, H0, HD0]), ALU.mult)\
                           .then_inc(*S.did("o", n))

            S, P = x0["dve"], x0["pe"]
            lg, top = SMALL[:, 0, :, :], SMALL[:, 1, :, :]
            for step, n in S.order:
                v, w = X0S[n % 4], X0U[n % 3]
                if step in ("stats", "mv", "var", "xn"):
                    ln_step(S, x0["pool"], step, n, v, X[:, n, :])
                elif step == "rope_a":
                    q_ps = PS[:, 7, 0:D].rearrange("p (h g d) -> p h g d", h=H0, g=2)
                    r1 = v["r1"].rearrange("p (h g d) -> p h g d", h=H0, g=2)
                    r2 = v["r2"].rearrange("p (h g d) -> p h g d", h=H0, g=2)
                    dve.wait_ge(*P.at("q", n))
                    for g in range(2):
                        cos = ROPE[:, 0, n, g, :].unsqueeze(1).to_broadcast([T, H0, 4])
                        sin = ROPE[:, 1, n, g, :].unsqueeze(1).to_broadcast([T, H0, 4])
                        dve.tensor_tensor(r1[:, :, g, :], q_ps[:, :, g, :], cos, ALU.mult)
                        ins = dve.tensor_tensor(r2[:, :, g, :], q_ps[:, :, 1 - g, :], sin, ALU.mult)
                    ins.then_inc(*S.did("rope_a", n))
                elif step == "rope":
                    dve.wait_ge(*S.at("rope_a", n))
                    dve.tensor_tensor(v["qr"], v["r1"], v["r2"], ALU.add).then_inc(*S.did("rope", n))
                elif step == "res":
                    dve.wait_ge(*P.at("wo", n))
                    dve.tensor_tensor(X[:, n, :], X[:, n, :], PS[:, 5 + n % 2, 384:512], ALU.add)\
                       .then_inc(*S.did("res", n))
                elif step in ("stats2", "mv2", "var2", "xn2"):
                    ln2_step(S, x0["pool"], step, n, v, X[:, n, :], "res")
                elif step == "lg":
                    dve.wait_ge(*P.at("gate", n))
                    dve.tensor_copy(lg[:, n, :], PS[:, 5 + n % 2, 0:E0]).then_inc(*S.did("lg", n))
                elif step == "max":
                    dve.wait_ge(*S.at("lg", n))
                    dve.max(top[:, n, :], lg[:, n, :]).then_inc(*S.did("max", n))
                elif step == "index":
                    dve.wait_ge(*S.at("max", n))
                    dve.max_index(TOPI[:, n, :], top[:, n, :], lg[:, n, :]).then_inc(*S.did("index", n))
                else:
                    narrow_heads(x0, step, n, v, w, M)
            dve.wait_ge(*S.at("index", B - 1))

            S, P = f0["dve"], f0["pe"]
            ti = SMALL[:, 2, :, :]
            dve.tensor_copy(ti, TOPI[:, :, :]).then_inc(*S.did("top_i"))
            w = SMALL[:, 3, :, :]
            dve.tensor_tensor(w[:, :, 0:1], top[:, :, 1:2], top[:, :, 0:1], ALU.subtract).then_inc(*S.did("dif"))
            dve.wait_ge(*f0["act"].at("top_exp"))
            dve.tensor_scalar(w[:, :, 2:3], w[:, :, 1:2], 1.0, None, ALU.add).then_inc(*S.did("den"))
            dve.wait_ge(*S.at("den"))
            dve.reciprocal(w[:, :, 3:4], w[:, :, 2:3]).then_inc(*S.did("w1"))
            dve.wait_ge(*S.at("w1"))
            dve.tensor_tensor(w[:, :, 4:5], w[:, :, 1:2], w[:, :, 3:4], ALU.mult).then_inc(*S.did("w2"))
            iota = IOTA.unsqueeze(1).to_broadcast([T, B, E0])
            for j, (step, stepw) in enumerate((("s1", "s1w"), ("s2", "s2w"))):
                dve.tensor_tensor(SMALL[:, 4 + j, :, :], iota, ti[:, :, j:j + 1].to_broadcast([T, B, E0]),
                                  ALU.is_equal).then_inc(*S.did(step))
            for j, (step, stepw) in enumerate((("s1", "s1w"), ("s2", "s2w"))):
                dve.wait_ge(*S.at("s2"))
                dve.tensor_tensor(SMALL[:, 4 + j, :, :], SMALL[:, 4 + j, :, :],
                                  w[:, :, 3 + j:4 + j].to_broadcast([T, B, E0]), ALU.mult).then_inc(*S.did(stepw))
            dve.wait_ge(*S.at("s2w"))
            dve.tensor_tensor(PROB, SMALL[:, 4, :, :], SMALL[:, 5, :, :], ALU.add).then_inc(*S.did("comb"))

            def moe_units(F, n, gated, last_step, finish=None):
                S, P = F["dve"], F["pe"]

                def acc(h, e):
                    dve.wait_ge(*P.at("y", h, e))
                    if (h, e) != (0, 0):
                        dve.wait_ge(*S.at("acc", *divmod(h * E0 + e - 1, E0)))
                    for j in range(4):
                        b = 4 * h + j
                        ins = dve.scalar_tensor_tensor(last_step[:, b, :], PS[:, 6 + e % 2, j * D:(j + 1) * D],
                                                       PROB[:, b, e:e + 1], last_step[:, b, :], ALU.mult, ALU.add)
                    ins.then_inc(*S.did("acc", h, e))

                def unit(step, k_):
                    if step == "end":
                        acc(1, E0 - 1)
                        return
                    h, e, c = units(n)[k_]
                    if gated:
                        if k_ >= 3:
                            ub = units(n)[k_ - 3]
                            dve.wait_ge(*P.at("y" if ub[2] == n - 1 else "yp", *(ub[:2] if ub[2] == n - 1 else ub)))
                        dve.wait_ge(*F["act"].at("silu", h, e, c))
                        dve.tensor_tensor(ACTB[:, k_ % 3, :], ACTS[:, k_ % 3, :], bank(2 * (k_ % 2) + 1), ALU.mult)\
                           .then_inc(*S.did("act", h, e, c))
                    if c == n - 1 and (h, e) != (0, 0):
                        prev = divmod(h * E0 + e - 1, E0)
                        acc(*prev)
                        if finish and prev[1] == E0 - 1:
                            finish(0)
                return unit

            dve.wait_ge(*S.at("comb"))
            f0_step = moe_units(f0, 2, True, X)

            bound = {p: float(np.log(p / (1 - p))) for p in (0.95, 0.85, 0.1, 0.25)}
            def a1_step(step, b):
                S, P, A = a1["dve"], a1["pe"], a1["act"]
                v = A1S[b % 6]
                if step == "stats":
                    dve.wait_ge(*f0["dve"].at("acc", b // (B // 2), E0 - 1))
                if step == "xn":
                    after(dve, P, "xt", b - 6)
                if step in ("stats", "mv", "var", "xn"):
                    ln_step(S, a1["pool"], step, b, v, X[:, b, :])
                elif step == "a":
                    dve.wait_ge(*P.at("s", b))
                    dve.tensor_scalar(v["a"], PS[:, A1BANK[b], 0:T], float(HD0 ** -0.5), None, ALU.mult).then_inc(*S.did("a", b))
                elif step == "g1":
                    dve.wait_ge(*S.at("a", b))
                    dve.tensor_scalar(v["r1"], v["a"], bound[0.95], None, ALU.is_gt).then_inc(*S.did("g1", b))
                elif step == "l1":
                    dve.wait_ge(*S.at("a", b))
                    dve.tensor_scalar(v["r2"], v["a"], bound[0.1], 2.0 / 7.0, ALU.is_lt, ALU.mult).then_inc(*S.did("l1", b))
                elif step == "g":
                    dve.wait_ge(*S.at("g1", b))
                    dve.scalar_tensor_tensor(v["r1"], v["a"], bound[0.85], v["r1"], ALU.is_gt, ALU.add)\
                       .then_inc(*S.did("g", b))
                elif step == "l":
                    dve.wait_ge(*S.at("l1", b))
                    dve.scalar_tensor_tensor(v["r2"], v["a"], bound[0.25], v["r2"], ALU.is_lt, ALU.add)\
                       .then_inc(*S.did("l", b))
                elif step == "ls":
                    dve.wait_ge(*S.at("l", b))
                    dve.tensor_scalar(v["r2"], v["r2"], -0.7, 1.0, ALU.mult, ALU.add).then_inc(*S.did("ls", b))
                elif step == "m":
                    dve.wait_ge(*S.at("g", b))
                    dve.wait_ge(*S.at("ls", b))
                    dve.scalar_tensor_tensor(v["r1"], v["r1"], 0.5, v["r2"], ALU.mult, ALU.add).then_inc(*S.did("m", b))
                elif step == "am":
                    dve.wait_ge(*S.at("m", b))
                    dve.tensor_tensor(v["a"], v["a"], v["r1"], ALU.mult).then_inc(*S.did("am", b))
                elif step == "mx":
                    dve.wait_ge(*S.at("am", b))
                    dve.tensor_reduce(v["mx"], v["a"], AX, ALU.max).then_inc(*S.did("mx", b))
                elif step == "nmx":
                    dve.wait_ge(*S.at("mx", b))
                    dve.tensor_scalar(v["mx"], v["mx"], -1.0, None, ALU.mult).then_inc(*S.did("nmx", b))
                elif step == "rz":
                    dve.wait_ge(*A.at("p", b))
                    dve.reciprocal(v["rz"], v["z"]).then_inc(*S.did("rz", b))
                elif step == "y":
                    dve.wait_ge(*P.at("out", b))
                    dve.wait_ge(*S.at("rz", b))
                    dve.scalar_tensor_tensor(v["y"], PS[:, A1BANK[b], 0:D], v["rz"], X[:, b, :], ALU.mult, ALU.add)\
                       .then_inc(*S.did("y", b))
                elif step == "res":
                    dve.wait_ge(*S.at("y", b))
                    dve.tensor_tensor(X[:, b, :], v["y"], row("a1_bproj"), ALU.add).then_inc(*S.did("res", b))

            def x1_step(step, n):
                S, P, A = x1["dve"], x1["pe"], x1["act"]
                if (step, n) == ("stats", 0):
                    dve.wait_ge(*f0["dve"].at("acc", 1, E0 - 1))
                    for v in X1S:
                        dve.memset(v["va"][:, :, HD1:HD1 + 1], 1.0)
                        ins = dve.memset(v["vb"][:, :, HD1:HD1 + 1], 1.0)
                    ins.then_inc(ones, 1)
                v, w = X1S[n % 2], X1U[n % 3]
                if step in ("stats", "mv", "var", "xn"):
                    ln_step(S, x1["pool"], step, n, v, X[:, n, :], a1["dve"])
                elif step in ("stats2", "mv2", "var2", "l0", "l1", "l2"):
                    ln2_step(S, x1["pool"], step, n, v, v["xn"], "xn", v["l2"], "gl", "bl", "l2")
                elif step in ("va", "vb"):
                    p, bk = (M, 7) if step == "va" else (T, 6)
                    dve.wait_ge(*P.at(step, n))
                    after(dve, P, "o", 4 * (n - 2) + 3)
                    dve.tensor_copy(v[step][0:p, :, 0:HD1], bank(bk)[0:p, :].rearrange("p (h d) -> p h d", h=H1))\
                       .then_inc(*S.did(step, n))
                elif step in ("mx", "sub"):
                    ps = PS[:, n % 2, 0:2 * J1].rearrange("p (h m) -> p h m", h=2)
                    softmax_step(S, P, A, step, n, w, ps, "s")
                elif step in ("rz0", "o0", "rz1", "o1"):
                    g = int(step[-1])
                    o = PS[:, 4 + g, 0:4 * (HD1 + 1)].rearrange("p (h d) -> p h d", h=4)
                    rz = v["rz"][:, 4 * g:4 * g + 4].unsqueeze(2)
                    if step[0] == "r":
                        dve.wait_ge(*P.at("o", 4 * n + 2 * g + 1))
                        dve.reciprocal(rz, o[:, :, HD1:HD1 + 1]).then_inc(*S.did(step, n))
                    else:
                        dve.wait_ge(*S.at(f"rz{g}", n))
                        after(dve, P, "ot", n - 2)
                        dve.tensor_tensor(v["o"][:, 256 * g:256 * g + 256].rearrange("p (h d) -> p h d", h=4),
                                          o[:, :, 0:HD1], rz.to_broadcast([128, 4, HD1]), ALU.mult)\
                           .then_inc(*S.did(step, n))
                elif step == "res":
                    dve.wait_ge(*P.at("out", n))
                    dve.tensor_tensor(X[:, n, :], X[:, n, :], PS[:, 5, 0:D], ALU.add).then_inc(*S.did("res", n))

            def g1_step(step, n):
                S, P, A = g1["dve"], g1["pe"], g1["act"]
                if (step, n) == ("stats", 0):
                    for v in G1S:
                        dve.memset(v["xp"][:, 0:1], 0.0)
                        dve.memset(v["xp"][:, T + 1:T + 2], 0.0)
                        ins = dve.memset(v["v"][:, :, HD0:HD0 + 1], 1.0)
                    ins.then_inc(ones, 1)
                v, w = G1S[n % 4], G1U[n % 3]
                if step in ("stats", "mv", "var", "xn"):
                    ln_step(S, g1["pool"], step, n, v, X[:, n, :], x1["dve"])
                elif step == "y":
                    dve.wait_ge(*P.at("y", n))
                    dve.tensor_tensor(v["y"], PS[:, 7, 0:D], row("conv_b"), ALU.add).then_inc(*S.did("y", n))
                elif step == "h":
                    dve.wait_ge(*P.at("wo", n))
                    dve.tensor_tensor(v["y"], v["y"], PS[:, 5 + n % 2, 384:512], ALU.add).then_inc(*S.did("h", n))
                elif step in ("stats2", "mv2", "var2", "l0", "l1", "xa"):
                    ln2_step(S, g1["pool"], step, n, v, v["y"], "h", XN1[:, n, :], "ln1_g", "ln1_b", "xa")
                elif step == "lg":
                    dve.wait_ge(*P.at("gate", n))
                    dve.tensor_tensor(SMALL[:, 0, n, :], PS[:, 5 + n % 2, 0:E1], row("gate_b", E1), ALU.add).then_inc(*S.did("lg", n))
                else:
                    narrow_heads(g1, step, n, v, w, T)
            overlapped("dve", {"f0": f0_step, "a1": a1_step, "x1": x1_step, "g1": g1_step})
            dve.wait_ge(*g1["dve"].at("lg", B - 1))

            F = f1
            S, P = F["dve"], F["pe"]
            lg = SMALL[:, 0, :, :]
            dve.tensor_reduce(SMALL[:, 1, :, 0], lg, AX, ALU.max).then_inc(*S.did("gmx"))
            dve.wait_ge(*S.at("gmx"))
            dve.tensor_tensor(lg, lg, SMALL[:, 1, :, 0:1].to_broadcast([T, B, E1]), ALU.subtract).then_inc(*S.did("gsub"))
            dve.wait_ge(*F["act"].at("gexp"))
            dve.tensor_reduce(SMALL[:, 1, :, 1], lg, AX, ALU.add).then_inc(*S.did("gsum"))
            dve.wait_ge(*S.at("gsum"))
            dve.reciprocal(SMALL[:, 1, :, 2], SMALL[:, 1, :, 1]).then_inc(*S.did("grz"))
            dve.wait_ge(*S.at("grz"))
            dve.tensor_tensor(PROB, lg, SMALL[:, 1, :, 2:3].to_broadcast([T, B, E1]), ALU.mult).then_inc(*S.did("prob"))
            dve.tensor_tensor(X[:, :, :], X[:, :, :], row_b("ln2_b"), ALU.add).then_inc(*S.did("b"))
            dve.wait_ge(*P.at("b2"))
            dve.tensor_tensor(XA.rearrange("p b c -> p (b c)"), XN1.rearrange("p b c -> p (b c)"), bank(4, 2), ALU.add)\
               .then_inc(*S.did("b2"))
            dve.wait_ge(*S.at("b2"))

            def finish(h):
                dve.wait_ge(*S.at("acc", h, E0 - 1))
                stats_all(S, XA, 128, "stats", "mv", "var", h)
                dve.wait_ge(*F["pool"].at("rstd", h))
                norm_all(S, XA, XA, 128, "xn", h)
                xa, x_ = (t[:, 4 * h:4 * h + 4, :] for t in (XA, X))
                dve.wait_ge(*S.at("xn", h))
                dve.tensor_tensor(xa, xa, row("ln2_g").unsqueeze(1).to_broadcast([T, 4, D]), ALU.mult)\
                   .then_inc(*S.did("g", h))
                dve.wait_ge(*S.at("g", h))
                dve.tensor_tensor(FIN[:, 4 * h:4 * h + 4, :], xa, x_, ALU.add).then_inc(*S.did("fin", h))

            f1_step = moe_units(f1, 4, False, XA, finish)
            for k in range(len(units(4))):
                f1_step("unit", k)
            f1_step("end", 0)
            finish(1)

        @block.gpsimd
        def _(pool):
            def rsqrt_all(S, wait, p, step, cols_=slice(0, B), *key):
                pool.wait_ge(*wait)
                pool.tensor_tensor(RS[0:p, cols_], RS[0:p, cols_], HALFNEG[0:p, cols_], ALU.pow).then_inc(*S.did(step, *key))

            rsqrt_all(mpool, mdve.at("var"), 128, "rstd")
            rsqrt_all(mpool, mdve.at("cvar"), M, "crstd")
            pool.wait_ge(*mdve.at("poly0", 1))
            pool.tensor_tensor(SPT[1], SPT[1], EXPV[1], ALU.mult).then_inc(*mpool.did("poly1", 1))
            pool.wait_ge(*mdve.at("pick", 0))
            for c in range(NC):
                i = pool.tensor_tensor(DELTA[0][:, c, :], SPR[0][:, c, :], SPL[0][:, c, :], ALU.add)
            i.then_inc(*mpool.did("delta", 0))
            pool.wait_ge(*mdve.at("delta", 1))
            pool.tensor_tensor(DU[1][:, 1, :], DELTA[1][:, 1, :], U[1][:, 1, :], ALU.mult).then_inc(*mpool.did("du", 1))
            for k in ("bu1", "hc1"):
                pool.nop().then_inc(L[k], CREDIT)
            for d in range(2):
                base = d * DS + CREDIT

                def inputs_b(s, n):
                    pool.wait_ge(L["b_sb"], n + 1)
                    pool.wait_ge(L["yacc"], n - 3)
                    pool.tensor_tensor(HB[s % 4][:, 1, :], DU[d][:, 1, :], BS[:, s % 2, :], ALU.mult).then_inc(L["bu1"], 1)

                def states_c(s, n):
                    pool.wait_ge(L["c_sb"], n + 1)
                    pool.wait_ge(L["h1"], n + 1)
                    pool.tensor_tensor(HB[s][:, 1, :], HB[s][:, 1, :], CS[:, s % 2, :], ALU.mult).then_inc(L["hc1"], 1)

                pool.wait_ge(*(mdve.at("du", 0) if d == 0 else mpool.at("du", 1)))
                if d == 1:
                    pool.wait_ge(L["bu1"], base)
                    pool.wait_ge(L["hc1"], base)
                inputs_b(0, base)
                with pool.Fori(0, DS // 4 - 1) as it:
                    for s in range(4):
                        inputs_b(s + 1, it * 4 + (s + 1 + base))
                        states_c(s, it * 4 + (s + base))
                for s in range(3):
                    if s < 2:
                        inputs_b(s + 1, base + DS - 4 + s + 1)
                    states_c(s, base + DS - 4 + s)
            for h in range(2):
                rsqrt_all(mpool, mdve.at("hvar", h), 128, "hrstd", slice(4 * h, 4 * h + 4), h)

            def layer(L_, slots_, groups=None, keys=None, keys_src=None):
                S, DV = L_["pool"], L_["dve"]

                def take(step, n):
                    v = slots_[n % len(slots_)]
                    if step == "rstd":
                        pool.wait_ge(*DV.at("var", n))
                        pool.tensor_tensor(v["rs"], v["var"], HALFNEG[:, 0:1], ALU.pow).then_inc(*S.did("rstd", n))
                    elif step == "rstd2":
                        pool.wait_ge(*DV.at("var2", n))
                        pool.tensor_tensor(v["rs2"], v["var2"], HALFNEG[:, 0:1], ALU.pow).then_inc(*S.did("rstd2", n))
                    elif step == "kx":
                        b, g = divmod(n, 4)
                        if keys == T and g == 0:
                            pool.wait_ge(*L_["act"].at("k", b))
                        after(pool, L_["pe"], "sc", n - 3)
                        pool.tensor_tensor(groups[n % 3]["kx"], keys_src(b).unsqueeze(1).to_broadcast([128, 4, keys]),
                                           MASK[:, 4 * g:4 * g + 4].unsqueeze(2).to_broadcast([128, 4, keys]), ALU.mult)\
                            .then_inc(*S.did("kx", n))
                return take

            x0_step = layer(x0, X0S, X0U, M, lambda b: KT0[:, b, :])
            for step, n in x0["pool"].order:
                x0_step(step, n)
            overlapped("pool", {"a1": layer(a1, A1S), "x1": layer(x1, X1S),
                                "g1": layer(g1, G1S, G1U, T, lambda b: G1S[b % 4]["kt"])})
            S = f1["pool"]
            for h in range(2):
                rsqrt_all(S, f1["dve"].at("var", h), 128, "rstd", slice(4 * h, 4 * h + 4), h)

        @block.scalar
        def _(act):
            act.wait_ge(ld_c, 48)
            act.activation(NEGA[:, :, :, :].rearrange("p a b c -> p (a b c)"), ALOG, ACT.Exp)\
               .then_inc(*mact.did("nega"))
            act.wait_ge(*mpe.at("xnt"))
            act.activation(XNT[:, :, :].rearrange("p b t -> p (b t)"), bank(6, 2), ACT.Copy).then_inc(*mact.did("xnt"))
            act.wait_ge(*mdve.at("rope7"))
            act.activation(SMALL[:, 3, :, 0:4], SMALL[:, 1, :, 0:4], ACT.Abs).then_inc(*mact.did("sin_abs"))
            act.activation(SMALL[:, 6, :, 0:4], SMALL[:, 1, :, 0:4], ACT.Sin)
            act.wait_ge(*mdve.at("rope8"))
            act.activation(SMALL[:, 5, :, 0:4], SMALL[:, 3, :, 0:4], ACT.Sin).then_inc(*mact.did("sin"))
            for k in ("b_sb", "c_sb", "da0", "da1"):
                act.nop().then_inc(L[k], CREDIT)
            for d in range(2):
                off = DC - 1 if d == 0 else 0
                for c in range(NC):
                    act.wait_ge(*mpe.at(f"xz{c}", d))
                    i = act.activation(XP[d][:, c, :, off:off + T], bank(2 * c, 2).rearrange("p (b t) -> p b t", b=B),
                                       ACT.Copy)
                i.then_inc(*mact.did("xp", d))
                for c in range(NC):
                    act.wait_ge(*mpe.at(f"xz{2 + c}", d))
                    i = act.activation(ZS[:, d, c, :], bank(4 + 2 * c, 2), ACT.Silu)
                i.then_inc(*mact.did("zs", d))
            for d in range(2):
                act.wait_ge(*mdve.at("conv", d))
                for c in range(NC):
                    i = act.activation(U[d][:, c, :], U[d][:, c, :], ACT.Silu)
                i.then_inc(*mact.did("u", d))
            for d in range(2):
                act.wait_ge(*mpe.at("low", d))
                act.activation(DTS[d][0:DR, :], bank(0, 2)[0:DR, :], ACT.Copy).then_inc(*mact.did("dts", d))
                for c in range(NC):
                    act.wait_ge(*mpe.at(f"dt{c}", d))
                    act.activation(SPR[d][:, c, :], bank(4 + 2 * c, 2), ACT.Relu, bias=DTB[d][:, c:c + 1])\
                       .then_inc(*mact.did(f"relu{c}", d))
                    act.activation(SPE[d][:, c, :], bank(4 + 2 * c, 2), ACT.Abs, bias=DTB[d][:, c:c + 1])\
                       .then_inc(*mact.did(f"abs{c}", d))
                act.wait_ge(*mact.at("abs1", d))
                for c in range(NC):
                    i = act.activation(SPE[d][:, c, :], SPE[d][:, c, :], ACT.Exp, scale=-1.0)
                i.then_inc(*mact.did("exp", d))
            for d in range(2):
                act.wait_ge(*mact.at("exp", d))
                act.wait_ge(*mdve.at("s3", d))
                for c in range(NC):
                    i = act.activation(SPL[d][:, c, :], SPE[d][:, c, :], ACT.Ln, bias=ONES[:, 0:1])
                i.then_inc(*mact.did("ln", d))
            act.wait_ge(*mpe.at("ct"))
            act.activation(KVT[:, :, 0:M], bank(0, 2).rearrange("p (b t) -> p b t", b=B)[:, :, 0:M], ACT.Copy)\
               .then_inc(*mact.did("ct"))
            act.wait_ge(*mpe.at("kt0"))
            for g in range(2):
                i = act.activation(KT0[:, 4 * g:4 * g + 4, :].rearrange("p b m -> p (b m)"), bank(2 + g)[:, 0:4 * M],
                                   ACT.Identity, bias=X0BK)
            i.then_inc(*mact.did("kt0"))
            act.wait_ge(*mpe.at("v0"))
            for g in range(2):
                i = act.activation(V0[:, 4 * g:4 * g + 4, :, 0:HD0].rearrange("p b h d -> p (b h) d"),
                                   bank(g)[0:M, :].rearrange("p (h d) -> p h d", d=HD0), ACT.Copy)
            i.then_inc(*mact.did("v0"))
            for d in range(2):
                act.wait_ge(*mdve.at("edge", d))
                cols_ = slice(1, T) if d == 0 else slice(0, T - 1)
                with act.Fori(0, DS // 4) as it:
                    for s in range(4):
                        n = it * 4 + (s + d * DS + CREDIT)
                        act.wait_ge(L["b_ps"], it * 4 + (s + d * DS + 1))
                        act.wait_ge(L["bu0"], n - 1)
                        act.wait_ge(L["bu1"], n - 1)
                        act.activation(BS[:, s % 2, :], bank(0, 2), ACT.Copy).then_inc(L["b_sb"], 1)
                        for c in (1, 0):
                            act.wait_ge(L[f"h{c}"], n - 1)
                            act.activation(DA[:, s % 2, c, :].rearrange("p (b t) -> p b t", b=B)[:, :, cols_],
                                           DELTA[d][:, c, :].rearrange("p (b t) -> p b t", b=B)[:, :, cols_], ACT.Exp,
                                           scale=NEGA[:, d, c, bass.ds(it * 4 + s, 1)]).then_inc(L[f"da{c}"], 1)
                        act.wait_ge(L["c_ps"], it * 4 + (s + d * DS + 1))
                        act.wait_ge(L["hc0"], n - 1)
                        act.wait_ge(L["hc1"], n - 1)
                        act.activation(CS[:, s % 2, :], bank(2, 2), ACT.Copy).then_inc(L["c_sb"], 1)

            def copy(L_, step, n, dst, src, func=ACT.Copy, wait=None, **k):
                act.wait_ge(*L_["pe"].at(wait or step, n))
                act.activation(dst, src, func, **k).then_inc(*L_["act"].did(step, n))

            def exp(L_, k, p, scale):
                act.wait_ge(*L_["dve"].at("sub", k))
                act.activation(p, p, ACT.Exp, scale=scale).then_inc(*L_["act"].did("p", k))

            act.wait_ge(*mdve.at("x", 1))
            for step, n in x0["act"].order:
                v, w = X0S[n % 4], X0U[n % 3]
                if step == "p":
                    exp(x0, n, w["p"], float(1 / np.sqrt(HD0)))
                elif step == "pt":
                    after(act, x0["pe"], "pv", n - 3)
                    copy(x0, step, n, w["pt"][0:M, :], bank(3 + n % 2)[0:M, :])
                elif step == "ot":
                    copy(x0, step, n, v["ot"], PS[:, 5 + n % 2, 256:384])
                elif step == "xt2":
                    copy(x0, step, n, XNT[:, n, :], PS[:, 5 + n % 2, 0:T])
                else:
                    copy(x0, step, n, v[step], PS[:, 7, 0:T])
            S, P = f0["act"], f0["pe"]
            act.wait_ge(*f0["dve"].at("dif"))
            act.activation(SMALL[:, 3, :, 1:2], SMALL[:, 3, :, 0:1], ACT.Exp).then_inc(*S.did("top_exp"))

            def f0_step(step, k):
                u = units(2)[k]
                act.wait_ge(*f0["pe"].at("hg", *u))
                if k >= 3:
                    act.wait_ge(*f0["dve"].at("act", *units(2)[k - 3]))
                act.activation(ACTS[:, k % 3, :], bank(2 * (k % 2)), ACT.Silu).then_inc(*f0["act"].did("silu", *u))

            def a1_step(step, b):
                v = A1S[b % 6]
                if step == "xt":
                    copy(a1, step, b, v["xt"], PS[:, A1BANK[b], 0:T])
                elif step in ("q", "k"):
                    i = "qk".index(step)
                    copy(a1, step, b, v[step + "t"], PS[:, A1BANK[b], i * T:(i + 1) * T], ACT.Identity, "qkv", bias=A1B[:, i:i + 1])
                elif step == "v":
                    copy(a1, step, b, v["v"], PS[:, A1BANK[b], 2 * D:3 * D], wait="qkv")
                elif step == "p":
                    act.wait_ge(*a1["dve"].at("nmx", b))
                    act.activation(v["p"], v["a"], ACT.Exp, bias=v["mx"], accum_out=v["z"]).then_inc(*a1["act"].did("p", b))
                elif step == "pt":
                    copy(a1, step, b, v["pt"], PS[:, A1BANK[b], 0:T])
                elif step == "o":
                    copy(a1, step, b, v["ot"], PS[:, A1BANK[b], 0:T])
            def x1_step(step, n):
                v, w = X1S[n % 2], X1U[n % 3]
                if step == "lt":
                    copy(x1, step, n, KVT[:, n, M:J1], PS[:, 6, 0:T])
                elif step == "q":
                    after(act, x1["pe"], "s", 4 * (n - 2) + 3)
                    copy(x1, step, n, v["qt"].rearrange("p c t -> p (c t)"), bank(6))
                elif step in ("k0", "k1"):
                    g = int(step[-1])
                    after(act, x1["pe"], "s", 4 * (n - 2) + 3)
                    copy(x1, step, n, v["kt"][:, 2 * g:2 * g + 2, :].rearrange("p c j -> p (c j)"), bank(7 - g)[:, 0:2 * J1])
                elif step == "p":
                    exp(x1, n, w["p"].rearrange("p h j -> p (h j)"), float(HD1 ** 0.5))
                elif step == "pt":
                    act.wait_ge(*x1["pe"].at("pt", n))
                    after(act, x1["pe"], "o", n - 3)
                    act.activation(w["pta"].rearrange("p h t -> p (h t)")[0:M, :], bank(2 + n % 2)[0:M, 0:2 * T], ACT.Copy)
                    copy(x1, step, n, w["ptb"].rearrange("p h t -> p (h t)"), bank(2 + n % 2)[:, 2 * T:4 * T])
                elif step == "ot":
                    after(act, x1["pe"], "out", n - 2)
                    copy(x1, step, n, v["ot"].rearrange("p c t -> p (c t)"), bank(5))
            def g1_step(step, n):
                v, w = G1S[n % 4], G1U[n % 3]
                if step == "xt":
                    copy(g1, step, n, v["xp"][:, 1:T + 1], PS[:, 7, 0:T])
                elif step == "yt":
                    copy(g1, step, n, v["yt"], PS[:, 7, 0:T])
                elif step in ("q", "k"):
                    i = "qk".index(step)
                    copy(g1, step, n, v[step + "t"], PS[:, 7, i * T:(i + 1) * T], ACT.Identity, "qkv", bias=F1B[:, i:i + 1])
                elif step == "v":
                    copy(g1, step, n, v["v"][:, :, 0:HD0], PS[:, 7, 2 * D:3 * D].rearrange("p (h d) -> p h d", h=H0), wait="qkv")
                elif step == "p":
                    exp(g1, n, w["p"], float(1 / np.sqrt(HD0)))
                elif step == "pt":
                    after(act, g1["pe"], "pv", n - 3)
                    copy(g1, step, n, w["pt"], bank(3 + n % 2))
                elif step == "ot":
                    copy(g1, step, n, v["ot"], PS[:, 5 + n % 2, 256:384])
                elif step == "xat":
                    copy(g1, step, n, XAT1[:, n, :], PS[:, 5 + n % 2, 0:T])
            overlapped("act", {"f0": f0_step, "a1": a1_step, "x1": x1_step, "g1": g1_step})
            S, P = f1["act"], f1["pe"]
            act.wait_ge(*f1["dve"].at("gsub"))
            act.activation(SMALL[:, 0, :, :], SMALL[:, 0, :, :], ACT.Exp).then_inc(*S.did("gexp"))
            for k, (h, e, c) in enumerate(units(4)):
                if k == 5:
                    act.wait_ge(*P.at("pt"))
                    act.activation(PROBT[0:E1, :, :].rearrange("p b t -> p (b t)"), bank(4, 2)[0:E1, :], ACT.Copy)\
                       .then_inc(*S.did("pt"))
                act.wait_ge(*P.at("hg", h, e, c))
                if k >= 4:
                    ub = units(4)[k - 4]
                    act.wait_ge(*P.at("y" if ub[2] == 3 else "yp", *(ub[:2] if ub[2] == 3 else ub)))
                act.activation(ACTB[:, k % 4, :], bank(k % 4), ACT.Relu, bias=B1[:, e, c:c + 1])\
                   .then_inc(*S.did("relu", h, e, c))

        @block.tensor
        def _(pe):
            def mm(out_, lhs, rhs, start=True, stop=True, **k):
                return pe.matmul(out_, lhs, rhs, start=start, stop=stop, **k)

            def bias(out_, name, n=D, p=128):
                mm(out_, ONES[0:1, 0:p], row(name, n, 1), True, False)

            pe.wait_ge(ld_x, 32)
            pe.wait_ge(*mdve.at("xn"))
            for b in range(B):
                i = pe.transpose(PS[:, 6 + b // 4, (b % 4) * T:(b % 4 + 1) * T], XN[:, b, :], IDN)
            i.then_inc(*mpe.did("xnt"))
            pe.wait_ge(ld_m, 32)
            pe.wait_ge(*mact.at("xnt"))
            pe.nop().then_inc(L["yacc"], CREDIT)
            xnt = XNT[:, :, :].rearrange("p b t -> p (b t)")
            for d in range(2):
                for c in range(4):
                    if d:
                        pe.wait_ge(*mact.at("xp" if c < NC else "zs", 0))
                    for h in range(2):
                        i = mm(bank(2 * c + h), WIN[:, d, c * 128:(c + 1) * 128], xnt[:, h * HALF:(h + 1) * HALF])
                    i.then_inc(*mpe.did(f"xz{c}", d))
            for d in range(2):
                pe.wait_ge(*mact.at("u", d))
                if d:
                    pe.wait_ge(*mact.at("dts", 0))
                    pe.wait_ge(*mdve.at("s3", 0))
                else:
                    pe.wait_ge(*mact.at("xp", 1))
                for h in range(2):
                    for c in range(NC):
                        i = mm(bank(2 + h)[0:96, :], WBC[:, d, c, :], U[d][:, c, h * HALF:(h + 1) * HALF],
                               c == 0, c == NC - 1)
                i.then_inc(*mpe.did("bc", d))
                for h in range(2):
                    for c in range(NC):
                        i = mm(bank(h)[0:DR, :], WDT[:, d, c, :], U[d][:, c, h * HALF:(h + 1) * HALF], c == 0, c == NC - 1)
                i.then_inc(*mpe.did("low", d))
                pe.wait_ge(*mact.at("dts", d))
                if d == 0:
                    pe.wait_ge(*mact.at("zs", 1))
                for c in range(NC):
                    if d:
                        pe.wait_ge(*mact.at(f"abs{c}", 0))
                    for h in range(2):
                        i = mm(bank(4 + 2 * c + h), DTW[:, d, c * 128:(c + 1) * 128], DTS[d][0:DR, h * HALF:(h + 1) * HALF])
                    i.then_inc(*mpe.did(f"dt{c}", d))
            pe.wait_ge(*mdve.at("cb"))
            for b in range(B):
                i = pe.transpose(PS[:, b // 4, (b % 4) * T:(b % 4) * T + M], CTX[:, b, :], IDN[0:M, 0:M])
            i.then_inc(*mpe.did("ct"))
            pe.wait_ge(ld_ctx, 48)
            pe.wait_ge(*mdve.at("s3", 1))
            for g in range(2):
                i = mm(bank(2 + g)[:, 0:4 * M], X0K, CTXT[:, 4 * g:4 * g + 4, :].rearrange("p b m -> p (b m)"))
            i.then_inc(*mpe.did("kt0"))
            pe.wait_ge(*mact.at("abs1", 1))
            pe.wait_ge(*mdve.at("diag"))
            for d in range(2):
                base = d * DS + CREDIT

                def start_y():
                    for c in range(NC):
                        for h in range(2):
                            i = mm(bank(4 + 2 * c + h), DIAG[:, d, c, :], U[d][:, c, h * HALF:(h + 1) * HALF], True, False)
                    i.then_inc(*mpe.did("y0", d))

                def row_bc(k, st, n):
                    off, ps = (0, 0) if k == "b" else (DS, 2)
                    pe.wait_ge(L[f"{k}_sb"], n)
                    for h in range(2):
                        ins = mm(bank(ps + h), SEL[:, bass.ds(st + off, 1)].to_broadcast([128, 128]),
                                 S3[d][:, h * HALF:(h + 1) * HALF])
                    ins.then_inc(L[f"{k}_ps"], 1)

                def rows_bc(st, n):
                    row_bc("b", st, n)
                    row_bc("c", st, n)

                def sum_y(s, n, stop=False):
                    for c in range(NC):
                        pe.wait_ge(L[f"hc{c}"], n + 1)
                        for h in range(2):
                            ins = mm(bank(4 + 2 * c + h), IDN, HB[s][:, c, h * HALF:(h + 1) * HALF], False, stop)
                    ins.then_inc(L["yacc"], 1)

                if d == 0:
                    start_y()
                    pe.wait_ge(ld_c, 48)
                    pe.wait_ge(*mact.at("ct"))
                    for b in range(B):
                        o = PS[0:M, b // 4, (b % 4) * D:(b % 4 + 1) * D]
                        bias(o, "x0_bv", p=M)
                        i = mm(o, CTXT[:, b, :], X0V, False, True)
                    i.then_inc(*mpe.did("v0"))
                    pe.wait_ge(*mact.at("v0"))
                rows_bc(0, base)
                row_bc("b", 1, base + 1)
                if d == 1:
                    pe.wait_ge(*mdve.at("y", 0))
                    start_y()
                row_bc("c", 1, base + 1)
                with pe.Fori(0, DS // 4 - 1) as it:
                    for s in range(4):
                        rows_bc(it * 4 + (s + 2), it * 4 + (s + 2 + base))
                        sum_y(s, it * 4 + (s + base))
                for s in range(4):
                    if s < 2:
                        rows_bc(DS - 2 + s, base + DS - 2 + s)
                    if d == 1 and s == 2:
                        pe.wait_ge(L["b_sb"], base + DS)
                        for b in range(B):
                            for c in range(NC):
                                mm(PS[:, b // 4, (b % 4) * D:(b % 4 + 1) * D], ZS[:, 0, c, b * T:(b + 1) * T], WOUT[:, 0, c, :],
                                   b % 4 == 0 and c == 0, False, skip_group_check=True)
                    sum_y(s, base + DS - 4 + s, s == 3)
            pe.wait_ge(*mdve.at("y", 1))
            for b in range(B):
                for c in range(NC):
                    i = mm(PS[:, b // 4, (b % 4) * D:(b % 4 + 1) * D], ZS[:, 1, c, b * T:(b + 1) * T], WOUT[:, 1, c, :],
                           False, b % 4 == 3 and c == NC - 1, skip_group_check=True)
                if b % 4 == 3:
                    i.then_inc(*mpe.did("out", b // 4))

            def turn(S, step, n, out_, src, wait):
                pe.wait_ge(*wait)
                pe.transpose(out_, src, IDN).then_inc(*S.did(step, n))

            def narrow_heads(L_, step, n, v, w, keys, values, w_out, b_out, bank_free):
                S, A, DV = L_["pe"], L_["act"], L_["dve"]

                def turned(k):
                    return (DV if ("pt", k) in DV.value else A).at("pt", k)

                if step == "sc":
                    if n % 4 == 0:
                        for k in ("qt",) if keys == M else ("q", "k", "v"):
                            pe.wait_ge(*A.at(k, n // 4))
                    pe.wait_ge(*L_["pool"].at("kx", n))
                    after(pe, DV, "sub", n - 3)
                    mm(bank(n % 3)[:, 0:4 * keys], v["qt"], w["kx"].rearrange("p h m -> p (h m)")).then_inc(*S.did("sc", n))
                elif step == "pt":
                    pe.wait_ge(*A.at("p", n))
                    if n >= 2:
                        pe.wait_ge(*turned(n - 2))
                    for h in range(4):
                        ins = pe.transpose(PS[0:keys, 3 + n % 2, h * T:(h + 1) * T], w["p"][:, h * keys:(h + 1) * keys], IDN)
                    ins.then_inc(*S.did("pt", n))
                elif step == "pv":
                    b, g = divmod(n, 4)
                    if g == 0:
                        after(pe, DV, bank_free, b - 2)
                    pe.wait_ge(*turned(n))
                    for h in range(4):
                        o = (4 * g + h) * (HD0 + 1)
                        ins = mm(PS[:, 5 + b % 2, o:o + HD0 + 1], w["pt"][0:keys, h * T:(h + 1) * T], values[:, 4 * g + h, :])
                    ins.then_inc(*S.did("pv", n))
                elif step == "ot":
                    turn(S, "ot", n, PS[:, 5 + n % 2, 256:384], v["o"], DV.at("o", n))
                elif step == "wo":
                    pe.wait_ge(*A.at("ot", n))
                    bias(PS[:, 5 + n % 2, 384:512], b_out)
                    mm(PS[:, 5 + n % 2, 384:512], v["ot"], w_out, False, True).then_inc(*S.did("wo", n))

            def moe_hidden(F, n, w_in, rhs):
                S = F["pe"]
                us = units(n)

                def hidden(k):
                    h, e, c = us[k]
                    if len(w_in) == 2:
                        if k >= 2:
                            pe.wait_ge(*F["dve"].at("act", *us[k - 2]))
                        for j in range(2):
                            ins = mm(bank(2 * (k % 2) + j), w_in[j][:, e, c * 128:(c + 1) * 128], rhs[:, h * HALF:(h + 1) * HALF])
                    else:
                        if k >= 4:
                            pe.wait_ge(*F["act"].at("relu", *us[k - 4]))
                        ins = mm(bank(k % 4), w_in[0][:, e, c * 128:(c + 1) * 128], rhs[:, h * HALF:(h + 1) * HALF])
                    ins.then_inc(*S.did("hg", h, e, c))
                return hidden

            hidden0 = moe_hidden(f0, 2, FW, xnt)
            S, A, DV = x0["pe"], x0["act"], x0["dve"]
            for step, n in S.order:
                if (step, n) == ("xt2", B - 1):
                    pe.wait_ge(ld_f0, 16)
                    pe.wait_ge(*A.at("xt2", B // 2 - 1))
                    pe.wait_ge(*DV.at("sub", 4 * B - 1))
                    hidden0(0)
                group = step in ("sc", "pt", "pv")
                b = n // 4 if group else n
                v, w = X0S[b % 4], X0U[n % 3]
                if step == "xt":
                    after(pe, A, "qt", b - 1)
                    turn(S, "xt", b, PS[:, 7, 0:T], v["xn"], DV.at("xn", b))
                elif step == "q":
                    pe.wait_ge(*A.at("xt", b))
                    bias(PS[:, 7, 0:D], "x0_bq")
                    mm(PS[:, 7, 0:D], v["xt"], X0Q, False, True).then_inc(*S.did("q", b))
                elif step == "qt":
                    turn(S, "qt", b, PS[:, 7, 0:T], v["qr"], DV.at("rope", b))
                elif step == "xt2":
                    turn(S, "xt2", b, PS[:, 5 + b % 2, 0:T], v["xn2"], DV.at("xn2", b))
                elif step == "gate":
                    if b == 0:
                        pe.wait_ge(ld_w1, 16)
                    pe.wait_ge(*A.at("xt2", b))
                    mm(PS[:, 5 + b % 2, 0:E0], XNT[:, b, :], f_g).then_inc(*S.did("gate", b))
                else:
                    narrow_heads(x0, step, n, v, w, M, V0[:, b, :, :], X0O, "x0_bo", "lg")

            def moe_units(F, n, ahead, w_in, w_out, hidden):
                S = F["pe"]
                us = units(n)

                def unit(step, k):
                    h, e, c = us[k]
                    if k + ahead < len(us):
                        hidden(k + ahead)
                    if len(w_in) == 2:
                        pe.wait_ge(*F["dve"].at("act", h, e, c))
                    else:
                        pe.wait_ge(*F["act"].at("relu", h, e, c))
                    ring = 3 if len(w_in) == 2 else 4
                    if c == 0 and h * E0 + e >= 2:
                        ph, pe_ = divmod(h * E0 + e - 2, E0)
                        pe.wait_ge(*F["dve"].at("acc", ph, pe_))
                    for j in range(4):
                        ins = mm(PS[:, 6 + e % 2, j * D:(j + 1) * D], ACTB[:, k % ring, j * T:(j + 1) * T],
                                 w_out[:, e, c, :], c == 0 and j == 0, c == n - 1 and j == 3, skip_group_check=True)
                    if c == n - 1:
                        ins.then_inc(*S.did("y", h, e))
                    else:
                        ins.then_inc(*S.did("yp", h, e, c))
                return unit

            S, A, DV = f0["pe"], f0["act"], f0["dve"]
            pe.wait_ge(*x0["dve"].at("lg", B - 1))
            f0_step = moe_units(f0, 2, 1, FW, FW3, hidden0)

            def a1_step(step, b):
                S, A, DV = a1["pe"], a1["act"], a1["dve"]
                v, ps = A1S[b % 6], PS[:, A1BANK[b], 0:T]
                if step == "xt":
                    if b < 6:
                        after(pe, DV, "y", b - 2)
                    else:
                        pe.wait_ge(*f0["dve"].at("acc", 1, E0 - 1))
                    turn(S, "xt", b, ps, v["xn"], DV.at("xn", b))
                elif step == "qkv":
                    pe.wait_ge(*A.at("xt", b))
                    for k in range(2):
                        mm(PS[:, A1BANK[b], k * T:(k + 1) * T], A1W[:, k * D:(k + 1) * D], v["xt"])
                    bias(PS[:, A1BANK[b], 2 * D:3 * D], "a1_bv")
                    mm(PS[:, A1BANK[b], 2 * D:3 * D], v["xt"], A1W[:, 2 * D:3 * D], False, True).then_inc(*S.did("qkv", b))
                elif step == "s":
                    for k in "qkv":
                        pe.wait_ge(*A.at(k, b))
                    mm(ps, v["qt"], v["kt"]).then_inc(*S.did("s", b))
                elif step == "pt":
                    turn(S, "pt", b, ps, v["p"], A.at("p", b))
                elif step == "o":
                    pe.wait_ge(*A.at("pt", b))
                    mm(ps, v["v"], v["pt"]).then_inc(*S.did("o", b))
                elif step == "out":
                    pe.wait_ge(*A.at("o", b))
                    mm(ps, v["ot"], A1P).then_inc(*S.did("out", b))

            def x1_step(step, n):
                S, A, DV = x1["pe"], x1["act"], x1["dve"]
                group = step in ("s", "pt", "o")
                b, g = divmod(n, 4) if group else (n, 0)
                v, w = X1S[b % 2], X1U[n % 3]
                rows_ = slice(64 * (g % 2), 64 * (g % 2) + 64)
                if (step, n) in (("lt", 0), ("k0", 0)):
                    pe.wait_ge(ld_x1, 16)
                    pe.wait_ge(ones, 1)
                    pe.wait_ge(*f0["dve"].at("acc", 1, E0 - 1))
                if (step, n) == ("pt", 0):
                    pe.wait_ge(*a1["dve"].at("y", B - 1))
                if step == "lt":
                    after(pe, DV, "vb", b - 1)
                    turn(S, "lt", b, PS[:, 6, 0:T], v["l2"], DV.at("l2", b))
                elif step == "q":
                    pe.wait_ge(*A.at("lt", b))
                    for c in range(4):
                        ins = mm(PS[:, 6, c * T:(c + 1) * T], X1Q[:, c * 128:(c + 1) * 128], KVT[:, b, M:J1])
                    ins.then_inc(*S.did("q", b))
                elif step in ("k0", "k1"):
                    if step == "k0":
                        pe.wait_ge(*A.at("lt", b))
                        after(pe, DV, "va", b - 1)
                    else:
                        pe.wait_ge(*A.at("q", b))
                    bk, c0_ = (7, 0) if step == "k0" else (6, 2)
                    for c in range(2):
                        ins = mm(PS[:, bk, c * J1:(c + 1) * J1], X1KV[:, (c0_ + c) * 128:(c0_ + c + 1) * 128], KVT[:, b, :])
                    ins.then_inc(*S.did(step, b))
                elif step == "va":
                    pe.wait_ge(*A.at("k0", b))
                    mm(bank(7)[0:M, :], KVT[:, b, 0:M], X1KV[:, 512:1024]).then_inc(*S.did("va", b))
                elif step == "vb":
                    pe.wait_ge(*A.at("k1", b))
                    mm(bank(6), KVT[:, b, M:J1], X1KV[:, 512:1024]).then_inc(*S.did("vb", b))
                elif step == "s":
                    if g == 0:
                        pe.wait_ge(*A.at("k0", b))
                        pe.wait_ge(*A.at("k1", b))
                    after(pe, DV, "sub", n - 2)
                    for j in range(2):
                        c = 2 * (g // 2) + j
                        ins = mm(PS[:, n % 2, j * J1:(j + 1) * J1], v["qt"][rows_, c, :], v["kt"][rows_, c, :])
                    ins.then_inc(*S.did("s", n))
                elif step == "pt":
                    pe.wait_ge(*A.at("p", n))
                    after(pe, A, "pt", n - 2)
                    for j in range(2):
                        pe.transpose(PS[0:M, 2 + n % 2, j * T:(j + 1) * T], w["p"][:, j, 0:M], IDN)
                        ins = pe.transpose(PS[:, 2 + n % 2, (2 + j) * T:(3 + j) * T], w["p"][:, j, M:J1], IDN)
                    ins.then_inc(*S.did("pt", n))
                elif step == "o":
                    if g == 0:
                        pe.wait_ge(*DV.at("va", b))
                        pe.wait_ge(*DV.at("vb", b))
                        after(pe, DV, "o0", b - 1)
                    if g == 2:
                        after(pe, DV, "res", b - 1)
                    pe.wait_ge(*A.at("pt", n))
                    for j in range(2):
                        h = 4 * (g // 2) + g % 2 + 2 * j
                        o = PS[:, 4 + g // 2, (h % 4) * (HD1 + 1):(h % 4 + 1) * (HD1 + 1)]
                        mm(o, w["pta"][0:M, j, :], v["va"][0:M, h, :], True, False)
                        ins = mm(o, w["ptb"][:, j, :], v["vb"][:, h, :], False, True)
                    ins.then_inc(*S.did("o", n))
                elif step == "ot":
                    pe.wait_ge(*DV.at("o0", b))
                    pe.wait_ge(*DV.at("o1", b))
                    for c in range(4):
                        ins = pe.transpose(PS[:, 5, c * T:(c + 1) * T], v["o"][:, c * 128:(c + 1) * 128], IDN)
                    ins.then_inc(*S.did("ot", b))
                elif step == "out":
                    pe.wait_ge(*A.at("ot", b))
                    for c in range(4):
                        ins = mm(PS[:, 5, 0:D], v["ot"][:, c, :], X1O[:, c, :], c == 0, c == 3)
                    ins.then_inc(*S.did("out", b))

            hidden1 = moe_hidden(f1, 4, [G1], XAT1.rearrange("p b t -> p (b t)"))

            def g1_step(step, n):
                S, A, DV = g1["pe"], g1["act"], g1["dve"]
                if (step, n) == ("xt", 0):
                    pe.wait_ge(ld_w2, 32)
                    pe.wait_ge(ones, 2)
                    pe.wait_ge(*x1["dve"].at("va", B - 1))
                elif (step, n) == ("sc", 0):
                    pe.wait_ge(*x1["dve"].at("sub", 4 * B - 1))
                    pe.wait_ge(*x1["act"].at("pt", 4 * B - 1))
                elif (step, n) == ("pt", 0):
                    pe.wait_ge(*x1["dve"].at("o0", B - 1))
                elif (step, n) == ("pv", 0):
                    pe.wait_ge(*x1["dve"].at("res", B - 1))
                elif (step, n) == ("xat", B - 1):
                    pe.wait_ge(*A.at("xat", B // 2 - 1))
                    pe.wait_ge(*DV.at("sub", 4 * B - 1))
                    for k in range(3):
                        hidden1(k)
                group = step in ("sc", "pt", "pv")
                b = n // 4 if group else n
                v, w = G1S[b % 4], G1U[n % 3]
                if step == "xt":
                    for k in "qkv":
                        after(pe, A, k, b - 1)
                    turn(S, "xt", b, PS[:, 7, 0:T], v["xn"], DV.at("xn", b))
                elif step == "y":
                    pe.wait_ge(*A.at("xt", b))
                    for k in range(3):
                        ins = mm(PS[:, 7, 0:D], v["xp"][:, k:k + T], GC[:, k, :], k == 0, k == 2)
                    ins.then_inc(*S.did("y", b))
                elif step == "yt":
                    turn(S, "yt", b, PS[:, 7, 0:T], v["y"], DV.at("y", b))
                elif step == "qkv":
                    pe.wait_ge(*A.at("yt", b))
                    for k in range(2):
                        mm(PS[:, 7, k * T:(k + 1) * T], G_QKV[:, k * D:(k + 1) * D], v["yt"])
                    bias(PS[:, 7, 2 * D:3 * D], "f1_bv")
                    mm(PS[:, 7, 2 * D:3 * D], v["yt"], G_QKV[:, 2 * D:3 * D], False, True).then_inc(*S.did("qkv", b))
                elif step == "xat":
                    turn(S, "xat", b, PS[:, 5 + b % 2, 0:T], XN1[:, b, :], DV.at("xa", b))
                elif step == "gate":
                    pe.wait_ge(*A.at("xat", b))
                    mm(PS[:, 5 + b % 2, 0:E1], XAT1[:, b, :], G_G).then_inc(*S.did("gate", b))
                else:
                    narrow_heads(g1, step, n, v, w, T, v["v"], G_O, "f1_bo", "lg")

            overlapped("pe", {"f0": f0_step, "a1": a1_step, "x1": x1_step, "g1": g1_step})

            S, A, DV = f1["pe"], f1["act"], f1["dve"]

            f1_step = moe_units(f1, 4, 3, [G1], G2, hidden1)
            pe.wait_ge(*g1["dve"].at("lg", B - 1))
            for k in range(len(units(4))):
                f1_step("unit", k)
                if k == 1:
                    pe.wait_ge(*DV.at("prob"))
                    for b in range(B):
                        i = pe.transpose(PS[0:E1, 4 + b // 4, (b % 4) * T:(b % 4 + 1) * T], PROB[:, b, :], IDN)
                    i.then_inc(*S.did("pt"))
                elif k == 2:
                    pe.wait_ge(*A.at("pt"))
                    for b in range(B):
                        i = mm(PS[:, 4 + b // 4, (b % 4) * D:(b % 4 + 1) * D], PROBT[0:E1, b, :], B2[:, :])
                    i.then_inc(*S.did("b2"))


def _constants():
    c = np.zeros((128, 156 + 2 * DS), np.float32)
    c[:, 0:128] = np.eye(128)
    c[:, 128:144] = np.arange(128)[:, None] // HD0 == np.arange(H0)[None, :]
    c[:, 144:148] = 1.0 / 10000.0 ** (np.arange(0, HD0, 2, dtype=np.float32) / HD0)
    c[:, 148:156] = np.arange(8)
    for r in range(96):
        c[r, 156 + r % 32] = 1
    return c


def kernel(**inp):
    import concourse.bacc as bacc
    from concourse.bass_utils import run_bass_kernel_spmd

    a = {k: np.asarray(v) for k, v in inp.items()}
    m = {d: {k[len("L0_attn_"):-2]: v for k, v in a.items() if k.startswith("L0_attn_") and k.endswith("_" + d)} for d in "fb"}

    def flat(*parts):
        return np.ascontiguousarray(np.concatenate([p.reshape(p.shape[0], -1) for p in parts], axis=1))

    def chunks(w, n=128):
        return w.reshape(w.shape[0] // n, n, -1).transpose(1, 0, 2)

    consts = _constants()
    w_m = flat(*[m[d]["in_proj"].T for d in "fb"],
               *[chunks(m[d]["x_proj"][0:DR].T) for d in "fb"],
               *[np.concatenate([chunks(m[d]["x_proj"][DR:].T)] * 3, axis=2) for d in "fb"],
               *[chunks(m[d]["out_proj"].T) for d in "fb"])
    dtw_t = np.ascontiguousarray(np.stack([m[d]["dt_w"].T for d in "fb"], axis=1))
    rows = {"ln_w": a["L0_attn_ln_w"], "ln_b": a["L0_attn_ln_b"], "gm": a["L1_xattn_gm"], "bm": a["L1_xattn_bm"],
            "gl": a["L1_xattn_gl"], "bl": a["L1_xattn_bl"], "ln1_g": a["L1_ffn_ln1_g"], "ln1_b": a["L1_ffn_ln1_b"],
            "ln2_g": a["L1_ffn_ln2_g"], "ln2_b": a["L1_ffn_ln2_b"], "x0_bq": a["L0_xattn_bq"],
            "x0_bv": a["L0_xattn_bv"], "x0_bo": a["L0_xattn_bo"], "a1_bv": a["L1_attn_b_qkv"][2 * D:],
            "a1_bproj": a["L1_attn_b_proj"], "conv_b": a["L1_ffn_conv_b"], "f1_bv": a["L1_ffn_bqkv"][2 * D:],
            "f1_bo": a["L1_ffn_bo"], "gate_b": a["L1_ffn_gate_b"]}
    row = np.zeros((1, len(ROWS) * D), np.float32)
    for i, k in enumerate(ROWS):
        row[0, i * D:i * D + rows[k].size] = rows[k]
    both = "fb"
    cols = flat(*[chunks(m[d]["conv_w"]) for d in both], *[chunks(m[d]["conv_b"][:, None]) for d in both],
                *[chunks(m[d]["dt_b"][:, None]) for d in both], *[chunks(m[d]["D"][:, None]) for d in both],
                *[chunks(m[d]["A_log"]) for d in both], a["L0_xattn_bk"][:, None],
                a["L1_attn_b_qkv"][0:2 * D].reshape(2, D).T, a["L1_ffn_bqkv"][0:2 * D].reshape(2, D).T,
                a["L1_ffn_b1"].reshape(E1, 4, 128).transpose(2, 0, 1))
    arrays = {
        "x": a["x"], "ctx": a["ctx_1024"], "ctx_t": np.ascontiguousarray(a["ctx_1024"].transpose(2, 0, 1)),
        "pos": np.ascontiguousarray(a["itok_BxS_1_4095"].T), "w_m": w_m, "dtw_t": dtw_t, "consts": consts,
        "rows": row, "cols": cols,
        "w_x0": flat(*[a[f"L0_xattn_W{k}"].T for k in "qkvo"]),
        "w_f0": flat(*[a[f"L0_ffn_W{k}"].transpose(1, 0, 2) for k in (1, 2)],
                     a["L0_ffn_W3"].reshape(E0, 2, 128, D).transpose(2, 0, 1, 3)),
        "w_a1": flat(a["L1_attn_W_qkv"], a["L1_attn_W_proj"], a["L0_ffn_Wg"]),
        "w_x1": flat(a["L1_xattn_Wq"], a["L1_xattn_Wkv"], chunks(a["L1_xattn_Wout"])),
        "w_f1": flat(a["L1_ffn_conv_w"].transpose(1, 2, 0), a["L1_ffn_wqkv"].T, a["L1_ffn_wo"].T, a["L1_ffn_gate_w"],
                     a["L1_ffn_w1"].transpose(1, 0, 2), a["L1_ffn_w2"].reshape(E1, 4, 128, D).transpose(2, 0, 1, 3)),
        "b2": a["L1_ffn_b2"],
    }
    nc = bacc.Bacc("TRN2", target_bir_lowering=False, num_devices=1)
    args = [nc.dram_tensor(f"in_{k}", v.shape, mybir.dt.from_np(v.dtype), kind="ExternalInput").ap()
            for k, v in arrays.items()]
    out = nc.dram_tensor("out_x", (B, T, D), F32, kind="ExternalOutput").ap()
    decoder_kernel(nc, *args, out)
    r = run_bass_kernel_spmd(nc, [{f"in_{k}": v for k, v in arrays.items()}], core_ids=[0])
    return r.results[0]["out_x"]
```
